# Optimizing a Trainium2 kernel written in Bass

```python
import numpy as np
import jax
import jax.numpy as jnp

def _softmax(x, axis=-1):
    return jax.nn.softmax(x, axis=axis)

def _gelu(x):
    return jax.nn.gelu(x, approximate=True)

def _silu(x):
    return jax.nn.silu(x)

def _sigmoid(x):
    return jax.nn.sigmoid(x)

def _layernorm(x, axis=-1, eps=1e-05):
    m = jnp.mean(x, axis=axis, keepdims=True)
    v = jnp.var(x, axis=axis, keepdims=True)
    return (x - m) / jnp.sqrt(v + eps)

def _scatter_add(tgt, idx, src, axis=0):
    return tgt.at[idx].add(src)

def _segment_sum(src, seg, n):
    return jax.ops.segment_sum(src, seg, n)
kernel_name = 'mk_decoder_postln_d2_seqx_r4_3dc8ec'

def setup_inputs(seed: int=0):
    np.random.seed(seed)
    _w = jnp.asarray

    def _rec_inputs():
        import jax
        import jax.numpy as jnp
        _rk = jax.random.key(seed)
        x = -0.0002928 + 1 * jax.random.normal(jax.random.fold_in(_rk, 1), (2, 1024, 256), jnp.float32)
        _lenS = 1024 - jax.random.randint(jax.random.fold_in(_rk, 7), (2,), 0, max(1, 1024 // 4) + 1, jnp.int32)
        _lenS2 = 154 - jax.random.randint(jax.random.fold_in(_rk, 8), (2,), 0, max(1, 154 // 4) + 1, jnp.int32)
        _ctx_1024P = jax.random.normal(jax.random.fold_in(_rk, 11), (2, 16, 256), jnp.float32)
        _ctx_1024c = jax.random.dirichlet(jax.random.fold_in(_rk, 511), 0.3 * jnp.ones((16,), jnp.float32), (2, 154))
        _ctx_1024t = jnp.einsum('bsk,bkd->bsd', _ctx_1024c, _ctx_1024P)
        _ctx_1024t = _ctx_1024t * jax.lax.rsqrt(jnp.mean(jnp.square(_ctx_1024t)) + 1e-12) * 0.953939
        ctx_1024 = 4.13588e-05 + 0.999923 * (_ctx_1024t + 0.3 * jax.random.normal(jax.random.fold_in(_rk, 611), (2, 154, 256), jnp.float32))
        _validS = jnp.arange(1024)[None, :] < _lenS[:, None]
        _validS2 = jnp.arange(154)[None, :] < _lenS2[:, None]
        _causal = jnp.tril(jnp.ones((1024, 1024), dtype=bool))
        mask_BxSxS2_bf0 = jnp.logical_not(jnp.ones((2, 1024, 154), dtype=bool))
        mask_Bx1xSxS2_ik1 = jnp.where(jnp.broadcast_to(_validS2[:, None, None, :], (2, 1, 1024, 154)), 1, 0).astype(jnp.int32)
        return (x, ctx_1024, mask_BxSxS2_bf0, mask_Bx1xSxS2_ik1)
    x, ctx_1024, mask_BxSxS2_bf0, mask_Bx1xSxS2_ik1 = _rec_inputs()

    def _L0_attn_setup():
        import jax, jax.numpy as jnp
        import numpy as np
        B, T, C = (64, 64, 256)
        N_HEAD, HEAD_SIZE, KV_RANK = (16, 64, 128)
        BLOCK_SIZE = 64
        key = jax.random.key(seed)
        ks = jax.random.split(key, 5)
        HD = N_HEAD * HEAD_SIZE

        def init(k, shape):
            fan_in = shape[0]
            bound = 1.0 / np.sqrt(fan_in)
            return jax.random.uniform(k, shape, jnp.float32, -bound, bound)
        return {'x': jax.random.normal(ks[0], (B, T, C), jnp.float32), 'w_kv_down': init(ks[1], (C, KV_RANK)), 'w_kv_up': init(ks[2], (KV_RANK, 2 * HD)), 'w_q': init(ks[3], (C, HD)), 'w_out': init(ks[4], (HD, C))}
    _L0_attn_all = _L0_attn_setup()
    _L0_attn_in = {k: v for k, v in _L0_attn_all.items() if k in ('w_kv_down', 'w_kv_up', 'w_q', 'w_out')}
    del _L0_attn_all

    def _L0_xattn_setup():
        import jax, jax.numpy as jnp
        import numpy as np
        HIDDEN = 256
        HEADS = 16
        D_K = HIDDEN // HEADS
        B, LQ, LKV = (4, 256, 512)
        NEG_INF = -1e+18
        key = jax.random.key(seed)
        ks = jax.random.split(key, 12)
        s = 1.0 / np.sqrt(HIDDEN)
        return {'tgt': jax.random.normal(ks[0], (B, LQ, HIDDEN), jnp.float32), 'memory': jax.random.normal(ks[1], (B, LKV, HIDDEN), jnp.float32), 'mask': jnp.zeros((B, LQ, LKV), dtype=bool), 'Wq': jax.random.normal(ks[2], (HIDDEN, HIDDEN), jnp.float32) * s, 'bq': jnp.zeros((HIDDEN,), jnp.float32), 'Wk': jax.random.normal(ks[3], (HIDDEN, HIDDEN), jnp.float32) * s, 'bk': jnp.zeros((HIDDEN,), jnp.float32), 'Wv': jax.random.normal(ks[4], (HIDDEN, HIDDEN), jnp.float32) * s, 'bv': jnp.zeros((HIDDEN,), jnp.float32), 'Wo': jax.random.normal(ks[5], (HIDDEN, HIDDEN), jnp.float32) * s, 'bo': jnp.zeros((HIDDEN,), jnp.float32)}
    _L0_xattn_all = _L0_xattn_setup()
    _L0_xattn_in = {k: v for k, v in _L0_xattn_all.items() if k in ('Wq', 'bq', 'Wk', 'bk', 'Wv', 'bv', 'Wo', 'bo')}
    del _L0_xattn_all

    def _L0_ffn_setup():
        import jax, jax.numpy as jnp
        import numpy as np
        LORA_DIM = 16
        LORA_TOKEN_INDEX = 1
        B, S, D, H = (4, 512, 256, 1024)
        key = jax.random.key(seed)
        ks = jax.random.split(key, 6)
        x = jax.random.normal(ks[0], (B, S, D), dtype=jnp.float32)
        W1 = jax.random.normal(ks[1], (H, D), dtype=jnp.float32) * 0.02
        b1 = jnp.zeros((H,), dtype=jnp.float32)
        W2 = jax.random.normal(ks[2], (D, H), dtype=jnp.float32) * 0.02
        b2 = jnp.zeros((D,), dtype=jnp.float32)
        scale = jnp.asarray(0.001, dtype=jnp.float32)
        return {'x': x, 'W1': W1, 'b1': b1, 'W2': W2, 'b2': b2, 'scale': scale}
    _L0_ffn_all = _L0_ffn_setup()
    _L0_ffn_in = {k: v for k, v in _L0_ffn_all.items() if k in ('W1', 'b1', 'W2', 'b2', 'scale')}
    del _L0_ffn_all

    def _L1_attn_setup():
        import jax, jax.numpy as jnp
        from jax import lax
        import numpy as np
        D = 256
        H = 16
        DK = D // 2 // H
        DV = D // H
        GATE_NORM = 16.0
        SCALE = DK ** (-0.5)
        EPS = 1e-05

        def _split_heads(x, dh):
            B, L, _ = x.shape
            return x.reshape(B, L, H, dh).transpose(0, 2, 1, 3)

        def _gla_scan(q, k, v, log_gate):
            B = q.shape[0]
            qt = jnp.moveaxis(q, 2, 0)
            kt = jnp.moveaxis(k, 2, 0)
            vt = jnp.moveaxis(v, 2, 0)
            gt = jnp.exp(jnp.moveaxis(log_gate, 2, 0))

            def step(state, inp):
                qq, kk, vv, gg = inp
                state = state * gg[..., None] + kk[..., :, None] * vv[..., None, :]
                out = jnp.einsum('bhd,bhde->bhe', qq, state)
                return (state, out)
            init = jnp.zeros((B, H, DK, DV), dtype=q.dtype)
            _, outs = lax.scan(step, init, (qt, kt, vt, gt))
            return jnp.moveaxis(outs, 0, 2)
        key = jax.random.key(seed)
        ks = jax.random.split(key, 10)
        s = 0.02
        return {'inputs': jax.random.normal(ks[0], (4, 1024, D), dtype=jnp.float32), 'Wq': jax.random.normal(ks[1], (D, D // 2), dtype=jnp.float32) * s, 'Wk': jax.random.normal(ks[2], (D, D // 2), dtype=jnp.float32) * s, 'Wg1': jax.random.normal(ks[3], (D, 16), dtype=jnp.float32) * s, 'Wg2': jax.random.normal(ks[4], (16, D // 2), dtype=jnp.float32) * s, 'Wv': jax.random.normal(ks[5], (D, D), dtype=jnp.float32) * s, 'Wg': jax.random.normal(ks[6], (D, D), dtype=jnp.float32) * s, 'bg': jax.random.normal(ks[7], (D,), dtype=jnp.float32) * s, 'Wo': jax.random.normal(ks[8], (D, D), dtype=jnp.float32) * s}
    _L1_attn_all = _L1_attn_setup()
    _L1_attn_in = {k: v for k, v in _L1_attn_all.items() if k in ('Wq', 'Wk', 'Wg1', 'Wg2', 'Wv', 'Wg', 'bg', 'Wo')}
    del _L1_attn_all

    def _L1_xattn_setup():
        import jax, jax.numpy as jnp
        import numpy as np
        EMBED = 256
        HEADS = 16
        HEAD_DIM = EMBED // HEADS
        key = jax.random.key(seed)
        ks = jax.random.split(key, 9)
        N, L = (2, 512)
        inp = {'values': jax.random.normal(ks[0], (N, L, EMBED), dtype=jnp.float32), 'keys': jax.random.normal(ks[1], (N, L, EMBED), dtype=jnp.float32), 'query': jax.random.normal(ks[2], (N, L, EMBED), dtype=jnp.float32), 'mask': jax.random.randint(ks[3], (N, 1, L, L), 0, 2, dtype=jnp.int32), 'Wv': jax.random.normal(ks[4], (HEAD_DIM, HEAD_DIM), dtype=jnp.float32) / np.sqrt(HEAD_DIM), 'Wk': jax.random.normal(ks[5], (HEAD_DIM, HEAD_DIM), dtype=jnp.float32) / np.sqrt(HEAD_DIM), 'Wq': jax.random.normal(ks[6], (HEAD_DIM, HEAD_DIM), dtype=jnp.float32) / np.sqrt(HEAD_DIM), 'Wo': jax.random.normal(ks[7], (EMBED, EMBED), dtype=jnp.float32) / np.sqrt(EMBED), 'bo': jax.random.normal(ks[8], (EMBED,), dtype=jnp.float32) * 0.02}
        return inp
    _L1_xattn_all = _L1_xattn_setup()
    _L1_xattn_in = {k: v for k, v in _L1_xattn_all.items() if k in ('Wv', 'Wk', 'Wq', 'Wo', 'bo')}
    del _L1_xattn_all

    def _L1_ffn_setup():
        import math
        import jax, jax.numpy as jnp
        import numpy as np
        E = 8
        K = 2
        CF = 1.25
        D = 256
        F = 512
        B, S = (4, 512)
        key = jax.random.key(seed)
        ks = jax.random.split(key, 8)
        sd = 1.0 / math.sqrt(D)
        sf = 1.0 / math.sqrt(F)
        return {'x': jax.random.normal(ks[0], (B, S, D), jnp.float32), 'router_w': jax.random.normal(ks[1], (D, E), jnp.float32) * sd, 'router_b': jnp.zeros((E,), jnp.float32), 'w1': jax.random.normal(ks[2], (E, D, F), jnp.float32) * sd, 'b1': jax.random.normal(ks[3], (E, F), jnp.float32) * 0.01, 'w2': jax.random.normal(ks[4], (E, F, D), jnp.float32) * sf, 'b2': jax.random.normal(ks[5], (E, D), jnp.float32) * 0.01}
    _L1_ffn_all = _L1_ffn_setup()
    _L1_ffn_in = {k: v for k, v in _L1_ffn_all.items() if k in ('router_w', 'router_b', 'w1', 'b1', 'w2', 'b2')}
    del _L1_ffn_all
    return {'x': x, 'ctx_1024': ctx_1024, 'mask_BxSxS2_bf0': mask_BxSxS2_bf0, 'mask_Bx1xSxS2_ik1': mask_Bx1xSxS2_ik1, 'L0_attn_w_kv_down': _L0_attn_in['w_kv_down'], 'L0_attn_w_kv_up': _L0_attn_in['w_kv_up'], 'L0_attn_w_q': _L0_attn_in['w_q'], 'L0_attn_w_out': _L0_attn_in['w_out'], 'L0_xattn_Wq': _L0_xattn_in['Wq'], 'L0_xattn_bq': _L0_xattn_in['bq'], 'L0_xattn_Wk': _L0_xattn_in['Wk'], 'L0_xattn_bk': _L0_xattn_in['bk'], 'L0_xattn_Wv': _L0_xattn_in['Wv'], 'L0_xattn_bv': _L0_xattn_in['bv'], 'L0_xattn_Wo': _L0_xattn_in['Wo'], 'L0_xattn_bo': _L0_xattn_in['bo'], 'L0_ffn_W1': _L0_ffn_in['W1'], 'L0_ffn_b1': _L0_ffn_in['b1'], 'L0_ffn_W2': _L0_ffn_in['W2'], 'L0_ffn_b2': _L0_ffn_in['b2'], 'L0_ffn_scale': _L0_ffn_in['scale'], 'L1_attn_Wq': _L1_attn_in['Wq'], 'L1_attn_Wk': _L1_attn_in['Wk'], 'L1_attn_Wg1': _L1_attn_in['Wg1'], 'L1_attn_Wg2': _L1_attn_in['Wg2'], 'L1_attn_Wv': _L1_attn_in['Wv'], 'L1_attn_Wg': _L1_attn_in['Wg'], 'L1_attn_bg': _L1_attn_in['bg'], 'L1_attn_Wo': _L1_attn_in['Wo'], 'L1_xattn_Wv': _L1_xattn_in['Wv'], 'L1_xattn_Wk': _L1_xattn_in['Wk'], 'L1_xattn_Wq': _L1_xattn_in['Wq'], 'L1_xattn_Wo': _L1_xattn_in['Wo'], 'L1_xattn_bo': _L1_xattn_in['bo'], 'L1_ffn_router_w': _L1_ffn_in['router_w'], 'L1_ffn_router_b': _L1_ffn_in['router_b'], 'L1_ffn_w1': _L1_ffn_in['w1'], 'L1_ffn_b1': _L1_ffn_in['b1'], 'L1_ffn_w2': _L1_ffn_in['w2'], 'L1_ffn_b2': _L1_ffn_in['b2']}

def reference(x, ctx_1024, mask_BxSxS2_bf0, mask_Bx1xSxS2_ik1, L0_attn_w_kv_down, L0_attn_w_kv_up, L0_attn_w_q, L0_attn_w_out, L0_xattn_Wq, L0_xattn_bq, L0_xattn_Wk, L0_xattn_bk, L0_xattn_Wv, L0_xattn_bv, L0_xattn_Wo, L0_xattn_bo, L0_ffn_W1, L0_ffn_b1, L0_ffn_W2, L0_ffn_b2, L0_ffn_scale, L1_attn_Wq, L1_attn_Wk, L1_attn_Wg1, L1_attn_Wg2, L1_attn_Wv, L1_attn_Wg, L1_attn_bg, L1_attn_Wo, L1_xattn_Wv, L1_xattn_Wk, L1_xattn_Wq, L1_xattn_Wo, L1_xattn_bo, L1_ffn_router_w, L1_ffn_router_b, L1_ffn_w1, L1_ffn_b1, L1_ffn_w2, L1_ffn_b2):
    import jax
    import jax.numpy as jnp

    def _L0_attn_ref(x, w_kv_down, w_kv_up, w_q, w_out):
        import jax, jax.numpy as jnp
        import numpy as np
        B, T, C = (64, 64, 256)
        N_HEAD, HEAD_SIZE, KV_RANK = (16, 64, 128)
        BLOCK_SIZE = 64
        Bx, Tx, Cx = x.shape
        HD = N_HEAD * HEAD_SIZE
        latent_kv = x @ w_kv_down
        kv = latent_kv @ w_kv_up
        k, v = (kv[..., :HD], kv[..., HD:])
        k = k.reshape(Bx, Tx, N_HEAD, HEAD_SIZE)
        v = v.reshape(Bx, Tx, N_HEAD, HEAD_SIZE)
        q = (x @ w_q).reshape(Bx, Tx, N_HEAD, HEAD_SIZE)
        scale = HEAD_SIZE ** (-0.5)
        att = jnp.einsum('bqhd,bkhd->bhqk', q, k) * scale
        causal = jnp.tril(jnp.ones((Tx, Tx), dtype=bool))
        att = jnp.where(causal, att, -jnp.inf)
        att = jax.nn.softmax(att, axis=-1)
        y = jnp.einsum('bhqk,bkhd->bqhd', att, v)
        y = y.reshape(Bx, Tx, HD)
        return y @ w_out

    def _L0_xattn_ref(tgt, memory, mask, Wq, bq, Wk, bk, Wv, bv, Wo, bo):
        import jax, jax.numpy as jnp
        import numpy as np
        HIDDEN = 256
        HEADS = 16
        D_K = HIDDEN // HEADS
        B, LQ, LKV = (4, 256, 512)
        NEG_INF = -1e+18
        b = tgt.shape[0]

        def heads(x):
            return x.reshape(b, -1, HEADS, D_K).transpose(0, 2, 1, 3)
        q = heads(tgt @ Wq + bq) / jnp.sqrt(jnp.asarray(D_K, tgt.dtype))
        k = heads(memory @ Wk + bk)
        v = heads(memory @ Wv + bv)
        scores = jnp.einsum('bhqd,bhkd->bhqk', q, k)
        scores = jnp.where(mask[:, None, :, :], NEG_INF, scores)
        attn = jax.nn.softmax(scores, axis=-1)
        ctx = jnp.einsum('bhqk,bhkd->bhqd', attn, v)
        ctx = ctx.transpose(0, 2, 1, 3).reshape(b, -1, HIDDEN)
        return ctx @ Wo + bo

    def _L0_ffn_ref(x, W1, b1, W2, b2, scale):
        import jax, jax.numpy as jnp
        import numpy as np
        LORA_DIM = 16
        LORA_TOKEN_INDEX = 1
        B, S, D, H = (4, 512, 256, 1024)
        Bx, Sx, Dx = x.shape
        Hx = W1.shape[0]
        lt = jax.lax.dynamic_slice_in_dim(x, LORA_TOKEN_INDEX, LORA_DIM, axis=1)
        even = lt[:, ::2, :]
        odd = lt[:, 1::2, :]
        m1 = (even[:, :4, :, None] * odd[:, :4, None, :]).reshape(Bx, Hx, Dx)
        m2 = (even[:, 4:, :, None] * odd[:, 4:, None, :]).reshape(Bx, Dx, Hx)
        h = jnp.einsum('bsd,hd->bsh', x, W1) + scale * jnp.einsum('bsd,bhd->bsh', x, m1) + b1
        h = jax.nn.gelu(h, approximate=False)
        out = jnp.einsum('bsh,oh->bso', h, W2) + scale * jnp.einsum('bsh,boh->bso', h, m2) + b2
        return out

    def _L1_attn_ref(inputs, Wq, Wk, Wg1, Wg2, Wv, Wg, bg, Wo):
        import jax, jax.numpy as jnp
        from jax import lax
        import numpy as np
        D = 256
        H = 16
        DK = D // 2 // H
        DV = D // H
        GATE_NORM = 16.0
        SCALE = DK ** (-0.5)
        EPS = 1e-05

        def _split_heads(x, dh):
            B, L, _ = x.shape
            return x.reshape(B, L, H, dh).transpose(0, 2, 1, 3)

        def _gla_scan(q, k, v, log_gate):
            B = q.shape[0]
            qt = jnp.moveaxis(q, 2, 0)
            kt = jnp.moveaxis(k, 2, 0)
            vt = jnp.moveaxis(v, 2, 0)
            gt = jnp.exp(jnp.moveaxis(log_gate, 2, 0))

            def step(state, inp):
                qq, kk, vv, gg = inp
                state = state * gg[..., None] + kk[..., :, None] * vv[..., None, :]
                out = jnp.einsum('bhd,bhde->bhe', qq, state)
                return (state, out)
            init = jnp.zeros((B, H, DK, DV), dtype=q.dtype)
            _, outs = lax.scan(step, init, (qt, kt, vt, gt))
            return jnp.moveaxis(outs, 0, 2)
        B, L, _ = inputs.shape
        q = _split_heads(inputs @ Wq, DK)
        k = _split_heads(inputs @ Wk * SCALE, DK)
        kg = _split_heads(inputs @ Wg1 @ Wg2, DK)
        v = _split_heads(inputs @ Wv, DV)
        gate = jax.nn.silu(inputs @ Wg + bg)
        log_gate = jax.nn.log_sigmoid(kg) / GATE_NORM
        o = _gla_scan(q, k, v, log_gate)
        mu = jnp.mean(o, axis=-1, keepdims=True)
        var = jnp.var(o, axis=-1, keepdims=True)
        o = (o - mu) * lax.rsqrt(var + EPS)
        o = o.transpose(0, 2, 1, 3).reshape(B, L, D)
        return gate * o @ Wo

    def _L1_xattn_ref(values, keys, query, mask, Wv, Wk, Wq, Wo, bo):
        import jax, jax.numpy as jnp
        import numpy as np
        EMBED = 256
        HEADS = 16
        HEAD_DIM = EMBED // HEADS
        N, Lq = (query.shape[0], query.shape[1])
        Lk = keys.shape[1]
        v = values.reshape(N, Lk, HEADS, HEAD_DIM)
        k = keys.reshape(N, Lk, HEADS, HEAD_DIM)
        q = query.reshape(N, Lq, HEADS, HEAD_DIM)
        v = jnp.einsum('nlhd,ed->nlhe', v, Wv)
        k = jnp.einsum('nlhd,ed->nlhe', k, Wk)
        q = jnp.einsum('nqhd,ed->nqhe', q, Wq)
        energy = jnp.einsum('nqhd,nkhd->nhqk', q, k) / np.sqrt(HEAD_DIM).astype(np.float32)
        energy = jnp.where(mask == 0, jnp.float32(-1e+20), energy)
        attn = jax.nn.softmax(energy, axis=-1)
        out = jnp.einsum('nhql,nlhd->nqhd', attn, v).reshape(N, Lq, EMBED)
        return out @ Wo.T + bo

    def _L1_ffn_ref(x, router_w, router_b, w1, b1, w2, b2):
        import math
        import jax, jax.numpy as jnp
        import numpy as np
        E = 8
        K = 2
        CF = 1.25
        D = 256
        F = 512
        B, S = (4, 512)
        b, s, d = x.shape
        xf = x.reshape(-1, d)
        T = b * s
        A = T * K
        cap = max(1, int(math.ceil(CF * A / E)))
        logits = xf @ router_w + router_b
        probs = jax.nn.softmax(logits, axis=-1)
        topk_p, topk_i = jax.lax.top_k(probs, K)
        topk_p = topk_p / jnp.clip(topk_p.sum(-1, keepdims=True), 1e-09)
        a_tok = jnp.repeat(jnp.arange(T), K)
        a_exp = topk_i.reshape(-1)
        a_w = topk_p.reshape(-1)
        order = jnp.argsort(a_exp)
        se, st, sw = (a_exp[order], a_tok[order], a_w[order])
        counts = jnp.bincount(se, length=E)
        starts = jnp.cumsum(counts) - counts
        rank = jnp.arange(A) - starts[se]
        keep = rank < cap
        slot = jnp.where(keep, se * cap + rank, E * cap)
        buf = jnp.zeros((E * cap + 1, d), x.dtype).at[slot].set(xf[st])
        buf = buf[:-1].reshape(E, cap, d)
        h = jax.nn.gelu(jnp.einsum('ecd,edf->ecf', buf, w1) + b1[:, None, :], approximate=False)
        eo = jnp.einsum('ecf,efd->ecd', h, w2) + b2[:, None, :]
        eo_flat = jnp.concatenate([eo.reshape(E * cap, d), jnp.zeros((1, d), x.dtype)], axis=0)
        w = jnp.where(keep, sw, 0.0)[:, None]
        out = jnp.zeros_like(xf).at[st].add(eo_flat[slot] * w)
        return out.reshape(b, s, d)
    x = _layernorm(x + _L0_attn_ref(x, L0_attn_w_kv_down, L0_attn_w_kv_up, L0_attn_w_q, L0_attn_w_out), axis=-1)
    x = _layernorm(x + _L0_xattn_ref(x, ctx_1024, mask_BxSxS2_bf0, L0_xattn_Wq, L0_xattn_bq, L0_xattn_Wk, L0_xattn_bk, L0_xattn_Wv, L0_xattn_bv, L0_xattn_Wo, L0_xattn_bo), axis=-1)
    x = _layernorm(x + _L0_ffn_ref(x, L0_ffn_W1, L0_ffn_b1, L0_ffn_W2, L0_ffn_b2, L0_ffn_scale), axis=-1)
    x = _layernorm(x + _L1_attn_ref(x, L1_attn_Wq, L1_attn_Wk, L1_attn_Wg1, L1_attn_Wg2, L1_attn_Wv, L1_attn_Wg, L1_attn_bg, L1_attn_Wo), axis=-1)
    x = _layernorm(x + _L1_xattn_ref(ctx_1024, ctx_1024, x, mask_Bx1xSxS2_ik1, L1_xattn_Wv, L1_xattn_Wk, L1_xattn_Wq, L1_xattn_Wo, L1_xattn_bo), axis=-1)
    x = _layernorm(x + _L1_ffn_ref(x, L1_ffn_router_w, L1_ffn_router_b, L1_ffn_w1, L1_ffn_b1, L1_ffn_w2, L1_ffn_b2), axis=-1)
    return x

_drawn_inputs = setup_inputs


def setup_inputs(seed=0):
    import zlib

    import numpy as np

    out = dict(_drawn_inputs(seed))
    spreads = {'L0_xattn_bq': (0.0, 0.1),
     'L0_xattn_bk': (0.0, 0.8),
     'L0_xattn_bv': (0.0, 0.1),
     'L0_xattn_bo': (0.0, 0.1),
     'L0_ffn_b1': (0.0, 0.1),
     'L0_ffn_b2': (0.0, 0.1),
     'L1_ffn_router_b': (0.0, 0.1)}
    factors = {'L0_attn_w_q': 2.984,
     'L1_attn_Wg1': 8.0,
     'L1_attn_Wg2': 8.0,
     'L1_attn_bg': 2.784,
     'L1_ffn_b1': 8.0,
     'L1_ffn_b2': 8.0}
    for name, (base, spread) in spreads.items():
        noise = np.random.default_rng([zlib.crc32(name.encode()), seed]).standard_normal(out[name].shape)
        drawn = base * np.exp(spread * noise) if base else spread * noise
        out[name] = jnp.asarray(drawn.astype(out[name].dtype))
    for name, factor in factors.items():
        out[name] = (out[name] * factor).astype(out[name].dtype)
    return out
```

```python
import concourse.bass as bass
from concourse import mybir
from contextlib import ExitStack

F32 = mybir.dt.float32
BF16 = mybir.dt.bfloat16
I32 = mybir.dt.int32
U8 = mybir.dt.uint8
ALU = mybir.AluOpType
ACT = mybir.ActivationFunctionType
AX = mybir.AxisListType.X

P = 128
B, S, D = 2, 1024, 256
CTX = 154
KT = D // P
TILES = B * S // P
SEQ_TILES = S // P
HEADS = 16
EPS = 1e-5
BANK = 512
NEG = -1e30


EXPERTS, TOP = 8, 2
CAPACITY = -(-5 * B * S * TOP // (4 * EXPERTS))


class Links:

    def __init__(self, engine, sem, base=0):
        self.engine, self.sem, self.base, self.n = engine, sem, base, 0

    def after(self, instruction):
        instruction.then_inc(self.sem, 1)
        self.n += 1
        self.engine.wait_ge(self.sem, self.base + self.n)


class Core:

    def __init__(self, nc, stack):
        self.nc = nc
        self.stack = stack

        def sb(name, shape, dt=F32):
            return stack.enter_context(nc.sbuf_tensor(name, shape, dt))

        self.x = sb("x_tok", [P, TILES, D])
        self.xT = sb("x_chan", [P, KT, B * S])
        self.ctxT = sb("ctx_chan", [P, KT, B, CTX])
        self.ident = sb("ident", [P, P])
        self.ident_bf = sb("ident_bf", [P, P], BF16)
        self.ones_row = sb("ones_row", [1, P])
        self.stats = sb("ln_stats", [P, TILES, 6])
        self.mean_var = sb("ln_mean_var", [P, TILES, 2])
        self.var_eps = sb("ln_var_eps", [P, TILES])
        self.rstd = sb("ln_rstd", [P, TILES])
        self.minus_half = sb("minus_half", [P, TILES])
        self.zeros = sb("zeros", [P, D])
        rows = EXPERTS * CAPACITY
        self.by_expert = nc.dram_tensor("rows_by_expert", (rows + TOP * B * S, D), F32).ap()
        self.y_by_expert = nc.dram_tensor("results_by_expert", (rows, D), F32).ap()
        self.ln_sems = [self.sem("ln_" + n) for n in ("dve_steps", "var_ready", "rstd_ready", "x_ready", "xT_in_psum",
                                                      "xT_copied", "stored")]
        self.zeroed = self.sem("rows_zeroed")

    def sem(self, name):
        return self.stack.enter_context(self.nc.semaphore(name))


def constants_and_loads(core, d):
    nc = core.nc
    with ExitStack() as st:
        loaded = core.sem("inputs_loaded")
        made = core.sem("constants_made")
        block = st.enter_context(nc.Block())

        @block.sync
        def _(sp):
            sp.dma_start(core.xT[:, :, :], d["x_chan"].rearrange("(k p) n -> p k n", p=P)).then_inc(loaded, 16)
            sp.dma_start(core.ctxT[:, :, :, :].rearrange("p k b n -> p k (b n)"),
                         d["ctx_chan"].rearrange("(k p) n -> p k n", p=P)).then_inc(loaded, 16)
            sp.dma_start(core.x[:, :, :], d["x"].rearrange("b (t p) c -> p (b t) c", p=P)).then_inc(loaded, 16)
            sp.wait_ge(made, 4)
            rows = EXPERTS * CAPACITY
            sp.dma_start(core.by_expert[0:rows, :].rearrange("(t p) c -> p t c", p=P),
                         core.zeros[:, :].rearrange("p (o c) -> p o c", o=1).to_broadcast([P, rows // P, D])).then_inc(core.zeroed, 16)
            sp.wait_ge(loaded, 48)

        @block.gpsimd
        def _(pool):
            step = Links(pool, made)
            nc.gpsimd.memset(core.ones_row[:, :], 1.0)
            nc.gpsimd.memset(core.minus_half[:, :], -0.5)
            step.after(nc.gpsimd.memset(core.ident[:, :], 0.0))
            step.after(nc.gpsimd.affine_select(out=core.ident[:, :], in_=core.ident[:, :], compare_op=ALU.not_equal,
                                               fill=1.0, base=0, pattern=[[-1, P]], channel_multiplier=1))
            step.after(nc.gpsimd.tensor_copy(core.ident_bf[:, :], core.ident[:, :]))
            step.after(nc.gpsimd.memset(core.zeros[:, :], 0.0))


def layer_norm(core, nth, out=None):
    nc = core.nc
    RING = 4
    GROUP = 4
    COPIES = TILES // GROUP * KT
    s_dve, var_ready, rstd_ready, x_ready, xT_in_psum, xT_copied, stored = core.ln_sems
    with ExitStack() as st:
        ring = st.enter_context(nc.psum_tensor(f"ln{nth}_xT_psum", [P, RING, BANK], F32))
        block = st.enter_context(nc.Block())

        @block.vector
        def _(dve):
            step = Links(dve, s_dve, nth)
            for t in range(TILES):
                last = nc.vector.bn_aggr(core.mean_var[:, t, :], core.stats[:, t, :])
            step.after(last)
            nc.vector.tensor_scalar(core.var_eps[:, :], core.mean_var[:, :, 1], EPS, None, ALU.add).then_inc(var_ready, 1)
            dve.wait_ge(rstd_ready, nth + 1)
            for t in range(TILES):
                nc.vector.tensor_scalar(core.x[:, t, :], core.x[:, t, :], core.mean_var[:, t, 0:1],
                                        core.rstd[:, t:t + 1], ALU.subtract, ALU.mult).then_inc(x_ready, 1)

        @block.gpsimd
        def _(pool):
            pool.wait_ge(var_ready, nth + 1)
            nc.gpsimd.tensor_tensor(core.rstd[:, :], core.var_eps[:, :], core.minus_half[:, :], ALU.pow).then_inc(rstd_ready, 1)

        if out is not None:
            @block.sync
            def _(sp):
                o = out.rearrange("b (t p) c -> p (b t) c", p=P)
                for g in range(TILES // GROUP):
                    sp.wait_ge(x_ready, TILES * nth + GROUP * (g + 1))
                    sp.dma_start(o[:, GROUP * g:GROUP * (g + 1), :],
                                 core.x[:, GROUP * g:GROUP * (g + 1), :]).then_inc(stored, 16)
                sp.wait_ge(stored, 16 * (TILES // GROUP))
            return

        @block.tensor
        def _(pe):
            for g in range(TILES // GROUP):
                for k in range(KT):
                    n = g * KT + k
                    if n >= RING:
                        pe.wait_ge(xT_copied, COPIES * nth + n - RING + 1)
                    for i in range(GROUP):
                        pe.wait_ge(x_ready, TILES * nth + GROUP * g + i + 1)
                        last = nc.tensor.transpose(ring[:, n % RING, i * P:(i + 1) * P],
                                                   core.x[:, GROUP * g + i, k * P:(k + 1) * P], core.ident[:, :])
                    last.then_inc(xT_in_psum, 1)

        @block.scalar
        def _(act):
            for g in range(TILES // GROUP):
                for k in range(KT):
                    n = g * KT + k
                    act.wait_ge(xT_in_psum, COPIES * nth + n + 1)
                    nc.scalar.activation(core.xT[:, k, g * BANK:(g + 1) * BANK], ring[:, n % RING, :],
                                         ACT.Copy).then_inc(xT_copied, 1)


def latent_attention(core, d):
    nc = core.nc
    DH, RANK = 64, P
    PAIRS = HEADS * DH // P
    SCALE = DH ** -0.5
    Q_GROUPS = B * S // BANK
    GROUPS = 3 * Q_GROUPS
    UNITS = [(b, t, h) for b in range(B) for t in range(SEQ_TILES) for h in range(2)]
    NU = len(UNITS)
    CHUNK = BANK // P
    CHUNKS = [(u, c) for u, (b, t, h) in enumerate(UNITS) for c in range((t + CHUNK) // CHUNK)]
    NC = len(CHUNKS)
    first_chunk = [min(i for i, (v, _) in enumerate(CHUNKS) if v == u) for u in range(NU)] + [NC]

    def blocks(u):
        return UNITS[u][1] + 1

    def by_dve(i):
        return i % 3 == 2

    dve_before = [sum(by_dve(j) for j in range(i)) for i in range(NC + 1)]
    act_before = [i - dve_before[i] for i in range(NC + 1)]

    with ExitStack() as st:
        def sb(n, shape, dt=F32):
            return st.enter_context(nc.sbuf_tensor("mla_" + n, shape, dt))

        def sem(n):
            return core.sem("mla_" + n)

        w_down = sb("w_down", [P, KT, RANK])
        w_q = sb("w_q", [P, KT, P])
        w_k = sb("w_k", [P, P])
        w_v = sb("w_v", [P, P])
        w_out = sb("w_out", [P, PAIRS, D])
        latT = sb("latent_chan", [P, B * S])
        qT = sb("q_chan", [P, B * S])
        kT = sb("k_chan", [P, B * S])
        v = sb("v_tok", [P, TILES, 2, DH + 1])
        causal = sb("causal", [P, P], BF16)
        causal32 = sb("causal32", [P, P])
        p_tok = sb("exps_tok", [P, 2, S])
        pT = sb("exps_key", [P, 2, SEQ_TILES, P])
        y = sb("y_tok", [P, TILES, HEADS * DH])
        yT = sb("y_chan", [P, 2, PAIRS, P])
        neg_max = sb("neg_max", [P, 4])
        row_max = sb("row_max", [P, 4])
        inv_sum = sb("inv_sum", [P, 2])
        scores = st.enter_context(nc.psum_tensor("mla_scores", [P, 4, BANK], F32))
        tpose = st.enter_context(nc.psum_tensor("mla_tpose", [P, 2, BANK], F32))
        outp = st.enter_context(nc.psum_tensor("mla_outp", [P, 2, BANK], F32))

        w_loaded, w_used, setup = sem("w_loaded"), sem("w_used"), sem("setup")
        wd_loaded, lat_done, lat_copied = sem("wd_loaded"), sem("lat_done"), sem("lat_copied")
        proj_done, proj_act, proj_dve = sem("proj_done"), sem("proj_by_act"), sem("proj_by_dve")
        qk_done, max_done, exp_done, t_done = sem("qk_done"), sem("max_done"), sem("exp_done"), sem("t_done")
        copied_act, copied_dve, pv_done, y_done = sem("pT_by_act"), sem("pT_by_dve"), sem("pv_done"), sem("y_done")
        s_dve = sem("dve_steps")
        yT_done, yT_copied, out_done, sum_done = sem("yT_done"), sem("yT_copied"), sem("out_done"), sem("sum_done")
        block = st.enter_context(nc.Block())

        @block.sync
        def _(sp):
            sp.dma_start(w_down[:, :, :], d["L0_attn_w_kv_down"].rearrange("(k p) n -> p k n", p=P)).then_inc(wd_loaded, 16)
            with sp.Fori(0, PAIRS) as i:
                sp.wait_ge(w_used, i)
                sp.dma_start(w_q[:, :, :], d["w_q_pairs"][i]).then_inc(w_loaded, 16)
                sp.dma_start(w_k[:, :], d["w_kv_up_pairs"][i]).then_inc(w_loaded, 16)
                sp.dma_start(w_v[:, :], d["w_kv_up_pairs"][i + PAIRS]).then_inc(w_loaded, 16)
            sp.dma_start(w_out[:, :, :], d["L0_attn_w_out"].rearrange("(k p) n -> p k n", p=P)).then_inc(wd_loaded, 16)

        @block.gpsimd
        def _(pool):
            nc.gpsimd.memset(v[:, :, :, DH:DH + 1], 1.0).then_inc(setup, 1)
            nc.gpsimd.memset(causal32[:, :], 0.0).then_inc(setup, 1)
            pool.wait_ge(setup, 2)
            nc.gpsimd.affine_select(out=causal32[:, :], in_=causal32[:, :], compare_op=ALU.is_ge, fill=NEG,
                                    base=0, pattern=[[-1, P]], channel_multiplier=1).then_inc(setup, 1)
            pool.wait_ge(setup, 3)
            nc.gpsimd.tensor_copy(causal[:, :], causal32[:, :]).then_inc(setup, 1)

        @block.tensor
        def _(pe):
            pe.wait_ge(wd_loaded, 16)
            for g in range(Q_GROUPS):
                for k in range(KT):
                    last = nc.tensor.matmul(scores[:, g, :], w_down[:, k, :], core.xT[:, k, g * BANK:(g + 1) * BANK],
                                            start=(k == 0), stop=(k == KT - 1))
                last.then_inc(lat_done, 1)
            pe.wait_ge(lat_copied, Q_GROUPS)
            pe.wait_ge(setup, 4)
            with pe.Fori(0, PAIRS) as i:
                pe.wait_ge(w_loaded, 48 * i + 48)
                pe.wait_ge(exp_done, NU * i)
                pe.wait_ge(y_done, NU * i)
                for g in range(GROUPS):
                    if g >= 4:
                        pe.wait_ge(proj_act, 6 * i + (g - 4) // 2 + 1) if g % 2 == 0 else \
                            pe.wait_ge(proj_dve, 6 * i + (g - 4) // 2 + 1)
                    n = g % Q_GROUPS
                    if g < Q_GROUPS:
                        for k in range(KT):
                            last = nc.tensor.matmul(scores[:, g % 4, :], w_q[:, k, :],
                                                    core.xT[:, k, n * BANK:(n + 1) * BANK],
                                                    start=(k == 0), stop=(k == KT - 1))
                    elif g < 2 * Q_GROUPS:
                        last = nc.tensor.matmul(scores[:, g % 4, :], w_k[:, :], latT[:, n * BANK:(n + 1) * BANK],
                                                start=True, stop=True)
                    else:
                        for j in range(4):
                            last = nc.tensor.matmul(scores[:, g % 4, j * P:(j + 1) * P],
                                                    latT[:, (4 * n + j) * P:(4 * n + j + 1) * P], w_v[:, :],
                                                    start=True, stop=True)
                    last.then_inc(proj_done, 1)
                last_proj = nc.tensor.matmul(outp[:, 0, 0:P], core.ident_bf[:, :], causal[:, :], start=True, stop=True)
                last_proj.then_inc(w_used, 1)
                pe.wait_ge(proj_act, 6 * i + 6)
                pe.wait_ge(proj_dve, 6 * i + 6)

                def qk(u):
                    b, t, h = UNITS[u]
                    if u >= 2:
                        pe.wait_ge(exp_done, NU * i + u - 1)
                    rows = slice(h * DH, (h + 1) * DH)
                    width = (t + 1) * P
                    for c in range(0, width, BANK):
                        n = min(BANK, width - c)
                        bank = 2 * (u % 2) + c // BANK
                        diagonal = c + n == width
                        last = nc.tensor.matmul(scores[:, bank, 0:n], qT[rows, b * S + t * P:b * S + (t + 1) * P],
                                                kT[rows, b * S + c:b * S + c + n], start=True, stop=not diagonal)
                        if diagonal:
                            last = nc.tensor.matmul(scores[:, bank, n - P:n], core.ident_bf[:, :], causal[:, :],
                                                    start=False, stop=True)
                    last.then_inc(qk_done, 1)

                def transposes(u):
                    pe.wait_ge(exp_done, NU * i + u + 1)
                    for c in range(first_chunk[u], first_chunk[u + 1]):
                        if c >= 2:
                            pe.wait_ge(copied_dve, dve_before[NC] * i + dve_before[c - 1]) if by_dve(c - 2) else \
                                pe.wait_ge(copied_act, act_before[NC] * i + act_before[c - 1])
                        part = CHUNKS[c][1]
                        for j in range(min(CHUNK, blocks(u) - part * CHUNK)):
                            at = (part * CHUNK + j) * P
                            last = nc.tensor.transpose(tpose[:, c % 2, j * P:(j + 1) * P],
                                                       p_tok[:, u % 2, at:at + P], core.ident[:, :])
                        last.then_inc(t_done, 1)

                def pv(u):
                    b, t, h = UNITS[u]
                    pe.wait_ge(copied_act, act_before[NC] * i + act_before[first_chunk[u + 1]])
                    pe.wait_ge(copied_dve, dve_before[NC] * i + dve_before[first_chunk[u + 1]])
                    if u >= 2:
                        pe.wait_ge(y_done, NU * i + u - 1)
                    for j in range(blocks(u)):
                        last = nc.tensor.matmul(outp[:, u % 2, 0:DH + 1], pT[:, u % 2, j, :],
                                                v[:, b * SEQ_TILES + j, h, :], start=(j == 0), stop=(j == blocks(u) - 1))
                    last.then_inc(pv_done, 1)

                qk(0)
                for u in range(NU):
                    if u + 1 < NU:
                        qk(u + 1)
                    transposes(u)
                    if u >= 1:
                        pv(u - 1)
                pv(NU - 1)

            pe.wait_ge(wd_loaded, 32)
            pe.wait_ge(y_done, NU * PAIRS)

            def project(t):
                pe.wait_ge(yT_copied, 2 * t + 2)
                if t >= 2:
                    pe.wait_ge(sum_done, t - 1)
                for k in range(PAIRS):
                    last = nc.tensor.matmul(outp[:, t % 2, 0:D], yT[:, t % 2, k, :], w_out[:, k, :],
                                            start=(k == 0), stop=(k == PAIRS - 1))
                last.then_inc(out_done, 1)

            for t in range(TILES):
                for half in range(2):
                    n = 2 * t + half
                    if n >= 4:
                        pe.wait_ge(yT_copied, n - 3)
                    for j in range(4):
                        k = 4 * half + j
                        last = nc.tensor.transpose(scores[:, n % 4, j * P:(j + 1) * P], y[:, t, k * P:(k + 1) * P],
                                                   core.ident[:, :])
                    last.then_inc(yT_done, 1)
                if t >= 1:
                    project(t - 1)
            project(TILES - 1)

        @block.scalar
        def _(act):
            for g in range(Q_GROUPS):
                act.wait_ge(lat_done, g + 1)
                nc.scalar.activation(latT[:, g * BANK:(g + 1) * BANK], scores[:, g, :], ACT.Copy).then_inc(lat_copied, 1)
            with act.Fori(0, PAIRS) as i:
                for g in range(0, GROUPS, 2):
                    act.wait_ge(proj_done, GROUPS * i + g + 1)
                    n = g % Q_GROUPS
                    if g < 2 * Q_GROUPS:
                        dst = (qT if g < Q_GROUPS else kT)[:, n * BANK:(n + 1) * BANK]
                        nc.scalar.activation(dst, scores[:, g % 4, :], ACT.Copy).then_inc(proj_act, 1)
                    else:
                        nc.scalar.activation(v[:, 4 * n:4 * n + 4, :, 0:DH],
                                             scores[:, g % 4, :].rearrange("p (t h e) -> p t h e", t=4, h=2),
                                             ACT.Copy).then_inc(proj_act, 1)

                def copies(u):
                    for c in range(first_chunk[u], first_chunk[u + 1]):
                        if by_dve(c):
                            continue
                        act.wait_ge(t_done, NC * i + c + 1)
                        if u >= 2:
                            act.wait_ge(pv_done, NU * i + u - 1)
                        part = CHUNKS[c][1]
                        n = min(CHUNK, blocks(u) - part * CHUNK)
                        nc.scalar.activation(pT[:, u % 2, part * CHUNK:part * CHUNK + n, :].rearrange("p j q -> p (j q)"),
                                             tpose[:, c % 2, 0:n * P], ACT.Copy).then_inc(copied_act, 1)

                for u in range(NU):
                    act.wait_ge(max_done, NU * i + u + 1)
                    if u >= 2:
                        act.wait_ge(t_done, NC * i + first_chunk[u - 1])
                    nc.scalar.activation(p_tok[:, u % 2, 0:blocks(u) * P],
                                         scores[:, 2 * (u % 2):2 * (u % 2) + 2, :].rearrange("p c n -> p (c n)")[:, 0:blocks(u) * P],
                                         ACT.Exp, bias=neg_max[:, u % 4:u % 4 + 1], scale=SCALE).then_inc(exp_done, 1)
                    if u >= 1:
                        copies(u - 1)
                copies(NU - 1)
            for n in range(2 * TILES):
                t, half = n // 2, n % 2
                act.wait_ge(yT_done, n + 1)
                if t >= 2:
                    act.wait_ge(out_done, t - 1)
                nc.scalar.activation(yT[:, t % 2, 4 * half:4 * half + 4, :].rearrange("p k q -> p (k q)"),
                                     scores[:, n % 4, :], ACT.Copy).then_inc(yT_copied, 1)

        @block.vector
        def _(dve):
            with dve.Fori(0, PAIRS) as i:
                step = Links(dve, s_dve, i * (2 * NU))
                for g in range(1, GROUPS, 2):
                    dve.wait_ge(proj_done, GROUPS * i + g + 1)
                    n = g % Q_GROUPS
                    if g < 2 * Q_GROUPS:
                        dst = (qT if g < Q_GROUPS else kT)[:, n * BANK:(n + 1) * BANK]
                        nc.vector.tensor_copy(dst, scores[:, g % 4, :]).then_inc(proj_dve, 1)
                    else:
                        nc.vector.tensor_copy(v[:, 4 * n:4 * n + 4, :, 0:DH],
                                              scores[:, g % 4, :].rearrange("p (t h e) -> p t h e", t=4, h=2)).then_inc(proj_dve, 1)

                def copies(u):
                    for c in range(first_chunk[u], first_chunk[u + 1]):
                        if not by_dve(c):
                            continue
                        dve.wait_ge(t_done, NC * i + c + 1)
                        if u >= 2:
                            dve.wait_ge(pv_done, NU * i + u - 1)
                        part = CHUNKS[c][1]
                        n = min(CHUNK, blocks(u) - part * CHUNK)
                        nc.vector.tensor_copy(pT[:, u % 2, part * CHUNK:part * CHUNK + n, :].rearrange("p j q -> p (j q)"),
                                              tpose[:, c % 2, 0:n * P]).then_inc(copied_dve, 1)

                def normalise(u):
                    b, t, h = UNITS[u]
                    dve.wait_ge(pv_done, NU * i + u + 1)
                    step.after(nc.vector.reciprocal(inv_sum[:, u % 2:u % 2 + 1], outp[:, u % 2, DH:DH + 1]))
                    nc.vector.tensor_scalar(y[:, b * SEQ_TILES + t, bass.ds(i * P + h * DH, DH)], outp[:, u % 2, 0:DH],
                                            inv_sum[:, u % 2:u % 2 + 1], None, ALU.mult).then_inc(y_done, 1)

                for u in range(NU):
                    dve.wait_ge(qk_done, NU * i + u + 1)
                    step.after(nc.vector.tensor_reduce(
                        row_max[:, u % 4:u % 4 + 1],
                        scores[:, 2 * (u % 2):2 * (u % 2) + 2, :].rearrange("p c n -> p (c n)")[:, 0:blocks(u) * P],
                        AX, ALU.max))
                    if u >= 4:
                        dve.wait_ge(exp_done, NU * i + u - 3)
                    nc.vector.tensor_scalar(neg_max[:, u % 4:u % 4 + 1], row_max[:, u % 4:u % 4 + 1], -SCALE, None,
                                            ALU.mult).then_inc(max_done, 1)
                    if u >= 1:
                        copies(u - 1)
                    if u >= 2:
                        normalise(u - 2)
                copies(NU - 1)
                normalise(NU - 2)
                normalise(NU - 1)
            step = Links(dve, s_dve, PAIRS * 2 * NU)
            for t in range(TILES):
                dve.wait_ge(out_done, t + 1)
                nc.vector.tensor_tensor(core.x[:, t, :], outp[:, t % 2, 0:D], core.x[:, t, :], ALU.add).then_inc(sum_done, 1)
                dve.wait_ge(sum_done, t + 1)
                nc.vector.bn_stats(core.stats[:, t, :], core.x[:, t, :])


def cross_attention(core, d, name, block_diagonal, mask_value):
    nc = core.nc
    DH = D // HEADS
    HH = HEADS // 2
    HB = 3
    SB = 3
    CK = CTX // 2
    SCALE = DH ** -0.5
    UNITS = [(b, half) for b in range(B) for half in range(2)]
    NU = len(UNITS)
    CHUNK = BANK // P
    NCH = 2 * HH // CHUNK
    NC = NU * NCH

    def by_dve(c):
        return c % 4 == 3

    dve_before = [sum(by_dve(j) for j in range(i)) for i in range(NC + 1)]
    act_before = [i - dve_before[i] for i in range(NC + 1)]

    with ExitStack() as st:
        def sb(n, shape, dt=F32):
            return st.enter_context(nc.sbuf_tensor(f"{name}_{n}", shape, dt))

        def ps(n, shape):
            return st.enter_context(nc.psum_tensor(f"{name}_{n}", shape, F32))

        def sem(n):
            return core.sem(f"{name}_{n}")

        w = {n: sb("w" + n, [P, KT, D]) for n in "qkvo"}
        bias_col = sb("bias_col", [P, 2, KT])
        bias_row = sb("bias_row", [1, 2, D])
        mask_raw = sb("mask_raw", [P, TILES, CTX], U8 if mask_value[0] == "hidden" else I32)
        mask = sb("mask", [P, TILES, CTX], BF16)
        head_of = sb("head_of", [P, HH])
        k_heads = sb("k_heads", [P, B, KT, HH, CTX])
        v = sb("v_tok", [CK, B, 2, HEADS, DH + 1])
        kT = sb("k_chan", [P, KT, B * CTX])
        qT = sb("q_chan", [P, B, KT, P])
        s_max = sb("s_max", [P, HB * SB])
        p_tok = sb("exps_tok", [P, 2, HB * SB, CTX])
        pT = sb("exps_key", [CK, 2, 2 * HH, P])
        inv_sum = sb("inv_sum", [P, HEADS])
        y = sb("y_tok", [P, D])
        yT = sb("y_chan", [P, KT, P])
        scores = ps("scores", [P, SB, BANK])
        tpose = ps("tpose", [P, 2, BANK])
        outp = ps("outp", [P, HEADS, DH + 1])
        q_ps = ps("q_psum", [P, KT, P])
        fin = ps("fin", [P, 2, D])

        w_loaded, mask_loaded, setup = sem("w_loaded"), sem("mask_loaded"), sem("setup")
        wz = sem("w_zero")
        kv_done, kv_copied, kv_heads = sem("kv_done"), sem("kv_copied"), sem("kv_heads")
        q_done, q_copied, qk_done, sub_done, exp_done = sem("q_done"), sem("q_copied"), sem("qk_done"), sem("sub_done"), sem("exp_done")
        t_done, copied_act, copied_dve, pv_done = sem("t_done"), sem("pT_by_act"), sem("pT_by_dve"), sem("pv_done")
        y_done, yT_done, yT_copied, out_done, sum_done, s_dve = (sem("y_done"), sem("yT_done"), sem("yT_copied"),
                                                                 sem("out_done"), sem("sum_done"), sem("dve_steps"))
        mask_ready = sem("mask_ready")
        block = st.enter_context(nc.Block())
        WD = len(w) if not block_diagonal else 1 + 3 * D // DH

        @block.sync
        def _(sp):
            sp.dma_start(mask_raw[:, :, :], d[name + "_mask"].rearrange("b (t p) c -> p (b t) c", p=P)).then_inc(mask_loaded, 16)
            if block_diagonal:
                sp.wait_ge(wz, 3)
                for n in "kqv":
                    for h in range(HEADS):
                        r = h * DH % P
                        sp.dma_start(w[n][r:r + DH, h * DH // P, h * DH:(h + 1) * DH], d[f"{name}_W{n}"]).then_inc(w_loaded, 16)
                sp.dma_start(w["o"][:, :, :], d[name + "_Wo"].rearrange("(k p) n -> p k n", p=P)).then_inc(w_loaded, 16)
            else:
                for n in "kqvo":
                    sp.dma_start(w[n][:, :, :], d[f"{name}_W{n}"].rearrange("(k p) n -> p k n", p=P)).then_inc(w_loaded, 16)
                for j, n in enumerate("qk"):
                    sp.dma_start(bias_col[:, j, :], d[f"{name}_b{n}"].rearrange("(k p) -> p k", p=P),
                                 allow_slow_non_contiguous=True).then_inc(w_loaded, 16)
                sp.dma_start(bias_row[0:1, 0, :], d[name + "_bv"].rearrange("(o n) -> o n", o=1)).then_inc(w_loaded, 16)
            sp.dma_start(bias_row[0:1, 1, :], d[name + "_bo"].rearrange("(o n) -> o n", o=1)).then_inc(w_loaded, 16)
        LOADS = 16 * (WD + 1 + (0 if block_diagonal else 3))

        @block.gpsimd
        def _(pool):
            if block_diagonal:
                for n in "kqv":
                    nc.gpsimd.memset(w[n][:, :, :], 0.0).then_inc(wz, 1)
            step = Links(pool, setup)
            step.after(nc.gpsimd.memset(head_of[:, :], 1.0))
            step.after(nc.gpsimd.affine_select(out=head_of[:, :], in_=head_of[:, :], compare_op=ALU.is_ge, fill=0.0,
                                               base=0, pattern=[[-DH, HH]], channel_multiplier=1))
            step.after(nc.gpsimd.affine_select(out=head_of[:, :], in_=head_of[:, :], compare_op=ALU.is_ge, fill=0.0,
                                               base=DH - 1, pattern=[[DH, HH]], channel_multiplier=-1))
            step.after(nc.gpsimd.memset(v[:, :, :, :, DH:DH + 1], 1.0))

        @block.tensor
        def _(pe):
            pe.wait_ge(w_loaded, LOADS)
            for m in range(KT):
                parts = [m] if block_diagonal else list(range(KT))
                for k in parts:
                    last = nc.tensor.matmul(scores[:, m, 0:B * CTX], w["k"][:, k, m * P:(m + 1) * P],
                                            core.ctxT[:, k, :, :].rearrange("p b n -> p (b n)"),
                                            start=(k == parts[0]), stop=(k == parts[-1]))
                last.then_inc(kv_done, 1)
            for b in range(B):
                for j in range(2):
                    n = 2 * b + j
                    dst = tpose[0:CK, n % 2, 0:D]
                    if n >= 2:
                        pe.wait_ge(kv_copied, KT + n - 1)
                    for k in range(KT):
                        last = nc.tensor.matmul(dst, core.ctxT[:, k, b, j * CK:(j + 1) * CK], w["v"][:, k, :],
                                                start=(k == 0), stop=(block_diagonal and k == KT - 1))
                    if not block_diagonal:
                        last = nc.tensor.matmul(dst, core.ones_row[0:1, 0:CK], bias_row[0:1, 0, :], start=False, stop=True)
                    last.then_inc(kv_done, 1)
            pe.wait_ge(kv_heads, B * KT)
            pe.wait_ge(kv_copied, KT + 2 * B)
            pe.wait_ge(mask_ready, 1)
            with pe.Fori(0, SEQ_TILES) as i:
                def queries(b):
                    pe.wait_ge(q_copied, i * (B * KT) + KT * b)
                    for m in range(KT):
                        parts = [m] if block_diagonal else list(range(KT))
                        for k in parts:
                            last = nc.tensor.matmul(q_ps[:, m, :], w["q"][:, k, m * P:(m + 1) * P],
                                                    core.xT[:, k, bass.ds(i * P + b * S, P)],
                                                    start=(k == parts[0]), stop=(k == parts[-1]))
                    last.then_inc(q_done, 1)

                def qk(u):
                    b, half = UNITS[u]
                    if half == 0:
                        pe.wait_ge(q_copied, i * (B * KT) + KT * (b + 1))
                    pe.wait_ge(sub_done, i * NU + u)
                    for c in range(SB):
                        heads = range(c * HB, min(HH, (c + 1) * HB))
                        n = len(heads) * CTX
                        nc.tensor.matmul(scores[:, c, 0:HB * CTX].rearrange("p (h n) -> p h n", h=HB), core.ident_bf[:, :],
                                         mask[:, bass.ds(i + b * SEQ_TILES, 1), :].to_broadcast([P, HB, CTX]),
                                         start=True, stop=False)
                        last = nc.tensor.matmul(scores[:, c, 0:n], qT[:, b, half, :],
                                                k_heads[:, b, half, c * HB:c * HB + len(heads), :].rearrange("p h n -> p (h n)"),
                                                start=False, stop=True)
                    last.then_inc(qk_done, 1)

                def transposes(u):
                    pe.wait_ge(exp_done, i * NU + u + 1)
                    for c in range(NCH * u, NCH * (u + 1)):
                        if c >= 2:
                            pe.wait_ge(copied_dve, i * dve_before[NC] + dve_before[c - 1]) if by_dve(c - 2) else \
                                pe.wait_ge(copied_act, i * act_before[NC] + act_before[c - 1])
                        for j in range(CHUNK):
                            n = (c - NCH * u) * CHUNK + j
                            h, part = n // 2, n % 2
                            last = nc.tensor.transpose(tpose[0:CK, c % 2, j * P:(j + 1) * P],
                                                       p_tok[:, u % 2, h, part * CK:(part + 1) * CK], core.ident[:, :])
                        last.then_inc(t_done, 1)

                def pv(u):
                    b, half = UNITS[u]
                    pe.wait_ge(copied_act, i * act_before[NC] + act_before[NCH * (u + 1)])
                    pe.wait_ge(copied_dve, i * dve_before[NC] + dve_before[NCH * (u + 1)])
                    if half == 0:
                        pe.wait_ge(y_done, i * B + b)
                    for h in range(HH):
                        for part in range(2):
                            last = nc.tensor.matmul(outp[:, half * HH + h, :], pT[:, u % 2, 2 * h + part, :],
                                                    v[:, b, part, half * HH + h, :], start=(part == 0), stop=(part == 1))
                    last.then_inc(pv_done, 1)

                def project(b):
                    n = i * B + b
                    pe.wait_ge(y_done, n + 1)
                    for k in range(KT):
                        last = nc.tensor.transpose(fin[:, 0, k * P:(k + 1) * P], y[:, k * P:(k + 1) * P], core.ident[:, :])
                    last.then_inc(yT_done, 1)
                    pe.wait_ge(yT_copied, n + 1)
                    for k in range(KT):
                        nc.tensor.matmul(fin[:, 1, :], yT[:, k, :], w["o"][:, k, :], start=(k == 0), stop=False)
                    pe.wait_ge(sum_done, n)
                    nc.tensor.matmul(fin[:, 1, :], core.ones_row[0:1, :], bias_row[0:1, 1, :],
                                     start=False, stop=True).then_inc(out_done, 1)

                queries(0)
                qk(0)
                for u in range(NU):
                    if u + 1 < NU:
                        if UNITS[u + 1][1] == 0:
                            queries(UNITS[u + 1][0])
                        qk(u + 1)
                    transposes(u)
                    if u >= 1:
                        pv(u - 1)
                        if UNITS[u - 1][1] == 1:
                            project(UNITS[u - 1][0])
                pv(NU - 1)
                project(B - 1)

        @block.scalar
        def _(act):
            for m in range(KT):
                act.wait_ge(kv_done, m + 1)
                if block_diagonal:
                    nc.scalar.activation(kT[:, m, :], scores[:, m, 0:B * CTX], ACT.Copy).then_inc(kv_copied, 1)
                else:
                    nc.scalar.activation(kT[:, m, :], scores[:, m, 0:B * CTX], ACT.Identity,
                                         bias=bias_col[:, 1, m:m + 1]).then_inc(kv_copied, 1)
            act.wait_ge(setup, 4)
            for n in range(2 * B):
                act.wait_ge(kv_done, KT + n + 1)
                nc.scalar.activation(v[:, n // 2, n % 2, :, 0:DH],
                                     tpose[0:CK, n % 2, 0:D].rearrange("p (h e) -> p h e", h=HEADS),
                                     ACT.Copy).then_inc(kv_copied, 1)
            with act.Fori(0, SEQ_TILES) as i:
                def queries(b):
                    act.wait_ge(q_done, i * B + b + 1)
                    if b == 0:
                        act.wait_ge(qk_done, i * NU)
                    for m in range(KT):
                        if block_diagonal:
                            nc.scalar.activation(qT[:, b, m, :], q_ps[:, m, :], ACT.Copy).then_inc(q_copied, 1)
                        else:
                            nc.scalar.activation(qT[:, b, m, :], q_ps[:, m, :], ACT.Identity,
                                                 bias=bias_col[:, 0, m:m + 1]).then_inc(q_copied, 1)

                def copies(u):
                    for c in range(NCH * u, NCH * (u + 1)):
                        if by_dve(c):
                            continue
                        act.wait_ge(t_done, i * NC + c + 1)
                        if u >= 2:
                            act.wait_ge(pv_done, i * NU + u - 1)
                        n = (c - NCH * u) * CHUNK
                        nc.scalar.activation(pT[:, u % 2, n:n + CHUNK, :].rearrange("p j q -> p (j q)"),
                                             tpose[0:CK, c % 2, :], ACT.Copy).then_inc(copied_act, 1)

                def yT_copy(b):
                    act.wait_ge(yT_done, i * B + b + 1)
                    act.wait_ge(out_done, i * B + b)
                    nc.scalar.activation(yT[:, :, :].rearrange("p k q -> p (k q)"), fin[:, 0, :], ACT.Copy).then_inc(yT_copied, 1)

                queries(0)
                for u in range(NU):
                    if u + 1 < NU and UNITS[u + 1][1] == 0:
                        queries(UNITS[u + 1][0])
                    act.wait_ge(sub_done, i * NU + u + 1)
                    nc.scalar.activation(p_tok[:, u % 2, 0:HH, :], p_tok[:, u % 2, 0:HH, :], ACT.Exp,
                                         scale=SCALE).then_inc(exp_done, 1)
                    copies(u)
                    if u >= 1 and UNITS[u - 1][1] == 1:
                        yT_copy(UNITS[u - 1][0])
                yT_copy(B - 1)

        @block.vector
        def _(dve):
            dve.wait_ge(mask_loaded, 16)
            nc.vector.tensor_scalar(mask[:, :, :], mask_raw[:, :, :], 0.0, mask_value[1],
                                    ALU.not_equal if mask_value[0] == "hidden" else ALU.is_equal, ALU.mult).then_inc(mask_ready, 1)
            dve.wait_ge(setup, 4)
            dve.wait_ge(kv_copied, KT)
            for b in range(B):
                for m in range(KT):
                    nc.vector.tensor_tensor(k_heads[:, b, m, :, :],
                                            kT[:, m, b * CTX:(b + 1) * CTX].rearrange("p (o n) -> p o n", o=1).to_broadcast([P, HH, CTX]),
                                            head_of[:, :].rearrange("p (h o) -> p h o", o=1).to_broadcast([P, HH, CTX]),
                                            ALU.mult).then_inc(kv_heads, 1)
            with dve.Fori(0, SEQ_TILES) as i:
                step = Links(dve, s_dve, i * (NU + B))

                def copies(u):
                    for c in range(NCH * u, NCH * (u + 1)):
                        if not by_dve(c):
                            continue
                        dve.wait_ge(t_done, i * NC + c + 1)
                        if u >= 2:
                            dve.wait_ge(pv_done, i * NU + u - 1)
                        n = (c - NCH * u) * CHUNK
                        nc.vector.tensor_copy(pT[:, u % 2, n:n + CHUNK, :].rearrange("p j q -> p (j q)"),
                                              tpose[0:CK, c % 2, :]).then_inc(copied_dve, 1)

                def normalise(b):
                    dve.wait_ge(pv_done, i * NU + 2 * b + 2)
                    step.after(nc.vector.reciprocal(inv_sum[:, :], outp[:, :, DH]))
                    dve.wait_ge(yT_done, i * B + b)
                    nc.vector.tensor_tensor(y[:, :].rearrange("p (h e) -> p h e", h=HEADS), outp[:, :, 0:DH],
                                            inv_sum[:, :].rearrange("p (h o) -> p h o", o=1).to_broadcast([P, HEADS, DH]),
                                            ALU.mult).then_inc(y_done, 1)

                def add(b):
                    dve.wait_ge(out_done, i * B + b + 1)
                    tile = bass.ds(i + b * SEQ_TILES, 1)
                    xt = core.x[:, tile, :].rearrange("p o c -> p (o c)")
                    nc.vector.tensor_tensor(xt, fin[:, 1, :], xt, ALU.add).then_inc(sum_done, 1)
                    dve.wait_ge(sum_done, i * B + b + 1)
                    nc.vector.bn_stats(core.stats[:, tile, :].rearrange("p o c -> p (o c)"), xt)

                for u in range(NU):
                    dve.wait_ge(qk_done, i * NU + u + 1)
                    sc = scores[:, :, 0:HB * CTX].rearrange("p c (h n) -> p c h n", h=HB)
                    step.after(nc.vector.tensor_reduce(s_max[:, :].rearrange("p (c h) -> p c h", c=SB), sc, AX, ALU.max))
                    if u >= 2:
                        dve.wait_ge(t_done, i * NC + NCH * (u - 1))
                    nc.vector.tensor_tensor(p_tok[:, u % 2, :, :].rearrange("p (c h) n -> p c h n", c=SB), sc,
                                            s_max[:, :].rearrange("p (c h o) -> p c h o", c=SB, o=1).to_broadcast([P, SB, HB, CTX]),
                                            ALU.subtract).then_inc(sub_done, 1)
                    if u >= 2 and UNITS[u - 2][1] == 1:
                        normalise(UNITS[u - 2][0])
                    copies(u)
                    if u >= 2 and UNITS[u - 2][1] == 1:
                        add(UNITS[u - 2][0])
                normalise(B - 1)
                add(B - 1)


def cross_attention_0(core, d):
    cross_attention(core, d, "x0", False, ("hidden", -1e18))


def cross_attention_1(core, d):
    cross_attention(core, d, "x1", True, ("seen", -1e20))


def lora_ffn(core, d):
    nc = core.nc
    H = 4 * D
    FT = H // P
    LORA, FIRST = 16, 1
    NP = LORA // 4
    BLOCKS = S // BANK
    BT = BANK // P
    W1_SETS = KT * H // BANK
    W2_SETS = FT // 2
    SETS = W1_SETS + W2_SETS
    RING = 4

    with ExitStack() as st:
        def sb(n, shape, dt=F32):
            return st.enter_context(nc.sbuf_tensor("ffn_" + n, shape, dt))

        def sem(n):
            return core.sem("ffn_" + n)

        w1T = sb("w1T", [P, KT, H])
        w2T = sb("w2T", [P, FT, D])
        w1 = sb("w1_seq", [P, B, KT, H])
        w2 = sb("w2_seq", [P, B, FT, D])
        b1 = sb("b1", [P, FT])
        b2 = sb("b2", [1, D])
        scale = sb("scale", [1, 1])
        tok = sb("lora_tok", [1, B, LORA, D])
        tok_scaled = sb("lora_scaled", [1, B, LORA, D])
        hidden = sb("hidden", [P, B, FT, BANK])
        ring = st.enter_context(nc.psum_tensor("ffn_ring", [P, RING, BANK], F32))
        outp = st.enter_context(nc.psum_tensor("ffn_out", [P, 2, BANK], F32))
        w_loaded, tok_loaded, tok_ready = sem("w_loaded"), sem("tok_loaded"), sem("tok_ready")
        outer_done, w_ready = sem("outer_done"), sem("w_ready")
        up_done, gelu_done, out_done, sum_done = sem("up_done"), sem("gelu_done"), sem("out_done"), sem("sum_done")
        block = st.enter_context(nc.Block())

        @block.sync
        def _(sp):
            for b in range(B):
                sp.dma_start(tok[0:1, b, :, :], core.x[FIRST:FIRST + LORA, b * SEQ_TILES, :]).then_inc(tok_loaded, 16)
            sp.dma_start(scale[:, :], d["L0_ffn_scale"]).then_inc(tok_loaded, 16)
            sp.dma_start(w1T[:, :, :], d["w1T"].rearrange("(k p) n -> p k n", p=P)).then_inc(w_loaded, 16)
            sp.dma_start(w2T[:, :, :], d["w2T"].rearrange("(k p) n -> p k n", p=P)).then_inc(w_loaded, 16)
            sp.dma_start(b1[:, :], d["L0_ffn_b1_cols"]).then_inc(w_loaded, 16)
            sp.dma_start(b2[:, :], d["L0_ffn_b2"].rearrange("(o n) -> o n", o=1)).then_inc(w_loaded, 16)

        @block.tensor
        def _(pe):
            pe.wait_ge(tok_ready, 1)
            for b in range(B):
                for n in range(SETS):
                    g = b * SETS + n
                    if g >= RING:
                        pe.wait_ge(w_ready, g - RING + 1)
                    if n < W1_SETS:
                        k, part = n // 2, n % 2
                        for i in range(2 * part, 2 * part + 2):
                            last = nc.tensor.matmul(ring[:, g % RING, (i % 2) * D:(i % 2 + 1) * D],
                                                    tok[0:1, b, 2 * i + 1, k * P:(k + 1) * P], tok_scaled[0:1, b, 2 * i, :],
                                                    start=True, stop=True)
                    else:
                        j = n - W1_SETS
                        for half in range(2):
                            for i in range(NP):
                                last = nc.tensor.matmul(
                                    ring[:, g % RING, half * D + i * (D // NP):half * D + (i + 1) * (D // NP)],
                                    tok[0:1, b, LORA // 2 + 2 * i + 1, half * P:(half + 1) * P],
                                    tok_scaled[0:1, b, LORA // 2 + 2 * i, :].rearrange("p (o j) -> p j o", j=4)[:, j, :],
                                    start=True, stop=True)
                    last.then_inc(outer_done, 1)
            pe.wait_ge(w_ready, B * SETS)
            with pe.Fori(0, BLOCKS) as i:
                for b in range(B):
                    for f in range(FT):
                        n = b * FT + f
                        if n >= RING:
                            pe.wait_ge(gelu_done, i * (B * FT) + n - RING + 1)
                        else:
                            pe.wait_ge(gelu_done, i * (B * FT))
                        for k in range(KT):
                            last = nc.tensor.matmul(ring[:, n % RING, :], w1[:, b, k, f * P:(f + 1) * P],
                                                    core.xT[:, k, bass.ds(i * BANK + b * S, BANK)],
                                                    start=(k == 0), stop=(k == KT - 1))
                        last.then_inc(up_done, 1)
                for b in range(B):
                    pe.wait_ge(gelu_done, i * (B * FT) + (b + 1) * FT)
                    for t in range(BT):
                        n = b * BT + t
                        if n >= 2:
                            pe.wait_ge(sum_done, i * (B * BT) + n - 1)
                        else:
                            pe.wait_ge(sum_done, i * (B * BT))
                        for f in range(FT):
                            nc.tensor.matmul(outp[:, n % 2, 0:D], hidden[:, b, f, t * P:(t + 1) * P], w2[:, b, f, :],
                                             start=(f == 0), stop=False)
                        nc.tensor.matmul(outp[:, n % 2, 0:D], core.ones_row[0:1, :], b2[0:1, :],
                                         start=False, stop=True).then_inc(out_done, 1)

        @block.scalar
        def _(act):
            act.wait_ge(w_loaded, 64)
            with act.Fori(0, BLOCKS) as i:
                for b in range(B):
                    act.wait_ge(out_done, i * (B * BT))
                    for f in range(FT):
                        n = b * FT + f
                        act.wait_ge(up_done, i * (B * FT) + n + 1)
                        nc.scalar.activation(hidden[:, b, f, :], ring[:, n % RING, :], ACT.Gelu,
                                             bias=b1[:, f:f + 1]).then_inc(gelu_done, 1)

        @block.vector
        def _(dve):
            dve.wait_ge(tok_loaded, 16 * (B + 1))
            nc.vector.tensor_scalar(tok_scaled[:, :, :, :], tok[:, :, :, :], scale[0:1, 0:1], None, ALU.mult).then_inc(tok_ready, 1)
            dve.wait_ge(w_loaded, 64)
            for b in range(B):
                for n in range(SETS):
                    g = b * SETS + n
                    dve.wait_ge(outer_done, g + 1)
                    if n < W1_SETS:
                        k, part = n // 2, n % 2
                        cols = slice(part * BANK, (part + 1) * BANK)
                        nc.vector.tensor_tensor(w1[:, b, k, cols], ring[:, g % RING, :], w1T[:, k, cols], ALU.add).then_inc(w_ready, 1)
                    else:
                        f = 2 * (n - W1_SETS)
                        nc.vector.tensor_tensor(w2[:, b, f:f + 2, :], ring[:, g % RING, :].rearrange("p (f c) -> p f c", f=2),
                                                w2T[:, f:f + 2, :], ALU.add).then_inc(w_ready, 1)
            with dve.Fori(0, BLOCKS) as i:
                for b in range(B):
                    for t in range(BT):
                        n = b * BT + t
                        dve.wait_ge(out_done, i * (B * BT) + n + 1)
                        tile = bass.ds(i * BT + (b * SEQ_TILES + t), 1)
                        xt = core.x[:, tile, :].rearrange("p o c -> p (o c)")
                        nc.vector.tensor_tensor(xt, outp[:, n % 2, 0:D], xt, ALU.add).then_inc(sum_done, 1)
                        dve.wait_ge(sum_done, i * (B * BT) + n + 1)
                        nc.vector.bn_stats(core.stats[:, tile, :].rearrange("p o c -> p (o c)"), xt)


def gated_linear_attention(core, d):
    nc = core.nc
    DK = D // 2 // HEADS
    DV = D // HEADS
    GATE_NORM = 16.0
    SCALE = DK ** -0.5
    R = 16
    G = B * S // BANK
    PER = 2
    UNITS = [(e, b) for e in range(PER) for b in range(B)]
    NU = len(UNITS)

    with ExitStack() as st:
        def sb(n, shape, dt=F32):
            return st.enter_context(nc.sbuf_tensor("gla_" + n, shape, dt))

        def sem(n):
            return core.sem("gla_" + n)

        w_q, w_k = sb("w_q", [P, KT, P]), sb("w_k", [P, KT, P])
        w_g1, w_g2 = sb("w_g1", [P, KT, R]), sb("w_g2", [R, P])
        w_v, w_g, w_o = sb("w_v", [P, KT, D]), sb("w_g", [P, KT, D]), sb("w_o", [P, KT, D])
        b_g = sb("b_g", [P, KT])
        w_ve = sb("w_ve", [P, PER, KT, P])
        head_sel = sb("head_sel", [P, HEADS])
        qT, kT = sb("q_chan", [P, B * S]), sb("k_chan", [P, B * S])
        g1T = sb("g1_chan", [R, B * S])
        decay = sb("decay", [P, B * S])
        tmp = sb("tmp", [P, B * S])
        gate = sb("gate", [P, KT, B * S])
        kv = sb("kv", [P, 2, S])
        state = sb("state", [P, 2, S])
        qs = sb("q_state", [P, 2, S])
        o = sb("o_tok", [P, TILES, DV, HEADS])
        on = sb("o_norm", [P, TILES, D])
        mu, var, rs = sb("o_mean", [P, TILES * HEADS]), sb("o_var", [P, TILES * HEADS]), sb("o_rstd", [P, TILES * HEADS])
        half = sb("minus_half", [P, TILES * HEADS])
        gT = sb("gated_chan", [P, 2, KT, P])
        ring = st.enter_context(nc.psum_tensor("gla_ring", [P, 4, BANK], F32))
        o_ps = st.enter_context(nc.psum_tensor("gla_o", [P, 2, BANK], F32))
        fin = st.enter_context(nc.psum_tensor("gla_fin", [P, 2, BANK], F32))
        w_loaded, setup, s_dve = sem("w_loaded"), sem("setup"), sem("dve_steps")
        proj_done, proj_copied = sem("proj_done"), sem("proj_copied")
        abs_done, softplus_done, log_done, decay_done, s_act = (sem("abs_done"), sem("softplus_done"), sem("log_done"),
                                                                sem("decay_done"), sem("act_steps"))
        wve_done, v_done, kv_done, scan_done, qs_done, o_done, o_copied = (
            sem("wve_done"), sem("v_done"), sem("kv_done"), sem("scan_done"), sem("qs_done"), sem("o_done"), sem("o_copied"))
        var_done, rs_done, on_done = sem("var_done"), sem("rs_done"), sem("on_done")
        oT_done, gT_done, out_done, sum_done = sem("oT_done"), sem("gT_done"), sem("out_done"), sem("sum_done")
        block = st.enter_context(nc.Block())
        WN = 8

        @block.sync
        def _(sp):
            for t, n in ((w_q, "Wq"), (w_k, "Wk"), (w_g1, "Wg1"), (w_v, "Wv"), (w_g, "Wg"), (w_o, "Wo")):
                sp.dma_start(t[:, :, :], d["L1_attn_" + n].rearrange("(k p) n -> p k n", p=P)).then_inc(w_loaded, 16)
            sp.dma_start(w_g2[:, :], d["L1_attn_Wg2"]).then_inc(w_loaded, 16)
            sp.dma_start(b_g[:, :], d["L1_attn_bg_cols"]).then_inc(w_loaded, 16)

        PROJ = [(n, g) for n in ("q", "k", "g1", "z0", "z1", "kg") for g in range(G)]

        @block.tensor
        def _(pe):
            pe.wait_ge(w_loaded, 16 * WN)
            for n, (what, g) in enumerate(PROJ):
                if n >= 4:
                    pe.wait_ge(proj_copied, n - 3)
                cols = slice(g * BANK, (g + 1) * BANK)
                if what == "kg":
                    pe.wait_ge(proj_copied, PROJ.index(("g1", g)) + 1)
                    last = nc.tensor.matmul(ring[:, n % 4, :], w_g2[:, :], g1T[:, cols], start=True, stop=True)
                else:
                    w, rows = {"q": (w_q, P), "k": (w_k, P), "g1": (w_g1, R), "z0": (w_g[:, :, 0:P], P),
                               "z1": (w_g[:, :, P:2 * P], P)}[what]
                    for k in range(KT):
                        last = nc.tensor.matmul(ring[0:rows, n % 4, :], w[:, k, :], core.xT[:, k, cols],
                                                start=(k == 0), stop=(k == KT - 1))
                last.then_inc(proj_done, 1)
            pe.wait_ge(proj_copied, len(PROJ))
            pe.wait_ge(setup, 3)
            with pe.Fori(0, DV // PER) as i:
                def values(u):
                    e, b = UNITS[u]
                    pe.wait_ge(wve_done, i * PER + e + 1)
                    pe.wait_ge(kv_done, i * NU + u - 1) if u >= 2 else pe.wait_ge(kv_done, i * NU)
                    for c in range(S // BANK):
                        for k in range(KT):
                            last = nc.tensor.matmul(ring[:, 2 * (u % 2) + c, :], w_ve[:, e, k, :],
                                                    core.xT[:, k, b * S + c * BANK:b * S + (c + 1) * BANK],
                                                    start=(k == 0), stop=(k == KT - 1))
                    last.then_inc(v_done, 1)

                def outputs(u):
                    pe.wait_ge(qs_done, i * NU + u + 1)
                    pe.wait_ge(o_copied, i * NU + u - 1) if u >= 2 else pe.wait_ge(o_copied, i * NU)
                    for t in range(SEQ_TILES):
                        last = nc.tensor.matmul(o_ps[:, u % 2, t * HEADS:(t + 1) * HEADS], qs[:, u % 2, t * P:(t + 1) * P],
                                                head_sel[:, :], start=True, stop=True)
                    last.then_inc(o_done, 1)

                values(0)
                values(1)
                for u in range(NU):
                    if u + 2 < NU:
                        values(u + 2)
                    outputs(u)
            pe.wait_ge(on_done, 1)

            def project(t):
                pe.wait_ge(gT_done, t + 1)
                if t >= 2:
                    pe.wait_ge(sum_done, t - 1)
                for k in range(KT):
                    last = nc.tensor.matmul(fin[:, t % 2, 0:D], gT[:, t % 2, k, :], w_o[:, k, :],
                                            start=(k == 0), stop=(k == KT - 1))
                last.then_inc(out_done, 1)

            for t in range(TILES):
                if t >= 2:
                    pe.wait_ge(gT_done, t - 1)
                for k in range(KT):
                    last = nc.tensor.transpose(ring[:, t % 2, k * P:(k + 1) * P], on[:, t, k * P:(k + 1) * P], core.ident[:, :])
                last.then_inc(oT_done, 1)
                if t >= 1:
                    project(t - 1)
            project(TILES - 1)

        @block.gpsimd
        def _(pool):
            nc.gpsimd.memset(half[:, :], -0.5)
            step = Links(pool, setup)
            step.after(nc.gpsimd.memset(head_sel[:, :], 1.0))
            step.after(nc.gpsimd.affine_select(out=head_sel[:, :], in_=head_sel[:, :], compare_op=ALU.is_ge, fill=0.0,
                                               base=0, pattern=[[-DK, HEADS]], channel_multiplier=1))
            step.after(nc.gpsimd.affine_select(out=head_sel[:, :], in_=head_sel[:, :], compare_op=ALU.is_ge, fill=0.0,
                                               base=DK - 1, pattern=[[DK, HEADS]], channel_multiplier=-1))
            pool.wait_ge(proj_copied, len(PROJ))
            with pool.Fori(0, DV // PER) as i:
                for u, (e, b) in enumerate(UNITS):
                    pool.wait_ge(scan_done, i * NU + u + 1)
                    pool.wait_ge(o_done, i * NU + u - 1) if u >= 2 else pool.wait_ge(o_done, i * NU)
                    nc.gpsimd.tensor_tensor(qs[:, u % 2, :], state[:, u % 2, :], qT[:, b * S:(b + 1) * S],
                                            ALU.mult).then_inc(qs_done, 1)
            pool.wait_ge(var_done, 1)
            nc.gpsimd.tensor_tensor(rs[:, :], var[:, :], half[:, :], ALU.pow).then_inc(rs_done, 1)

        @block.scalar
        def _(act):
            act.wait_ge(w_loaded, 16 * WN)
            for n, (what, g) in enumerate(PROJ):
                act.wait_ge(proj_done, n + 1)
                cols = slice(g * BANK, (g + 1) * BANK)
                if what == "q":
                    nc.scalar.activation(qT[:, cols], ring[:, n % 4, :], ACT.Copy).then_inc(proj_copied, 1)
                elif what == "k":
                    nc.scalar.activation(kT[:, cols], ring[:, n % 4, :], ACT.Copy, scale=SCALE).then_inc(proj_copied, 1)
                elif what == "g1":
                    nc.scalar.activation(g1T[:, cols], ring[0:R, n % 4, :], ACT.Copy).then_inc(proj_copied, 1)
                elif what == "kg":
                    nc.scalar.activation(decay[:, cols], ring[:, n % 4, :], ACT.Copy).then_inc(proj_copied, 1)
                else:
                    k = int(what[1])
                    nc.scalar.activation(gate[:, k, cols], ring[:, n % 4, :], ACT.Silu, bias=b_g[:, k:k + 1]).then_inc(proj_copied, 1)
            act.wait_ge(abs_done, 1)
            nc.scalar.activation(tmp[:, :], tmp[:, :], ACT.Exp, scale=-1.0).then_inc(s_act, 1)
            act.wait_ge(s_act, 1)
            nc.scalar.activation(tmp[:, :], tmp[:, :], ACT.Ln, bias=1.0).then_inc(softplus_done, 1)
            act.wait_ge(log_done, 1)
            nc.scalar.activation(decay[:, :], decay[:, :], ACT.Exp, scale=1.0 / GATE_NORM).then_inc(decay_done, 1)
            with act.Fori(0, DV // PER) as i:
                for u, (e, b) in enumerate(UNITS):
                    if b == 0:
                        act.wait_ge(v_done, i * NU)
                        src = w_v[:, :, :].rearrange("p k (h e) -> p k h e", h=HEADS)[:, :, :, bass.ds(i * PER + e, 1)]
                        for k in range(KT):
                            last = nc.scalar.activation(w_ve[:, e, k, :].rearrange("p (h c) -> p h c", h=HEADS),
                                                        src[:, k, :, :].to_broadcast([P, HEADS, DK]), ACT.Copy)
                        last.then_inc(wve_done, 1)
                for u, (e, b) in enumerate(UNITS):
                    act.wait_ge(o_done, i * NU + u + 1)
                    dst = o[:, b * SEQ_TILES:(b + 1) * SEQ_TILES, bass.ds(i * PER + e, 1), :].rearrange("p t o h -> p t (o h)")
                    nc.scalar.activation(dst, o_ps[:, u % 2, 0:SEQ_TILES * HEADS].rearrange("p (t h) -> p t h", h=HEADS),
                                         ACT.Copy).then_inc(o_copied, 1)

        @block.vector
        def _(dve):
            step = Links(dve, s_dve)
            dve.wait_ge(proj_copied, len(PROJ))
            nc.vector.scalar_tensor_tensor(tmp[:, :], decay[:, :], -1.0, decay[:, :], ALU.mult, ALU.max).then_inc(abs_done, 1)
            dve.wait_ge(softplus_done, 1)
            nc.vector.scalar_tensor_tensor(decay[:, :], decay[:, :], 0.0, tmp[:, :], ALU.min, ALU.subtract).then_inc(log_done, 1)
            dve.wait_ge(decay_done, 1)
            with dve.Fori(0, DV // PER) as i:
                for u, (e, b) in enumerate(UNITS):
                    dve.wait_ge(v_done, i * NU + u + 1)
                    nc.vector.tensor_tensor(kv[:, u % 2, :], ring[:, 2 * (u % 2):2 * (u % 2) + 2, :].rearrange("p c n -> p (c n)"),
                                            kT[:, b * S:(b + 1) * S], ALU.mult).then_inc(kv_done, 1)
                    dve.wait_ge(kv_done, i * NU + u + 1)
                    dve.wait_ge(qs_done, i * NU + u - 1) if u >= 2 else dve.wait_ge(qs_done, i * NU)
                    nc.vector.tensor_tensor_scan(state[:, u % 2, :], decay[:, b * S:(b + 1) * S], kv[:, u % 2, :], 0.0,
                                                 ALU.mult, ALU.add).then_inc(scan_done, 1)
            dve.wait_ge(o_copied, DV * B)
            by_head = o[:, :, :, :].rearrange("p t e h -> p t h e")
            onv = on[:, :, :].rearrange("p t (h e) -> p t h e", h=HEADS)

            def wide(a):
                return a[:, :].rearrange("p (t h o) -> p t h o", t=TILES, o=1).to_broadcast([P, TILES, HEADS, DV])

            step.after(nc.vector.tensor_reduce(mu[:, :].rearrange("p (t h) -> p t h", h=HEADS), by_head, AX, ALU.add))
            step.after(nc.vector.tensor_scalar(mu[:, :], mu[:, :], 1.0 / DV, None, ALU.mult))
            step.after(nc.vector.tensor_tensor(onv, by_head, wide(mu), ALU.subtract))
            o2 = o[:, :, :, :].rearrange("p t e h -> p t (e h)")
            step.after(nc.vector.tensor_tensor(o2, on[:, :, :], on[:, :, :], ALU.mult))
            step.after(nc.vector.tensor_reduce(var[:, :].rearrange("p (t h) -> p t h", h=HEADS),
                                               o2.rearrange("p t (h e) -> p t h e", h=HEADS), AX, ALU.add))
            nc.vector.tensor_scalar(var[:, :], var[:, :], 1.0 / DV, EPS, ALU.mult, ALU.add).then_inc(var_done, 1)
            dve.wait_ge(rs_done, 1)
            nc.vector.tensor_tensor(onv, onv, wide(rs), ALU.mult).then_inc(on_done, 1)
            for t in range(TILES + 1):
                if t < TILES:
                    dve.wait_ge(oT_done, t + 1)
                    if t >= 2:
                        dve.wait_ge(out_done, t - 1)
                    nc.vector.tensor_tensor(gT[:, t % 2, :, :], ring[:, t % 2, 0:D].rearrange("p (k q) -> p k q", k=KT),
                                            gate[:, :, t * P:(t + 1) * P], ALU.mult).then_inc(gT_done, 1)
                if t >= 1:
                    dve.wait_ge(out_done, t)
                    nc.vector.tensor_tensor(core.x[:, t - 1, :], fin[:, (t - 1) % 2, 0:D], core.x[:, t - 1, :], ALU.add).then_inc(sum_done, 1)
                    dve.wait_ge(sum_done, t)
                    nc.vector.bn_stats(core.stats[:, t - 1, :], core.x[:, t - 1, :])


def expert_ffn(core, d):
    nc = core.nc
    E, K, F = EXPERTS, TOP, 512
    CAP = CAPACITY
    FT = F // P
    CT = CAP // P
    PARTS = [(0, 3), (3, CT)]
    PER = 2
    N = TILES * E
    UPS = FT * len(PARTS)
    TPS = KT * len(PARTS)
    GR = 4

    with ExitStack() as st:
        def sb(n, shape, dt=F32):
            return st.enter_context(nc.sbuf_tensor("moe_" + n, shape, dt))

        def sem(n):
            return core.sem("moe_" + n)

        w_r = sb("w_router", [P, KT, E])
        b_r = sb("b_router", [1, E])
        before = sb("before", [P, P])
        ones = sb("ones", [P, P])
        e_less8 = sb("e_less8", [P, E])
        e_row = sb("e_row", [P, E])
        spare = sb("spare", [P, K, TILES])
        logit, prob, hit, rest = (sb(n, [P, TILES, E]) for n in ("logit", "prob", "hit", "rest"))
        best = [sb(f"best{k}", [P, TILES, E]) for k in range(K)]
        chosen = sb("chosen", [P, TILES, E])
        upto = sb("upto", [P, TILES, E])
        rank = sb("rank", [P, TILES, E])
        row = [sb(f"row{n}", [P, TILES]) for n in range(3)]
        p_best = sb("p_best", [P, K, TILES])
        weight = sb("weight", [P, K, TILES])
        rk, slot, keep = (sb(n, [P, K, TILES]) for n in ("rk", "slot", "keep"))
        to_row = sb("to_row", [P, K, TILES], I32)
        from_row = sb("from_row", [P, K, TILES], I32)
        xe = sb("x_expert", [P, PER, CT, D])
        xeT = sb("x_expert_chan", [P, PER, KT, CAP])
        w1, w2 = sb("w1", [P, PER, KT, F]), sb("w2", [P, PER, FT, D])
        b1, b2 = sb("b1", [P, PER, FT]), sb("b2", [1, PER, D])
        hidden = sb("hidden", [P, PER, FT, CAP])
        ye = sb("y_expert", [P, PER, CT, D])
        got = sb("gathered", [P, GR, K, D])
        route = st.enter_context(nc.psum_tensor("moe_route", [P, BANK], F32))
        tp = st.enter_context(nc.psum_tensor("moe_tp", [P, 2, BANK], F32))
        up = st.enter_context(nc.psum_tensor("moe_up", [P, 3, BANK], F32))
        dn = st.enter_context(nc.psum_tensor("moe_dn", [P, 2, BANK], F32))

        r_loaded, setup, s_dve, logits_done, shifted, exp_done, chosen_done, rank_done, rows_ready = (
            sem(n) for n in ("r_loaded", "setup", "dve_steps", "logits_done", "shifted", "exp_done", "chosen_done",
                             "rank_done", "rows_ready"))
        x_loaded = [sem(f"x_loaded{m}") for m in range(PER)]
        scattered, w_loaded, tp_done, tp_copied, up_done, gelu_done, dn_done, dn_copied, stored = (
            sem(n) for n in ("scattered", "w_loaded", "tp_done", "tp_copied", "up_done", "gelu_done",
                             "dn_done", "dn_copied", "stored"))
        gathered = [sem(f"gathered{n}") for n in range(GR)]
        summed = sem("summed")
        block = st.enter_context(nc.Block())

        @block.sync
        def _(sp):
            sp.dma_start(w_r[:, :, :], d["L1_ffn_router_w"].rearrange("(k p) n -> p k n", p=P)).then_inc(r_loaded, 16)
            sp.dma_start(b_r[:, :], d["L1_ffn_router_b"].rearrange("(o n) -> o n", o=1)).then_inc(r_loaded, 16)
            rows = core.by_expert[0:E * CAP, :].rearrange("(e t p) c -> e p t c", e=E, p=P)
            results = core.y_by_expert[:, :].rearrange("(e t p) c -> e p t c", e=E, p=P)
            with sp.Fori(0, E // PER) as r:
                e = r * PER
                for m in range(PER):
                    sp.wait_ge(dn_done, e * CT)
                    sp.dma_start(w1[:, m, :, :], d["moe_w1"][e + m].rearrange("(k p) n -> p k n", p=P)).then_inc(w_loaded, 16)
                    sp.dma_start(w2[:, m, :, :], d["moe_w2"][e + m].rearrange("(k p) n -> p k n", p=P)).then_inc(w_loaded, 16)
                    sp.dma_start(b1[:, m, :], d["moe_b1_cols"][e + m]).then_inc(w_loaded, 16)
                    sp.dma_start(b2[0:1, m, :], d["moe_b2"][e + m].rearrange("(o n) -> o n", o=1)).then_inc(w_loaded, 16)
                for m in range(PER):
                    sp.wait_ge(scattered, 16 * K * TILES)
                    sp.wait_ge(tp_done, e * TPS)
                    sp.dma_start(xe[:, m, :, :], rows[e + m]).then_inc(x_loaded[m], 16)
                for m in range(PER):
                    sp.wait_ge(dn_copied, e * CT + (m + 1) * CT)
                    sp.dma_start(results[e + m], ye[:, m, :, :]).then_inc(stored, 16)

        @block.tensor
        def _(pe):
            pe.wait_ge(r_loaded, 32)
            for t in range(TILES):
                dst = route[:, t * E:(t + 1) * E]
                for k in range(KT):
                    nc.tensor.matmul(dst, core.xT[:, k, t * P:(t + 1) * P], w_r[:, k, :], start=(k == 0), stop=False)
                last = nc.tensor.matmul(dst, core.ones_row[0:1, :], b_r[0:1, :], start=False, stop=True)
            last.then_inc(logits_done, 1)
            pe.wait_ge(chosen_done, 1)
            pe.wait_ge(setup, 6)
            ch = chosen[:, :, :].rearrange("p t e -> p (t e)")
            nc.tensor.matmul(route[:, N:2 * N], before[:, :], ch, start=True, stop=True)
            nc.tensor.matmul(route[:, 2 * N:3 * N], ones[:, :], ch, start=True, stop=True).then_inc(rank_done, 1)
            with pe.Fori(0, E // PER) as r:
                e = r * PER
                for m in range(PER):
                    pe.wait_ge(x_loaded[m], r * 16 + 16)
                    n = 0
                    for lo, hi in PARTS:
                        for k in range(KT):
                            if m * TPS + n >= 2:
                                pe.wait_ge(tp_copied, e * TPS + m * TPS + n - 1)
                            else:
                                pe.wait_ge(tp_copied, e * TPS)
                            for t in range(lo, hi):
                                last = nc.tensor.transpose(tp[:, n % 2, (t - lo) * P:(t - lo + 1) * P],
                                                           xe[:, m, t, k * P:(k + 1) * P], core.ident[:, :])
                            last.then_inc(tp_done, 1)
                            n += 1
                    pe.wait_ge(w_loaded, e * 64 + 64 * PER)
                    n = 0
                    for q, (lo, hi) in enumerate(PARTS):
                        pe.wait_ge(tp_copied, e * TPS + m * TPS + (q + 1) * KT)
                        for f in range(FT):
                            if m * UPS + n >= 3:
                                pe.wait_ge(gelu_done, e * UPS + m * UPS + n - 2)
                            else:
                                pe.wait_ge(gelu_done, e * UPS)
                            for k in range(KT):
                                last = nc.tensor.matmul(up[:, (m * UPS + n) % 3, 0:(hi - lo) * P], w1[:, m, k, f * P:(f + 1) * P],
                                                        xeT[:, m, k, lo * P:hi * P], start=(k == 0), stop=(k == KT - 1))
                            last.then_inc(up_done, 1)
                            n += 1
                    pe.wait_ge(gelu_done, e * UPS + (m + 1) * UPS)
                    for t in range(CT):
                        n = m * CT + t
                        if n >= 2:
                            pe.wait_ge(dn_copied, e * CT + n - 1)
                        else:
                            pe.wait_ge(dn_copied, e * CT)
                        for f in range(FT):
                            nc.tensor.matmul(dn[:, n % 2, 0:D], hidden[:, m, f, t * P:(t + 1) * P], w2[:, m, f, :],
                                             start=(f == 0), stop=False)
                        nc.tensor.matmul(dn[:, n % 2, 0:D], core.ones_row[0:1, :], b2[0:1, m, :],
                                         start=False, stop=True).then_inc(dn_done, 1)

        @block.scalar
        def _(act):
            act.wait_ge(shifted, 1)
            nc.scalar.activation(prob[:, :, :], logit[:, :, :], ACT.Exp).then_inc(exp_done, 1)
            with act.Fori(0, E // PER) as r:
                e = r * PER
                for m in range(PER):
                    act.wait_ge(dn_done, e * CT)
                    n = 0
                    for q, (lo, hi) in enumerate(PARTS):
                        for f in range(FT):
                            act.wait_ge(up_done, e * UPS + m * UPS + n + 1)
                            nc.scalar.activation(hidden[:, m, f, lo * P:hi * P], up[:, (m * UPS + n) % 3, 0:(hi - lo) * P],
                                                 ACT.Gelu, bias=b1[:, m, f:f + 1]).then_inc(gelu_done, 1)
                            n += 1

        @block.gpsimd
        def _(pool):
            step = Links(pool, setup)
            nc.gpsimd.memset(ones[:, :], 1.0)
            step.after(nc.gpsimd.memset(before[:, :], 1.0))
            step.after(nc.gpsimd.affine_select(out=before[:, :], in_=before[:, :], compare_op=ALU.is_gt, fill=0.0,
                                               base=0, pattern=[[1, P]], channel_multiplier=-1))
            step.after(nc.gpsimd.iota(e_less8[:, :], pattern=[[1, E]], base=-E, channel_multiplier=0,
                                      allow_small_or_imprecise_dtypes=True))
            step.after(nc.gpsimd.iota(e_row[:, :], pattern=[[CAP, E]], base=0, channel_multiplier=0,
                                      allow_small_or_imprecise_dtypes=True))
            step.after(nc.gpsimd.iota(spare[:, :, :], pattern=[[B * S, K], [P, TILES]], base=E * CAP, channel_multiplier=1,
                                      allow_small_or_imprecise_dtypes=True))
            step.after(nc.gpsimd.memset(upto[:, :, :], 1.0))
            pool.wait_ge(core.zeroed, 16)
            pool.wait_ge(rows_ready, 1)
            for t in range(TILES):
                for k in range(K):
                    nc.gpsimd.indirect_dma_start(out=core.by_expert[:, :],
                                                 out_offset=bass.IndirectOffsetOnAxis(ap=to_row[:, k, t:t + 1], axis=0),
                                                 in_=core.x[:, t, :], in_offset=None).then_inc(scattered, 16)
            pool.wait_ge(stored, 16 * E)
            for t in range(TILES):
                if t >= GR:
                    pool.wait_ge(summed, t - GR + 1)
                for k in range(K):
                    nc.gpsimd.indirect_dma_start(out=got[:, t % GR, k, :], out_offset=None, in_=core.y_by_expert[:, :],
                                                 in_offset=bass.IndirectOffsetOnAxis(ap=from_row[:, k, t:t + 1], axis=0)
                                                 ).then_inc(gathered[t % GR], 16)

        @block.vector
        def _(dve):
            step = Links(dve, s_dve)
            shape = [P, TILES, E]

            def per_tile(a):
                return a.rearrange("p (t o) -> p t o", o=1).to_broadcast(shape)

            def per_expert(a):
                return a[:, :].rearrange("p (o e) -> p o e", o=1).to_broadcast(shape)

            def combine(out, a, b, op):
                step.after(nc.vector.tensor_tensor(out, a, b, op))

            dve.wait_ge(logits_done, 1)
            lg = route[:, 0:N].rearrange("p (t e) -> p t e", e=E)
            step.after(nc.vector.tensor_reduce(row[0][:, :], lg, AX, ALU.max))
            nc.vector.tensor_tensor(logit[:, :, :], lg, per_tile(row[0][:, :]), ALU.subtract).then_inc(shifted, 1)
            dve.wait_ge(exp_done, 1)
            step.after(nc.vector.tensor_reduce(row[1][:, :], prob[:, :, :], AX, ALU.add))
            step.after(nc.vector.reciprocal(row[2][:, :], row[1][:, :]))
            combine(prob[:, :, :], prob[:, :, :], per_tile(row[2][:, :]), ALU.mult)
            dve.wait_ge(setup, 6)
            left = prob
            for k in range(K):
                step.after(nc.vector.tensor_reduce(p_best[:, k, :], left[:, :, :], AX, ALU.max))
                combine(hit[:, :, :], left[:, :, :], per_tile(p_best[:, k, :]), ALU.is_equal)
                combine(hit[:, :, :], hit[:, :, :], per_expert(e_less8), ALU.mult)
                step.after(nc.vector.tensor_reduce(row[0][:, :], hit[:, :, :], AX, ALU.min))
                combine(best[k][:, :, :], per_expert(e_less8), per_tile(row[0][:, :]), ALU.is_equal)
                if k + 1 < K:
                    step.after(nc.vector.scalar_tensor_tensor(rest[:, :, :], best[k][:, :, :], -2.0, left[:, :, :], ALU.mult, ALU.add))
                    left = rest
            combine(chosen[:, :, :], best[0][:, :, :], best[1][:, :, :], ALU.add)
            dve.sem_inc(chosen_done, 1)
            combine(row[1][:, :], p_best[:, 0, :], p_best[:, 1, :], ALU.add)
            step.after(nc.vector.tensor_scalar(row[1][:, :], row[1][:, :], 1e-9, None, ALU.max))
            step.after(nc.vector.reciprocal(row[2][:, :], row[1][:, :]))
            for k in range(K):
                combine(weight[:, k, :], p_best[:, k, :], row[2][:, :], ALU.mult)
            dve.wait_ge(rank_done, 1)
            totals = route[:, 2 * N:3 * N].rearrange("p (t e) -> p t e", e=E)
            for e in range(E):
                last = nc.vector.tensor_tensor_scan(rest[:, :, e], upto[:, :, e], totals[:, :, e], 0.0, ALU.mult, ALU.add)
            step.after(last)
            combine(rest[:, :, :], rest[:, :, :], totals, ALU.subtract)
            combine(rank[:, :, :], rest[:, :, :], route[:, N:2 * N].rearrange("p (t e) -> p t e", e=E), ALU.add)
            for k in range(K):
                combine(hit[:, :, :], best[k][:, :, :], rank[:, :, :], ALU.mult)
                step.after(nc.vector.tensor_reduce(rk[:, k, :], hit[:, :, :], AX, ALU.add))
                combine(hit[:, :, :], best[k][:, :, :], per_expert(e_row), ALU.mult)
                step.after(nc.vector.tensor_reduce(slot[:, k, :], hit[:, :, :], AX, ALU.add))
            combine(slot[:, :, :], slot[:, :, :], rk[:, :, :], ALU.add)
            step.after(nc.vector.tensor_scalar(keep[:, :, :], rk[:, :, :], float(CAP), None, ALU.is_lt))
            combine(weight[:, :, :], weight[:, :, :], keep[:, :, :], ALU.mult)
            combine(from_row[:, :, :], slot[:, :, :], keep[:, :, :], ALU.mult)
            combine(slot[:, :, :], slot[:, :, :], spare[:, :, :], ALU.subtract)
            combine(slot[:, :, :], slot[:, :, :], keep[:, :, :], ALU.mult)
            combine(to_row[:, :, :], slot[:, :, :], spare[:, :, :], ALU.add)
            dve.sem_inc(rows_ready, 1)
            with dve.Fori(0, E // PER) as r:
                e = r * PER
                for m in range(PER):
                    dve.wait_ge(up_done, e * UPS)
                    n = 0
                    for lo, hi in PARTS:
                        for k in range(KT):
                            dve.wait_ge(tp_done, e * TPS + m * TPS + n + 1)
                            nc.vector.tensor_copy(xeT[:, m, k, lo * P:hi * P], tp[:, n % 2, 0:(hi - lo) * P]).then_inc(tp_copied, 1)
                            n += 1
                    dve.wait_ge(stored, e * 16)
                    for t in range(CT):
                        n = m * CT + t
                        dve.wait_ge(dn_done, e * CT + n + 1)
                        nc.vector.tensor_copy(ye[:, m, t, :], dn[:, n % 2, 0:D]).then_inc(dn_copied, 1)
            for t in range(TILES):
                dve.wait_ge(gathered[t % GR], 16 * K * (t // GR + 1))
                for k in range(K):
                    last = nc.vector.scalar_tensor_tensor(core.x[:, t, :], got[:, t % GR, k, :], weight[:, k, t:t + 1],
                                                          core.x[:, t, :], ALU.mult, ALU.add)
                    step.after(last)
                nc.vector.bn_stats(core.stats[:, t, :], core.x[:, t, :]).then_inc(summed, 1)


LAYERS = [latent_attention, cross_attention_0, lora_ffn, gated_linear_attention, cross_attention_1, expert_ffn]


def build(nc, d, out, layers=range(len(LAYERS))):
    with ExitStack() as stack:
        core = Core(nc, stack)
        constants_and_loads(core, d)
        for nth, n in enumerate(layers):
            LAYERS[n](core, d)
            layer_norm(core, nth, out if n == layers[-1] else None)


def arrays_of(inputs):
    import numpy as np
    a = {n: np.ascontiguousarray(v) for n, v in inputs.items()}
    a["x_chan"] = np.ascontiguousarray(a["x"].reshape(B * S, D).T)
    a["ctx_chan"] = np.ascontiguousarray(a["ctx_1024"].reshape(B * CTX, D).T)
    a["w_q_pairs"] = np.ascontiguousarray(a["L0_attn_w_q"].reshape(KT, P, 8, P).transpose(2, 1, 0, 3))
    a["w_kv_up_pairs"] = np.ascontiguousarray(a["L0_attn_w_kv_up"].reshape(P, 16, P).transpose(1, 0, 2))
    a["x0_mask"] = a.pop("mask_BxSxS2_bf0")
    a["x1_mask"] = a.pop("mask_Bx1xSxS2_ik1").reshape(B, S, CTX)
    for n in ("Wq", "Wk", "Wv", "Wo", "bq", "bk", "bv", "bo"):
        a["x0_" + n] = a.pop("L0_xattn_" + n)
    for n in ("Wq", "Wk", "Wv", "Wo"):
        a["x1_" + n] = np.ascontiguousarray(a.pop("L1_xattn_" + n).T)
    a["w1T"] = np.ascontiguousarray(a.pop("L0_ffn_W1").T)
    a["w2T"] = np.ascontiguousarray(a.pop("L0_ffn_W2").T)
    a["L0_ffn_b1_cols"] = np.ascontiguousarray(a.pop("L0_ffn_b1").reshape(-1, P).T)
    a["L0_ffn_scale"] = a["L0_ffn_scale"].reshape(1, 1)
    a["L1_attn_bg_cols"] = np.ascontiguousarray(a.pop("L1_attn_bg").reshape(-1, P).T)
    a["moe_w1"], a["moe_w2"], a["moe_b2"] = a.pop("L1_ffn_w1"), a.pop("L1_ffn_w2"), a.pop("L1_ffn_b2")
    a["moe_b1_cols"] = np.ascontiguousarray(a.pop("L1_ffn_b1").reshape(EXPERTS, -1, P).transpose(0, 2, 1))
    a["x1_bo"] = a.pop("L1_xattn_bo")
    return a


def kernel(**inputs):
    import numpy as np
    from concourse import bacc
    from concourse.bass_utils import run_bass_kernel_spmd

    nc = bacc.Bacc("TRN2", target_bir_lowering=False, num_devices=1)
    arrays = {"in_" + n: v for n, v in arrays_of({n: np.asarray(v) for n, v in inputs.items()}).items()}
    d = {n[3:]: nc.dram_tensor(n, v.shape, mybir.dt.from_np(v.dtype), kind="ExternalInput").ap() for n, v in arrays.items()}
    out = nc.dram_tensor("out", (B, S, D), F32, kind="ExternalOutput").ap()
    build(nc, d, out)
    return run_bass_kernel_spmd(nc, [arrays], core_ids=[0]).results[0]["out"]
```

```python
import concourse.bass as bass
from concourse import mybir
from contextlib import ExitStack

F32 = mybir.dt.float32
F32R = mybir.dt.float32r
BF16 = mybir.dt.bfloat16
I32 = mybir.dt.int32
U8 = mybir.dt.uint8
ALU = mybir.AluOpType
ACT = mybir.ActivationFunctionType
AX = mybir.AxisListType.X

P = 128
B, S, D = 2, 1024, 256
CTX = 154
KT = D // P
TILES = B * S // P
SEQ_TILES = S // P
HEADS = 16
EPS = 1e-5
BANK = 512
NEG = -1e30


EXPERTS, TOP = 8, 2
CAPACITY = -(-5 * B * S * TOP // (4 * EXPERTS))


class Links:

    def __init__(self, engine, sem, base=0):
        self.engine, self.sem, self.base, self.n = engine, sem, base, 0

    def after(self, instruction):
        instruction.then_inc(self.sem, 1)
        self.n += 1
        self.engine.wait_ge(self.sem, self.base + self.n)

    def mark(self, instruction):
        instruction.then_inc(self.sem, 1)
        self.n += 1
        return self.base + self.n

    def reached(self, mark):
        self.engine.wait_ge(self.sem, mark)


def wait(engine, sem, n):
    if not isinstance(n, int) or n > 0:
        engine.wait_ge(sem, n)


def rounds(engine, n, body):
    body(0, True, n == 1)
    if n > 2:
        with engine.Fori(1, n - 1) as i:
            body(i, False, False)
    if n > 1:
        body(n - 1, False, True)


class Core:

    def __init__(self, nc, stack):
        self.nc = nc
        self.stack = stack

        def sb(name, shape, dt=F32):
            return stack.enter_context(nc.sbuf_tensor(name, shape, dt))

        self.x = sb("x_tok", [P, TILES, D])
        self.xT = sb("x_chan", [P, KT, B * S])
        self.ctxT = sb("ctx_chan", [P, KT, B, CTX])
        self.ident = sb("ident", [P, P])
        self.ident_bf = sb("ident_bf", [P, P], BF16)
        self.ones_row = sb("ones_row", [1, P])
        self.stats = sb("ln_stats", [P, TILES, 6])
        self.mean_var = sb("ln_mean_var", [P, TILES, 2])
        self.var_eps = sb("ln_var_eps", [P, TILES])
        self.rstd = sb("ln_rstd", [P, TILES])
        self.minus_half = sb("minus_half", [P, TILES])
        self.zeros = sb("zeros", [P, D])
        rows = EXPERTS * CAPACITY
        self.by_expert = nc.dram_tensor("rows_by_expert", (rows + TOP * B * S, D), F32).ap()
        self.y_by_expert = nc.dram_tensor("results_by_expert", (rows, D), F32).ap()
        self.ln_sems = [self.sem("ln_" + n) for n in ("dve_steps", "var_ready", "rstd_ready", "x_ready", "xT_in_psum",
                                                      "xT_copied", "stored")]
        self.zeroed = self.sem("rows_zeroed")

    def sem(self, name):
        return self.stack.enter_context(self.nc.semaphore(name))


def constants_and_loads(core, d):
    nc = core.nc
    with ExitStack() as st:
        loaded = core.sem("inputs_loaded")
        made = core.sem("constants_made")
        block = st.enter_context(nc.Block())

        @block.sync
        def _(sp):
            sp.dma_start(core.xT[:, :, :], d["x_chan"].rearrange("(k p) n -> p k n", p=P)).then_inc(loaded, 16)
            sp.dma_start(core.ctxT[:, :, :, :].rearrange("p k b n -> p k (b n)"),
                         d["ctx_chan"].rearrange("(k p) n -> p k n", p=P)).then_inc(loaded, 16)
            sp.dma_start(core.x[:, :, :], d["x"].rearrange("b (t p) c -> p (b t) c", p=P)).then_inc(loaded, 16)
            sp.wait_ge(made, 4)
            rows = EXPERTS * CAPACITY
            sp.dma_start(core.by_expert[0:rows, :].rearrange("(t p) c -> p t c", p=P),
                         core.zeros[:, :].rearrange("p (o c) -> p o c", o=1).to_broadcast([P, rows // P, D])).then_inc(core.zeroed, 16)
            sp.wait_ge(loaded, 48)

        @block.gpsimd
        def _(pool):
            step = Links(pool, made)
            nc.gpsimd.memset(core.ones_row[:, :], 1.0)
            nc.gpsimd.memset(core.minus_half[:, :], -0.5)
            step.after(nc.gpsimd.memset(core.ident[:, :], 0.0))
            step.after(nc.gpsimd.affine_select(out=core.ident[:, :], in_=core.ident[:, :], compare_op=ALU.not_equal,
                                               fill=1.0, base=0, pattern=[[-1, P]], channel_multiplier=1))
            step.after(nc.gpsimd.tensor_copy(core.ident_bf[:, :], core.ident[:, :]))
            step.after(nc.gpsimd.memset(core.zeros[:, :], 0.0))


def layer_norm(core, nth, out=None):
    nc = core.nc
    RING = 4
    GROUP = 4
    COPIES = TILES // GROUP * KT
    s_dve, var_ready, rstd_ready, x_ready, xT_in_psum, xT_copied, stored = core.ln_sems
    with ExitStack() as st:
        ring = st.enter_context(nc.psum_tensor(f"ln{nth}_xT_psum", [P, RING, BANK], F32))
        block = st.enter_context(nc.Block())

        @block.vector
        def _(dve):
            step = Links(dve, s_dve, nth)
            for t in range(TILES):
                last = nc.vector.bn_aggr(core.mean_var[:, t, :], core.stats[:, t, :])
            step.after(last)
            nc.vector.tensor_scalar(core.var_eps[:, :], core.mean_var[:, :, 1], EPS, None, ALU.add).then_inc(var_ready, 1)
            dve.wait_ge(rstd_ready, nth + 1)
            for t in range(TILES):
                nc.vector.tensor_scalar(core.x[:, t, :], core.x[:, t, :], core.mean_var[:, t, 0:1],
                                        core.rstd[:, t:t + 1], ALU.subtract, ALU.mult).then_inc(x_ready, 1)

        @block.gpsimd
        def _(pool):
            pool.wait_ge(var_ready, nth + 1)
            nc.gpsimd.tensor_tensor(core.rstd[:, :], core.var_eps[:, :], core.minus_half[:, :], ALU.pow).then_inc(rstd_ready, 1)

        if out is not None:
            @block.sync
            def _(sp):
                o = out.rearrange("b (t p) c -> p (b t) c", p=P)
                for g in range(TILES // GROUP):
                    sp.wait_ge(x_ready, TILES * nth + GROUP * (g + 1))
                    sp.dma_start(o[:, GROUP * g:GROUP * (g + 1), :],
                                 core.x[:, GROUP * g:GROUP * (g + 1), :]).then_inc(stored, 16)
                sp.wait_ge(stored, 16 * (TILES // GROUP))
            return

        @block.tensor
        def _(pe):
            for g in range(TILES // GROUP):
                for k in range(KT):
                    n = g * KT + k
                    if n >= RING:
                        pe.wait_ge(xT_copied, COPIES * nth + n - RING + 1)
                    for i in range(GROUP):
                        pe.wait_ge(x_ready, TILES * nth + GROUP * g + i + 1)
                        last = nc.tensor.transpose(ring[:, n % RING, i * P:(i + 1) * P],
                                                   core.x[:, GROUP * g + i, k * P:(k + 1) * P], core.ident[:, :])
                    last.then_inc(xT_in_psum, 1)

        @block.scalar
        def _(act):
            for g in range(TILES // GROUP):
                for k in range(KT):
                    n = g * KT + k
                    act.wait_ge(xT_in_psum, COPIES * nth + n + 1)
                    nc.scalar.activation(core.xT[:, k, g * BANK:(g + 1) * BANK], ring[:, n % RING, :],
                                         ACT.Copy).then_inc(xT_copied, 1)


def latent_attention(core, d):
    nc = core.nc
    DH, RANK = 64, P
    PAIRS = HEADS * DH // P
    SCALE = DH ** -0.5
    Q_GROUPS = B * S // BANK
    GROUPS = 3 * Q_GROUPS
    UNITS = [(b, t, h) for b in range(B) for t in range(SEQ_TILES) for h in range(2)]
    NU = len(UNITS)
    CHUNK = BANK // P
    VW = 2 * DH + 2
    CHUNKS = [(u, c) for u, (b, t, h) in enumerate(UNITS) for c in range((t + CHUNK) // CHUNK)]
    NC = len(CHUNKS)
    RING = 2
    assert NC % RING == 0
    first_chunk = [min(i for i, (v, _) in enumerate(CHUNKS) if v == u) for u in range(NU)] + [NC]

    def blocks(u):
        return UNITS[u][1] + 1

    with ExitStack() as st:
        def sb(n, shape, dt=F32):
            return st.enter_context(nc.sbuf_tensor("mla_" + n, shape, dt))

        def sem(n):
            return core.sem("mla_" + n)

        w_down = sb("w_down", [P, KT, RANK])
        w_q = sb("w_q", [P, KT, P])
        w_k = sb("w_k", [P, P])
        w_v = sb("w_v", [P, P])
        latT = sb("latent_chan", [P, B * S])
        assert PAIRS * D == B * S
        w_out = latT[:, :].rearrange("p (k n) -> p k n", k=PAIRS)
        q_split = sb("q_split", [P, 2, B * S], F32R)
        k_high = sb("k_high", [P, 2, B * S], F32R)
        k_low = sb("k_low", [P, 2, B * S], F32R)
        v = sb("v_tok", [P, TILES, 2, VW], F32R)
        causal = sb("causal", [P, P], BF16)
        causal32 = sb("causal32", [P, P])
        p_tok = sb("exps_tok", [P, 2, S])
        pT_high = sb("exps_key_high", [P, 2, SEQ_TILES, P], F32R)
        pT_low = sb("exps_key_low", [P, 2, SEQ_TILES, P], F32R)
        y = sb("y_tok", [P, TILES, HEADS * DH])
        yT = p_tok[:, :, :].rearrange("p b (k q) -> p b k q", k=PAIRS)
        neg_max = sb("neg_max", [P, 4])
        inv_sum = sb("inv_sum", [P, 2])
        y_high = sb("y_high", [P, 2, DH])
        one_zero = sb("one_zero", [P, 2])
        scores = st.enter_context(nc.psum_tensor("mla_scores", [P, 4, BANK], F32))
        tpose = st.enter_context(nc.psum_tensor("mla_tpose", [P, RING, BANK], F32))
        outp = st.enter_context(nc.psum_tensor("mla_outp", [P, 2, BANK], F32))

        w_loaded, w_used, setup = sem("w_loaded"), sem("w_used"), sem("setup")
        wd_loaded, lat_done, lat_copied = sem("wd_loaded"), sem("lat_done"), sem("lat_copied")
        proj_done, proj_act, proj_dve = sem("proj_done"), sem("proj_by_act"), sem("proj_by_dve")
        qk_done, max_done, exp_done, t_done = sem("qk_done"), sem("max_done"), sem("exp_done"), sem("t_done")
        pT_high_done, pT_split, pv_done, y_done = sem("pT_high_done"), sem("pT_split"), sem("pv_done"), sem("y_done")
        s_dve = sem("dve_steps")
        yT_done, yT_copied, out_done, sum_done = sem("yT_done"), sem("yT_copied"), sem("out_done"), sem("sum_done")
        block = st.enter_context(nc.Block())

        @block.sync
        def _(sp):
            sp.dma_start(w_down[:, :, :], d["L0_attn_w_kv_down"].rearrange("(k p) n -> p k n", p=P)).then_inc(wd_loaded, 16)

            def weights(i, first, last):
                if not first:
                    sp.wait_ge(w_used, i)
                sp.dma_start(w_q[:, :, :], d["w_q_pairs"][i]).then_inc(w_loaded, 16)
                sp.dma_start(w_k[:, :], d["w_kv_up_pairs"][i]).then_inc(w_loaded, 16)
                sp.dma_start(w_v[:, :], d["w_kv_up_pairs"][i + PAIRS]).then_inc(w_loaded, 16)

            rounds(sp, PAIRS, weights)
            sp.wait_ge(w_used, PAIRS)
            sp.dma_start(w_out, d["L0_attn_w_out"].rearrange("(k p) n -> p k n", p=P)).then_inc(wd_loaded, 16)

        @block.gpsimd
        def _(pool):
            step = Links(pool, setup)
            step.after(nc.gpsimd.memset(one_zero[:, 0:1], 1.0))
            step.after(nc.gpsimd.memset(one_zero[:, 1:2], 0.0))
            step.after(nc.gpsimd.tensor_copy(v[:, :, :, DH:DH + 2].rearrange("p t h c -> p (t h) c"),
                                             one_zero[:, :].rearrange("p (o c) -> p o c", o=1).to_broadcast([P, 2 * TILES, 2])))
            step.after(nc.gpsimd.memset(k_low[DH:P, 0, :].bitcast(F32), 0.0))
            step.after(nc.gpsimd.memset(k_low[0:DH, 1, :].bitcast(F32), 0.0))
            step.after(nc.gpsimd.memset(causal32[:, :], 0.0))
            step.after(nc.gpsimd.affine_select(out=causal32[:, :], in_=causal32[:, :], compare_op=ALU.is_ge, fill=NEG,
                                               base=0, pattern=[[-1, P]], channel_multiplier=1))
            step.after(nc.gpsimd.tensor_copy(causal[:, :], causal32[:, :]))

        @block.tensor
        def _(pe):
            pe.wait_ge(wd_loaded, 16)
            for g in range(Q_GROUPS):
                for k in range(KT):
                    last = nc.tensor.matmul(scores[:, g, :], w_down[:, k, :], core.xT[:, k, g * BANK:(g + 1) * BANK],
                                            start=(k == 0), stop=(k == KT - 1))
                last.then_inc(lat_done, 1)
            pe.wait_ge(lat_copied, Q_GROUPS)
            pe.wait_ge(setup, 8)

            def pair(i, first, last):
                pe.wait_ge(w_loaded, 48 * i + 48)
                if not first:
                    pe.wait_ge(exp_done, NU * i)
                    pe.wait_ge(y_done, NU * i)
                for g in range(GROUPS):
                    if g >= 4:
                        pe.wait_ge(proj_dve, GROUPS * i + g - 3)
                    n = g % Q_GROUPS
                    if g < Q_GROUPS:
                        for k in range(KT):
                            last = nc.tensor.matmul(scores[:, g % 4, :], w_q[:, k, :],
                                                    core.xT[:, k, n * BANK:(n + 1) * BANK],
                                                    start=(k == 0), stop=(k == KT - 1))
                    elif g < 2 * Q_GROUPS:
                        last = nc.tensor.matmul(scores[:, g % 4, :], w_k[:, :], latT[:, n * BANK:(n + 1) * BANK],
                                                start=True, stop=True)
                    else:
                        for j in range(4):
                            last = nc.tensor.matmul(scores[:, g % 4, j * P:(j + 1) * P],
                                                    latT[:, (4 * n + j) * P:(4 * n + j + 1) * P], w_v[:, :],
                                                    start=True, stop=True)
                    last.then_inc(proj_done, 1)
                last_proj = nc.tensor.matmul(outp[:, 0, 0:P], core.ident_bf[:, :], causal[:, :], start=True, stop=True)
                last_proj.then_inc(w_used, 1)
                pe.wait_ge(proj_dve, GROUPS * i + GROUPS)

                def qk(u):
                    b, t, h = UNITS[u]
                    if u >= 2:
                        pe.wait_ge(exp_done, NU * i + u - 1)
                    width = (t + 1) * P
                    for c in range(0, width, BANK):
                        n = min(BANK, width - c)
                        bank = 2 * (u % 2) + c // BANK
                        diagonal = c + n == width
                        lhs = q_split[:, h, b * S + t * P:b * S + (t + 1) * P]
                        nc.tensor.matmul(scores[:, bank, 0:n], lhs, k_high[:, h, b * S + c:b * S + c + n], start=True, stop=False)
                        last = nc.tensor.matmul(scores[:, bank, 0:n], lhs, k_low[:, h, b * S + c:b * S + c + n],
                                                start=False, stop=not diagonal)
                        if diagonal:
                            last = nc.tensor.matmul(scores[:, bank, n - P:n], core.ident_bf[:, :], causal[:, :],
                                                    start=False, stop=True)
                    last.then_inc(qk_done, 1)

                def transposes(u):
                    pe.wait_ge(exp_done, NU * i + u + 1)
                    for c in range(first_chunk[u], first_chunk[u + 1]):
                        if c >= RING:
                            pe.wait_ge(pT_split, NC * i + c - RING + 1)
                        part = CHUNKS[c][1]
                        for j in range(min(CHUNK, blocks(u) - part * CHUNK)):
                            at = (part * CHUNK + j) * P
                            last = nc.tensor.transpose(tpose[:, c % RING, j * P:(j + 1) * P],
                                                       p_tok[:, u % 2, at:at + P], core.ident[:, :])
                        last.then_inc(t_done, 1)

                def pv(u):
                    b, t, h = UNITS[u]
                    pe.wait_ge(pT_split, NC * i + first_chunk[u + 1])
                    if u >= 2:
                        pe.wait_ge(y_done, NU * i + u - 1)
                    for j in range(blocks(u)):
                        for pT in pT_high, pT_low:
                            last = nc.tensor.matmul(outp[:, u % 2, 0:VW], pT[:, u % 2, j, :], v[:, b * SEQ_TILES + j, h, :],
                                                    start=(j == 0 and pT is pT_high),
                                                    stop=(j == blocks(u) - 1 and pT is pT_low))
                    last.then_inc(pv_done, 1)

                qk(0)
                qk(1)
                for u in range(NU):
                    if u + 2 < NU:
                        qk(u + 2)
                    if u >= 2:
                        pv(u - 2)
                    transposes(u)
                pv(NU - 2)
                pv(NU - 1)

            rounds(pe, PAIRS, pair)
            pe.wait_ge(wd_loaded, 32)
            pe.wait_ge(y_done, NU * PAIRS)

            def project(t):
                pe.wait_ge(yT_copied, 2 * t + 2)
                if t >= 2:
                    pe.wait_ge(sum_done, t - 1)
                for k in range(PAIRS):
                    last = nc.tensor.matmul(tpose[:, t % 2, 0:D], yT[:, t % 2, k, :], w_out[:, k, :],
                                            start=(k == 0), stop=(k == PAIRS - 1))
                last.then_inc(out_done, 1)

            for t in range(TILES):
                for half in range(2):
                    n = 2 * t + half
                    if n >= 4:
                        pe.wait_ge(yT_copied, n - 3)
                    for j in range(4):
                        k = 4 * half + j
                        last = nc.tensor.transpose(scores[:, n % 4, j * P:(j + 1) * P], y[:, t, k * P:(k + 1) * P],
                                                   core.ident[:, :])
                    last.then_inc(yT_done, 1)
                if t >= 1:
                    project(t - 1)
            project(TILES - 1)

        HEAD = [slice(0, DH), slice(DH, P)]

        @block.scalar
        def _(act):
            for g in range(Q_GROUPS):
                act.wait_ge(lat_done, g + 1)
                nc.scalar.activation(latT[:, g * BANK:(g + 1) * BANK], scores[:, g, :], ACT.Copy).then_inc(lat_copied, 1)
            act.wait_ge(setup, 8)

            def pair(i, first, last):
                for g in range(GROUPS):
                    act.wait_ge(proj_done, GROUPS * i + g + 1)
                    n = g % Q_GROUPS
                    cols = slice(n * BANK, (n + 1) * BANK)
                    src = scores[:, g % 4, :]
                    if g < 2 * Q_GROUPS:
                        dst = q_split if g < Q_GROUPS else k_high
                        if g >= Q_GROUPS:
                            nc.scalar.copy(k_high[HEAD[1], 0, cols], src[HEAD[0], :])
                        for h in range(2):
                            done = nc.scalar.activation(dst[HEAD[h], h, cols], src[HEAD[h], :], ACT.Copy,
                                                        scale=SCALE if g < Q_GROUPS else 1.0)
                    else:
                        done = nc.scalar.activation(v[:, 4 * n:4 * n + 4, :, 0:DH],
                                                    src.rearrange("p (t h e) -> p t h e", t=4, h=2), ACT.Copy)
                    done.then_inc(proj_act, 1)

                def copies(u):
                    for c in range(first_chunk[u], first_chunk[u + 1]):
                        act.wait_ge(t_done, NC * i + c + 1)
                        if u >= 2:
                            act.wait_ge(pv_done, NU * i + u - 1)
                        part = CHUNKS[c][1]
                        n = min(CHUNK, blocks(u) - part * CHUNK)
                        nc.scalar.copy(pT_high[:, u % 2, part * CHUNK:part * CHUNK + n, :].rearrange("p j q -> p (j q)"),
                                       tpose[:, c % RING, 0:n * P]).then_inc(pT_high_done, 1)

                for u in range(NU):
                    act.wait_ge(max_done, NU * i + u + 1)
                    if u >= 2:
                        act.wait_ge(t_done, NC * i + first_chunk[u - 1])
                    nc.scalar.activation(p_tok[:, u % 2, 0:blocks(u) * P],
                                         scores[:, 2 * (u % 2):2 * (u % 2) + 2, :].rearrange("p c n -> p (c n)")[:, 0:blocks(u) * P],
                                         ACT.Exp, bias=neg_max[:, u % 4:u % 4 + 1]).then_inc(exp_done, 1)
                    if u >= 1:
                        copies(u - 1)
                copies(NU - 1)

            rounds(act, PAIRS, pair)
            for n in range(2 * TILES):
                t, half = n // 2, n % 2
                act.wait_ge(yT_done, n + 1)
                if t >= 2:
                    act.wait_ge(out_done, t - 1)
                nc.scalar.activation(yT[:, t % 2, 4 * half:4 * half + 4, :].rearrange("p k q -> p (k q)"),
                                     scores[:, n % 4, :], ACT.Copy).then_inc(yT_copied, 1)

        @block.vector
        def _(dve):

            def pair(i, first, last):
                step = Links(dve, s_dve, i * (2 * NU))
                for g in range(GROUPS):
                    dve.wait_ge(proj_act, GROUPS * i + g + 1)
                    n = g % Q_GROUPS
                    cols = slice(n * BANK, (n + 1) * BANK)
                    src = scores[:, g % 4, :]
                    if g < 2 * Q_GROUPS:
                        high, low = (q_split, q_split) if g < Q_GROUPS else (k_high, k_low)
                        if g >= Q_GROUPS:
                            nc.vector.tensor_copy(k_high[HEAD[0], 1, cols], src[HEAD[1], :])
                        for h in range(2):
                            rows = HEAD[1 - h] if g < Q_GROUPS else HEAD[h]
                            done = nc.vector.scalar_tensor_tensor(low[rows, h, cols], src[HEAD[h], :],
                                                                  SCALE if g < Q_GROUPS else 1.0,
                                                                  high[HEAD[h], h, cols].bitcast(F32), ALU.mult, ALU.subtract)
                    else:
                        done = nc.vector.tensor_tensor(v[:, 4 * n:4 * n + 4, :, DH + 2:VW],
                                                       src.rearrange("p (t h e) -> p t h e", t=4, h=2),
                                                       v[:, 4 * n:4 * n + 4, :, 0:DH].bitcast(F32), ALU.subtract)
                    done.then_inc(proj_dve, 1)

                def low_parts(c):
                    dve.wait_ge(pT_high_done, NC * i + c + 1)
                    u, part = CHUNKS[c]
                    n = min(CHUNK, blocks(u) - part * CHUNK)
                    here = (slice(None), u % 2, slice(part * CHUNK, part * CHUNK + n), slice(None))
                    nc.vector.tensor_tensor(pT_low[here].rearrange("p j q -> p (j q)"), tpose[:, c % RING, 0:n * P],
                                            pT_high[here].rearrange("p j q -> p (j q)").bitcast(F32),
                                            ALU.subtract).then_inc(pT_split, 1)

                def maximum(u):
                    dve.wait_ge(qk_done, NU * i + u + 1)
                    if u >= 4:
                        dve.wait_ge(exp_done, NU * i + u - 3)
                    nc.vector.tensor_reduce(
                        neg_max[:, u % 4:u % 4 + 1],
                        scores[:, 2 * (u % 2):2 * (u % 2) + 2, :].rearrange("p c n -> p (c n)")[:, 0:blocks(u) * P],
                        AX, ALU.max, negate=True).then_inc(max_done, 1)

                marks = {}

                def inverse(u):
                    dve.wait_ge(pv_done, NU * i + u + 1)
                    marks[u] = step.mark(nc.vector.reciprocal(inv_sum[:, u % 2:u % 2 + 1], outp[:, u % 2, DH:DH + 1]))

                def normalise_high(u):
                    step.reached(marks[u])
                    marks[u] = step.mark(nc.vector.tensor_scalar(y_high[:, u % 2, :], outp[:, u % 2, 0:DH],
                                                                 inv_sum[:, u % 2:u % 2 + 1], None, ALU.mult))

                def normalise_low(u):
                    b, t, h = UNITS[u]
                    step.reached(marks[u])
                    nc.vector.scalar_tensor_tensor(y[:, b * SEQ_TILES + t, bass.ds(i * P + h * DH, DH)],
                                                   outp[:, u % 2, DH + 2:VW], inv_sum[:, u % 2:u % 2 + 1],
                                                   y_high[:, u % 2, :], ALU.mult, ALU.add).then_inc(y_done, 1)

                for u in range(NU + 4):
                    if u >= 4:
                        inverse(u - 4)
                    if u < NU:
                        maximum(u)
                    if u >= 4:
                        normalise_high(u - 4)
                    if 2 <= u < NU + 2:
                        for c in range(first_chunk[u - 2], first_chunk[u - 1]):
                            low_parts(c)
                    if u >= 4:
                        normalise_low(u - 4)

            rounds(dve, PAIRS, pair)
            for t in range(TILES):
                dve.wait_ge(out_done, t + 1)
                nc.vector.tensor_tensor(core.x[:, t, :], tpose[:, t % 2, 0:D], core.x[:, t, :], ALU.add).then_inc(sum_done, 1)
                dve.wait_ge(sum_done, t + 1)
                nc.vector.bn_stats(core.stats[:, t, :], core.x[:, t, :])


def cross_attention(core, d, name, block_diagonal, mask_value):
    nc = core.nc
    DH = D // HEADS
    HH = HEADS // 2
    HB = 3
    SB = 3
    REST = CTX - P
    RH = 4
    VW = HH * (DH + 1)
    SCALE = DH ** -0.5
    UNITS = [(b, half) for b in range(B) for half in range(2)]
    NU = len(UNITS)
    CHUNK = BANK // P
    BLOCKS = [(h, None) for h in range(HH)] + [(None, r) for r in range(HH // RH)]
    NCH = -(-len(BLOCKS) // CHUNK)

    def by_dve(c):
        return c == 1

    ACT_CHUNKS = NCH - 1

    with ExitStack() as st:
        def sb(n, shape, dt=F32):
            return st.enter_context(nc.sbuf_tensor(f"{name}_{n}", shape, dt))

        def ps(n, shape):
            return st.enter_context(nc.psum_tensor(f"{name}_{n}", shape, F32))

        def sem(n):
            return core.sem(f"{name}_{n}")

        w = {n: sb("w" + n, [P, KT, D]) for n in "qkvo"}
        bias_col = sb("bias_col", [P, 2, KT])
        bias_row = sb("bias_row", [1, D])
        mask_raw = sb("mask_raw", [P, TILES, CTX], U8 if mask_value[0] == "hidden" else I32)
        mask = sb("mask", [P, TILES, CTX], BF16)
        head_of = sb("head_of", [P, HH])
        k_heads = sb("k_heads", [P, B, KT, HH, CTX])
        v = sb("v_tok", [P, B, 2, HH * (VW + DH + 1)])
        v_rest = sb("v_rest", [RH * REST, B, 2, HH // RH, VW])
        row_of = sb("row_of", [RH * REST, RH])
        bias_out = sb("bias_out", [P, D])
        kT = sb("k_chan", [P, KT, B * CTX])
        qT = sb("q_chan", [P, B, KT, P])
        s_max = sb("s_max", [P, HB * SB])
        SLOTS = HB * SB
        p_tok = sb("exps_tok", [P, 2, SLOTS * CTX])
        ctx_rest = sb("ctx_rest", [P, KT, B, RH * REST])
        pT = sb("exps_key", [P, 2, len(BLOCKS), P])
        inv_sum = sb("inv_sum", [P, HEADS])
        y = sb("y_tok", [P, D])
        yT = sb("y_chan", [P, KT, P])
        scores = ps("scores", [P, SB, BANK])
        tpose = ps("tpose", [P, 2, BANK])
        outp = ps("outp", [P, 2, HH, DH + 1])
        q_ps = ps("q_psum", [P, KT, P])
        fin = ps("fin", [P, 2, D])

        w_loaded, mask_loaded, setup = sem("w_loaded"), sem("mask_loaded"), sem("setup")
        wz = sem("w_zero")
        kv_done, kv_copied, kv_heads = sem("kv_done"), sem("kv_copied"), sem("kv_heads")
        q_done, q_copied, qk_done, sub_done, exp_done = sem("q_done"), sem("q_copied"), sem("qk_done"), sem("sub_done"), sem("exp_done")
        t_done, copied_act, copied_dve, pv_done = sem("t_done"), sem("pT_by_act"), sem("pT_by_dve"), sem("pv_done")
        y_done, yT_done, yT_copied, out_done, sum_done, s_dve = (sem("y_done"), sem("yT_done"), sem("yT_copied"),
                                                                 sem("out_done"), sem("sum_done"), sem("dve_steps"))
        mask_ready, bias_added, v_ready = sem("mask_ready"), sem("bias_added"), sem("v_ready")
        block = st.enter_context(nc.Block())
        WD = len(w) if not block_diagonal else 1 + 3 * D // DH

        def copy_chunk(copy, u, c):
            first = c * CHUNK
            n = min(CHUNK, len(BLOCKS) - first)
            rows = P if first < HH else RH * REST
            return copy(pT[0:rows, u % 2, first:first + n, :].rearrange("p j q -> p (j q)"), tpose[0:rows, (NCH * u + c) % 2, 0:n * P])

        SETUP = 3 + 3 + 3

        @block.sync
        def _(sp):
            sp.dma_start(mask_raw[:, :, :], d[name + "_mask"].rearrange("b (t p) c -> p (b t) c", p=P)).then_inc(mask_loaded, 16)
            if block_diagonal:
                sp.wait_ge(wz, 3)
                for n in "kqv":
                    for h in range(HEADS):
                        r = h * DH % P
                        sp.dma_start(w[n][r:r + DH, h * DH // P, h * DH:(h + 1) * DH], d[f"{name}_W{n}"]).then_inc(w_loaded, 16)
                sp.dma_start(w["o"][:, :, :], d[name + "_Wo"].rearrange("(k p) n -> p k n", p=P)).then_inc(w_loaded, 16)
            else:
                for n in "kqvo":
                    sp.dma_start(w[n][:, :, :], d[f"{name}_W{n}"].rearrange("(k p) n -> p k n", p=P)).then_inc(w_loaded, 16)
                for j, n in enumerate("qk"):
                    sp.dma_start(bias_col[:, j, :], d[f"{name}_b{n}"].rearrange("(k p) -> p k", p=P),
                                 allow_slow_non_contiguous=True).then_inc(w_loaded, 16)
                sp.dma_start(bias_row[0:1, :], d[name + "_bv"].rearrange("(o n) -> o n", o=1)).then_inc(w_loaded, 16)
            sp.dma_start(bias_out[:, :], d[name + "_bo"].rearrange("(o n) -> o n", o=1).to_broadcast([P, D])).then_inc(w_loaded, 16)
        LOADS = 16 * (WD + 1 + (0 if block_diagonal else 3))

        @block.gpsimd
        def _(pool):
            if block_diagonal:
                for n in "kqv":
                    nc.gpsimd.memset(w[n][:, :, :], 0.0).then_inc(wz, 1)
            step = Links(pool, setup)
            step.after(nc.gpsimd.memset(head_of[:, :], 1.0))
            step.after(nc.gpsimd.affine_select(out=head_of[:, :], in_=head_of[:, :], compare_op=ALU.is_ge, fill=0.0,
                                               base=0, pattern=[[-DH, HH]], channel_multiplier=1))
            step.after(nc.gpsimd.affine_select(out=head_of[:, :], in_=head_of[:, :], compare_op=ALU.is_ge, fill=0.0,
                                               base=DH - 1, pattern=[[DH, HH]], channel_multiplier=-1))
            step.after(nc.gpsimd.memset(row_of[:, :], 1.0))
            step.after(nc.gpsimd.affine_select(out=row_of[:, :], in_=row_of[:, :], compare_op=ALU.is_ge, fill=0.0,
                                               base=0, pattern=[[-REST, RH]], channel_multiplier=1))
            step.after(nc.gpsimd.affine_select(out=row_of[:, :], in_=row_of[:, :], compare_op=ALU.is_ge, fill=0.0,
                                               base=REST - 1, pattern=[[REST, RH]], channel_multiplier=-1))
            step.after(nc.gpsimd.memset(v[:, :, :, :], 0.0))
            step.after(nc.gpsimd.memset(v_rest[:, :, :, :, :], 0.0))
            for b in range(B):
                for k in range(KT):
                    nc.gpsimd.tensor_copy(ctx_rest[:, k, b, :].rearrange("p (h n) -> p h n", h=RH),
                                          core.ctxT[:, k, b:b + 1, P:CTX].to_broadcast([P, RH, REST]))
            own = v[:, :, :, :].rearrange("p b f (h c) -> p b f h c", c=VW + DH + 1)
            for b in range(B):
                for half in range(2):
                    last = nc.gpsimd.memset(own[:, b, half, :, DH:DH + 1], 1.0)
                    for r in range(HH // RH):
                        first = r * RH * (DH + 1)
                        ones = v_rest[:, b, half, r, first:first + RH * (DH + 1)].rearrange("p (h c) -> p h c", c=DH + 1)
                        last = nc.gpsimd.tensor_copy(ones[:, :, DH], row_of[:, :])
            step.after(last)
            pool.wait_ge(w_loaded, LOADS)
            nc.gpsimd.tensor_tensor(core.x[:, :, :], core.x[:, :, :],
                                    bias_out[:, :].rearrange("p (o c) -> p o c", o=1).to_broadcast([P, TILES, D]),
                                    ALU.add).then_inc(bias_added, 1)

        @block.tensor
        def _(pe):
            pe.wait_ge(w_loaded, LOADS)
            pe.wait_ge(setup, SETUP)
            for m in range(KT):
                parts = [m] if block_diagonal else list(range(KT))
                for k in parts:
                    last = nc.tensor.matmul(scores[:, m, 0:B * CTX], w["k"][:, k, m * P:(m + 1) * P],
                                            core.ctxT[:, k, :, :].rearrange("p b n -> p (b n)"),
                                            start=(k == parts[0]), stop=(k == parts[-1]))
                last.then_inc(kv_done, 1)
            for b in range(B):
                for rest in range(2):
                    n = 2 * b + rest
                    rows = RH * REST if rest else P
                    dst = tpose[0:rows, n % 2, 0:D]
                    if n >= 2:
                        pe.wait_ge(v_ready, n - 1)
                    for k in range(KT):
                        src = ctx_rest[:, k, b, :] if rest else core.ctxT[:, k, b, 0:P]
                        last = nc.tensor.matmul(dst, src, w["v"][:, k, :],
                                                start=(k == 0), stop=(block_diagonal and k == KT - 1))
                    if not block_diagonal:
                        last = nc.tensor.matmul(dst, core.ones_row[0:1, 0:rows], bias_row[0:1, :], start=False, stop=True)
                    last.then_inc(kv_done, 1)
            pe.wait_ge(kv_heads, B * KT)
            pe.wait_ge(v_ready, 2 * B)
            pe.wait_ge(mask_ready, 1)

            def queries(i, b):
                wait(pe, q_copied, KT * (i * B + b))
                for m in range(KT):
                    parts = [m] if block_diagonal else list(range(KT))
                    for k in parts:
                        last = nc.tensor.matmul(q_ps[:, m, :], w["q"][:, k, m * P:(m + 1) * P],
                                                core.xT[:, k, bass.ds(i * P + b * S, P)],
                                                start=(k == parts[0]), stop=(k == parts[-1]))
                last.then_inc(q_done, 1)

            def qk(i, u):
                b, half = UNITS[u]
                if half == 0:
                    queries(i, b)
                    wait(pe, q_copied, KT * (i * B + b + 1))
                wait(pe, sub_done, i * NU + u)
                for c in range(SB):
                    heads = range(c * HB, min(HH, (c + 1) * HB))
                    n = len(heads) * CTX
                    nc.tensor.matmul(scores[:, c, 0:HB * CTX].rearrange("p (h n) -> p h n", h=HB), core.ident_bf[:, :],
                                     mask[:, bass.ds(i + b * SEQ_TILES, 1), :].to_broadcast([P, HB, CTX]),
                                     start=True, stop=False)
                    last = nc.tensor.matmul(scores[:, c, 0:n], qT[:, b, half, :],
                                            k_heads[:, b, half, c * HB:c * HB + len(heads), :].rearrange("p h n -> p (h n)"),
                                            start=False, stop=True)
                last.then_inc(qk_done, 1)

            def transposes(i, u):
                wait(pe, exp_done, i * NU + u + 1)
                for c in range(NCH):
                    ring = (NCH * u + c) % 2
                    if c >= 2:
                        wait(pe, copied_act, (i * NU + u) * ACT_CHUNKS + 1)
                    elif c == 0:
                        wait(pe, copied_act, (i * NU + u) * ACT_CHUNKS)
                        wait(pe, copied_dve, i * NU + u)
                    for j, (h, r) in enumerate(BLOCKS[c * CHUNK:(c + 1) * CHUNK]):
                        rows = P if r is None else RH * REST
                        first = SLOTS * REST + h * P if r is None else r * RH * REST
                        src = p_tok[:, u % 2, first:first + rows]
                        last = nc.tensor.transpose(tpose[0:rows, ring, j * P:(j + 1) * P], src, core.ident[:, :])
                    last.then_inc(t_done, 1)

            def pv(i, u):
                b, half = UNITS[u]
                wait(pe, copied_act, (i * NU + u + 1) * ACT_CHUNKS)
                wait(pe, copied_dve, i * NU + u + 1)
                if half == 0:
                    wait(pe, y_done, i * B + b)
                for n, (h, r) in enumerate(BLOCKS):
                    rows = P if r is None else RH * REST
                    value = v[:, b, half, h * VW:(h + 1) * VW] if r is None else v_rest[:, b, half, r, :]
                    last = nc.tensor.matmul(outp[:, half, :, :].rearrange("p h c -> p (h c)"), pT[0:rows, u % 2, n, :],
                                            value, start=(n == 0), stop=(n == len(BLOCKS) - 1))
                last.then_inc(pv_done, 1)

            def project(i, b):
                wait(pe, y_done, i * B + b + 1)
                for k in range(KT):
                    last = nc.tensor.transpose(fin[:, 0, k * P:(k + 1) * P], y[:, k * P:(k + 1) * P], core.ident[:, :])
                last.then_inc(yT_done, 1)
                wait(pe, yT_copied, i * B + b + 1)
                wait(pe, sum_done, i * B + b)
                for k in range(KT):
                    last = nc.tensor.matmul(fin[:, 1, :], yT[:, k, :], w["o"][:, k, :], start=(k == 0), stop=(k == KT - 1))
                last.then_inc(out_done, 1)

            def one_round(i, first, last):
                if first:
                    qk(i, 0)
                for u in range(NU):
                    if u + 1 < NU:
                        qk(i, u + 1)
                    elif not last:
                        qk(i + 1, 0)
                    transposes(i, u)
                    if u > 0:
                        pv(i, u - 1)
                    elif not first:
                        pv(i - 1, NU - 1)
                    if u == 3:
                        project(i, 0)
                    if u == 1 and not first:
                        project(i - 1, 1)
                if last:
                    pv(i, NU - 1)
                    project(i, 1)

            rounds(pe, SEQ_TILES, one_round)

        @block.scalar
        def _(act):
            for m in range(KT):
                act.wait_ge(kv_done, m + 1)
                if block_diagonal:
                    nc.scalar.activation(kT[:, m, :], scores[:, m, 0:B * CTX], ACT.Copy).then_inc(kv_copied, 1)
                else:
                    nc.scalar.activation(kT[:, m, :], scores[:, m, 0:B * CTX], ACT.Identity,
                                         bias=bias_col[:, 1, m:m + 1]).then_inc(kv_copied, 1)
            act.wait_ge(setup, SETUP)
            for b in range(B):
                act.wait_ge(kv_done, KT + 2 * b + 1)
                for half in range(2):
                    own = v[:, b, half, :].rearrange("p (h c) -> p h c", c=VW + DH + 1)
                    last = nc.scalar.activation(own[:, :, 0:DH], tpose[:, 0, half * P:(half + 1) * P].rearrange("p (h e) -> p h e", h=HH),
                                                ACT.Copy)
                last.then_inc(v_ready, 1)
                act.wait_ge(v_ready, 2 * b + 2)

            def queries(i, b):
                act.wait_ge(q_done, i * B + b + 1)
                wait(act, qk_done, (i - 1) * NU + 2 * b + 2)
                for m in range(KT):
                    if block_diagonal:
                        nc.scalar.activation(qT[:, b, m, :], q_ps[:, m, :], ACT.Copy).then_inc(q_copied, 1)
                    else:
                        nc.scalar.activation(qT[:, b, m, :], q_ps[:, m, :], ACT.Identity,
                                             bias=bias_col[:, 0, m:m + 1]).then_inc(q_copied, 1)

            def exps(i, u):
                act.wait_ge(sub_done, i * NU + u + 1)
                e = p_tok[:, u % 2, 0:SLOTS * REST + HH * P]
                nc.scalar.activation(e, e, ACT.Exp, scale=SCALE).then_inc(exp_done, 1)

            def copies(i, u):
                for c in range(NCH):
                    if by_dve(c):
                        continue
                    act.wait_ge(t_done, (i * NU + u) * NCH + c + 1)
                    wait(act, pv_done, i * NU + u - 1)
                    copy_chunk(nc.scalar.copy, u, c).then_inc(copied_act, 1)

            def yT_copy(i, b):
                act.wait_ge(yT_done, i * B + b + 1)
                wait(act, out_done, i * B + b)
                nc.scalar.activation(yT[:, :, :].rearrange("p k q -> p (k q)"), fin[:, 0, :], ACT.Copy).then_inc(yT_copied, 1)

            def one_round(i, first, last):
                if first:
                    queries(i, 0)
                for u in range(NU):
                    if u == 1:
                        queries(i, 1)
                    if u == 3 and not last:
                        queries(i + 1, 0)
                    exps(i, u)
                    copies(i, u)
                    if u == 3:
                        yT_copy(i, 0)
                    if u == 1 and not first:
                        yT_copy(i - 1, 1)
                if last:
                    yT_copy(i, 1)

            rounds(act, SEQ_TILES, one_round)

        @block.vector
        def _(dve):
            dve.wait_ge(mask_loaded, 16)
            nc.vector.tensor_scalar(mask[:, :, :], mask_raw[:, :, :], 0.0, mask_value[1],
                                    ALU.not_equal if mask_value[0] == "hidden" else ALU.is_equal, ALU.mult).then_inc(mask_ready, 1)
            dve.wait_ge(setup, SETUP)
            dve.wait_ge(kv_copied, KT)
            for b in range(B):
                for m in range(KT):
                    nc.vector.tensor_tensor(k_heads[:, b, m, :, :],
                                            kT[:, m, b * CTX:(b + 1) * CTX].rearrange("p (o n) -> p o n", o=1).to_broadcast([P, HH, CTX]),
                                            head_of[:, :].rearrange("p (h o) -> p h o", o=1).to_broadcast([P, HH, CTX]),
                                            ALU.mult).then_inc(kv_heads, 1)
            for b in range(B):
                dve.wait_ge(kv_done, KT + 2 * b + 2)
                dve.wait_ge(v_ready, 2 * b + 1)
                for half in range(2):
                    for r in range(HH // RH):
                        first = r * RH * (DH + 1)
                        nh = half * HH + r * RH
                        last = nc.vector.tensor_tensor(
                            v_rest[:, b, half, r, first:first + RH * (DH + 1)].rearrange("p (h c) -> p h c", c=DH + 1)[:, :, 0:DH],
                            tpose[0:RH * REST, 1, nh * DH:(nh + RH) * DH].rearrange("p (h e) -> p h e", h=RH),
                            row_of[:, :].rearrange("p (h o) -> p h o", o=1).to_broadcast([RH * REST, RH, DH]), ALU.mult)
                last.then_inc(v_ready, 1)
            dve.wait_ge(bias_added, 1)
            sc = scores[:, :, 0:HB * CTX].rearrange("p c (h n) -> p c h n", h=HB)
            by_head = outp[:, :, :, :].rearrange("p f h c -> p (f h) c")

            def shift(i, u, step):
                dve.wait_ge(qk_done, i * NU + u + 1)
                step.after(nc.vector.tensor_reduce(s_max[:, :].rearrange("p (c h) -> p c h", c=SB), sc, AX, ALU.max))
                wait(dve, t_done, (i * NU + u - 1) * NCH)
                for lo, hi, dst in ((P, CTX, p_tok[:, u % 2, 0:SLOTS * REST]), (0, P, p_tok[:, u % 2, SLOTS * REST:])):
                    last = nc.vector.tensor_tensor(
                        dst.rearrange("p (c h n) -> p c h n", c=SB, h=HB), sc[:, :, :, lo:hi],
                        s_max[:, :].rearrange("p (c h o) -> p c h o", c=SB, o=1).to_broadcast([P, SB, HB, hi - lo]),
                        ALU.subtract)
                last.then_inc(sub_done, 1)

            def copies(i, u):
                for c in range(NCH):
                    if by_dve(c):
                        dve.wait_ge(t_done, (i * NU + u) * NCH + c + 1)
                        wait(dve, pv_done, i * NU + u - 1)
                        copy_chunk(nc.vector.tensor_copy, u, c).then_inc(copied_dve, 1)

            def normalise(i, b, step):
                dve.wait_ge(pv_done, i * NU + 2 * b + 2)
                step.after(nc.vector.reciprocal(inv_sum[:, :], by_head[:, :, DH]))
                wait(dve, yT_done, i * B + b)
                nc.vector.tensor_tensor(y[:, :].rearrange("p (h e) -> p h e", h=HEADS), by_head[:, :, 0:DH],
                                        inv_sum[:, :].rearrange("p (h o) -> p h o", o=1).to_broadcast([P, HEADS, DH]),
                                        ALU.mult).then_inc(y_done, 1)

            def add(i, b):
                dve.wait_ge(out_done, i * B + b + 1)
                tile = bass.ds(i + b * SEQ_TILES, 1)
                xt = core.x[:, tile, :].rearrange("p o c -> p (o c)")
                nc.vector.tensor_tensor(xt, fin[:, 1, :], xt, ALU.add).then_inc(sum_done, 1)
                dve.wait_ge(sum_done, i * B + b + 1)
                nc.vector.bn_stats(core.stats[:, tile, :].rearrange("p o c -> p (o c)"), xt)

            def one_round(i, first, last):
                step = Links(dve, s_dve, 0 if first else i * (NU + B) - 1)
                for u in range(NU):
                    shift(i, u, step)
                    if u > 0:
                        copies(i, u - 1)
                    elif not first:
                        copies(i - 1, NU - 1)
                    if u == 3:
                        normalise(i, 0, step)
                    if u == 1 and not first:
                        normalise(i - 1, 1, step)
                    if u == 0 and not first:
                        add(i - 1, 0)
                    if u == 2 and not first:
                        add(i - 1, 1)
                if last:
                    copies(i, NU - 1)
                    add(i, 0)
                    normalise(i, 1, step)
                    add(i, 1)

            rounds(dve, SEQ_TILES, one_round)


def cross_attention_0(core, d):
    cross_attention(core, d, "x0", False, ("hidden", -1e18))


def cross_attention_1(core, d):
    cross_attention(core, d, "x1", True, ("seen", -1e20))


def lora_ffn(core, d):
    nc = core.nc
    H = 4 * D
    FT = H // P
    LORA, FIRST = 16, 1
    NP = LORA // 4
    BLOCKS = S // BANK
    BT = BANK // P
    W1_SETS = KT * H // BANK
    W2_SETS = FT // 2
    SETS = W1_SETS + W2_SETS
    RING = 4

    with ExitStack() as st:
        def sb(n, shape, dt=F32):
            return st.enter_context(nc.sbuf_tensor("ffn_" + n, shape, dt))

        def sem(n):
            return core.sem("ffn_" + n)

        w1T = sb("w1T", [P, KT, H])
        w2T = sb("w2T", [P, FT, D])
        w1 = sb("w1_seq", [P, B, KT, H])
        w2 = sb("w2_seq", [P, B, FT, D])
        b1 = sb("b1", [P, FT])
        b2 = sb("b2", [1, D])
        scale = sb("scale", [1, 1])
        tok = sb("lora_tok", [1, B, LORA, D])
        tok_scaled = sb("lora_scaled", [1, B, LORA, D])
        hidden = sb("hidden", [P, B, FT, BANK])
        ring = st.enter_context(nc.psum_tensor("ffn_ring", [P, RING, BANK], F32))
        outp = st.enter_context(nc.psum_tensor("ffn_out", [P, 2, BANK], F32))
        w_loaded, tok_loaded, tok_ready = sem("w_loaded"), sem("tok_loaded"), sem("tok_ready")
        outer_done, w_ready = sem("outer_done"), sem("w_ready")
        up_done, gelu_done, out_done, sum_done = sem("up_done"), sem("gelu_done"), sem("out_done"), sem("sum_done")
        block = st.enter_context(nc.Block())

        @block.sync
        def _(sp):
            for b in range(B):
                sp.dma_start(tok[0:1, b, :, :], core.x[FIRST:FIRST + LORA, b * SEQ_TILES, :]).then_inc(tok_loaded, 16)
            sp.dma_start(scale[:, :], d["L0_ffn_scale"]).then_inc(tok_loaded, 16)
            sp.dma_start(w1T[:, :, :], d["w1T"].rearrange("(k p) n -> p k n", p=P)).then_inc(w_loaded, 16)
            sp.dma_start(w2T[:, :, :], d["w2T"].rearrange("(k p) n -> p k n", p=P)).then_inc(w_loaded, 16)
            sp.dma_start(b1[:, :], d["L0_ffn_b1_cols"]).then_inc(w_loaded, 16)
            sp.dma_start(b2[:, :], d["L0_ffn_b2"].rearrange("(o n) -> o n", o=1)).then_inc(w_loaded, 16)

        @block.tensor
        def _(pe):
            pe.wait_ge(tok_ready, 1)
            for b in range(B):
                for n in range(SETS):
                    g = b * SETS + n
                    if g >= RING:
                        pe.wait_ge(w_ready, g - RING + 1)
                    if n < W1_SETS:
                        k, part = n // 2, n % 2
                        for i in range(2 * part, 2 * part + 2):
                            last = nc.tensor.matmul(ring[:, g % RING, (i % 2) * D:(i % 2 + 1) * D],
                                                    tok[0:1, b, 2 * i + 1, k * P:(k + 1) * P], tok_scaled[0:1, b, 2 * i, :],
                                                    start=True, stop=True)
                    else:
                        j = n - W1_SETS
                        for half in range(2):
                            for i in range(NP):
                                last = nc.tensor.matmul(
                                    ring[:, g % RING, half * D + i * (D // NP):half * D + (i + 1) * (D // NP)],
                                    tok[0:1, b, LORA // 2 + 2 * i + 1, half * P:(half + 1) * P],
                                    tok_scaled[0:1, b, LORA // 2 + 2 * i, :].rearrange("p (o j) -> p j o", j=4)[:, j, :],
                                    start=True, stop=True)
                    last.then_inc(outer_done, 1)
            pe.wait_ge(w_ready, B * SETS)

            def one_round(i, first, last):
                for b in range(B):
                    for f in range(FT):
                        n = b * FT + f
                        if n >= RING:
                            wait(pe, gelu_done, i * (B * FT) + n - RING + 1)
                        else:
                            wait(pe, gelu_done, i * (B * FT))
                        for k in range(KT):
                            last = nc.tensor.matmul(ring[:, n % RING, :], w1[:, b, k, f * P:(f + 1) * P],
                                                    core.xT[:, k, bass.ds(i * BANK + b * S, BANK)],
                                                    start=(k == 0), stop=(k == KT - 1))
                        last.then_inc(up_done, 1)
                for b in range(B):
                    wait(pe, gelu_done, i * (B * FT) + (b + 1) * FT)
                    for t in range(BT):
                        n = b * BT + t
                        if n >= 2:
                            wait(pe, sum_done, i * (B * BT) + n - 1)
                        else:
                            wait(pe, sum_done, i * (B * BT))
                        for f in range(FT):
                            nc.tensor.matmul(outp[:, n % 2, 0:D], hidden[:, b, f, t * P:(t + 1) * P], w2[:, b, f, :],
                                             start=(f == 0), stop=False)
                        nc.tensor.matmul(outp[:, n % 2, 0:D], core.ones_row[0:1, :], b2[0:1, :],
                                         start=False, stop=True).then_inc(out_done, 1)

            rounds(pe, BLOCKS, one_round)

        @block.scalar
        def _(act):
            act.wait_ge(w_loaded, 64)

            def one_round(i, first, last):
                for b in range(B):
                    wait(act, out_done, i * (B * BT))
                    for f in range(FT):
                        n = b * FT + f
                        wait(act, up_done, i * (B * FT) + n + 1)
                        nc.scalar.activation(hidden[:, b, f, :], ring[:, n % RING, :], ACT.Gelu,
                                             bias=b1[:, f:f + 1]).then_inc(gelu_done, 1)

            rounds(act, BLOCKS, one_round)

        @block.vector
        def _(dve):
            dve.wait_ge(tok_loaded, 16 * (B + 1))
            nc.vector.tensor_scalar(tok_scaled[:, :, :, :], tok[:, :, :, :], scale[0:1, 0:1], None, ALU.mult).then_inc(tok_ready, 1)
            dve.wait_ge(w_loaded, 64)
            for b in range(B):
                for n in range(SETS):
                    g = b * SETS + n
                    dve.wait_ge(outer_done, g + 1)
                    if n < W1_SETS:
                        k, part = n // 2, n % 2
                        cols = slice(part * BANK, (part + 1) * BANK)
                        nc.vector.tensor_tensor(w1[:, b, k, cols], ring[:, g % RING, :], w1T[:, k, cols], ALU.add).then_inc(w_ready, 1)
                    else:
                        f = 2 * (n - W1_SETS)
                        nc.vector.tensor_tensor(w2[:, b, f:f + 2, :], ring[:, g % RING, :].rearrange("p (f c) -> p f c", f=2),
                                                w2T[:, f:f + 2, :], ALU.add).then_inc(w_ready, 1)

            def one_round(i, first, last):
                for b in range(B):
                    for t in range(BT):
                        n = b * BT + t
                        wait(dve, out_done, i * (B * BT) + n + 1)
                        tile = bass.ds(i * BT + (b * SEQ_TILES + t), 1)
                        xt = core.x[:, tile, :].rearrange("p o c -> p (o c)")
                        nc.vector.tensor_tensor(xt, outp[:, n % 2, 0:D], xt, ALU.add).then_inc(sum_done, 1)
                        wait(dve, sum_done, i * (B * BT) + n + 1)
                        nc.vector.bn_stats(core.stats[:, tile, :].rearrange("p o c -> p (o c)"), xt)

            rounds(dve, BLOCKS, one_round)
def gated_linear_attention(core, d):
    nc = core.nc
    DK = D // 2 // HEADS
    DV = D // HEADS
    GATE_NORM = 16.0
    SCALE = DK ** -0.5
    R = 16
    G = B * S // BANK
    GB = S // BANK
    WIDE = P // HEADS
    QUAD = P // 2 // HEADS
    UNITS = [(e, b) for e in range(WIDE) for b in range(B)]
    NU = len(UNITS)
    ROUNDS = DV // WIDE

    with ExitStack() as st:
        def sb(n, shape, dt=F32):
            return st.enter_context(nc.sbuf_tensor("gla_" + n, shape, dt))

        def sem(n):
            return core.sem("gla_" + n)

        w_q, w_k = sb("w_q", [P, KT, P]), sb("w_k", [P, KT, P])
        w_g1, w_g2 = sb("w_g1", [P, KT, R]), sb("w_g2", [R, P])
        w_v, w_g, w_o = sb("w_v", [P, KT, D]), sb("w_g", [P, KT, D]), sb("w_o", [P, KT, D])
        b_g = sb("b_g", [P, KT])
        spread = sb("spread", [P, QUAD, P], F32R)
        head_sel = sb("head_sel", [P, HEADS])
        collect = sb("collect", [P, WIDE, P])
        of_head = sb("of_head", [P, HEADS])
        average = sb("average", [P, P])
        qT, kT = sb("q_chan", [P, B * S]), sb("k_chan", [P, B * S])
        g1T = sb("g1_chan", [R, B * S])
        decay = sb("decay", [P, B * S])
        tmp = sb("tmp", [P, B * S])
        v_split = sb("v_split", [P, DV // QUAD, B * S], F32R)
        gate = sb("gate", [P, KT, B * S])
        kv = sb("kv", [P, 2, S])
        state = sb("state", [P, 2, S])
        qs = sb("q_state", [P, 2, S])
        oT = sb("o_chan", [P, KT, B * S])
        squares = sb("squares", [P, 2, KT, BANK])
        eps = sb("eps", [P, 1])
        ring = st.enter_context(nc.psum_tensor("gla_ring", [P, 4, BANK], F32))
        acc = st.enter_context(nc.psum_tensor("gla_acc", [P, 4, BANK], F32))
        w_loaded, w_end_loaded, setup, s_dve, s_act = (sem("w_loaded"), sem("w_end_loaded"), sem("setup"), sem("dve_steps"),
                                                       sem("act_steps"))
        v_high_done, proj_done, by_act, by_dve = sem("v_high_done"), sem("proj_done"), sem("proj_by_act"), sem("proj_by_dve")
        abs_done, softplus_done, log_done, decay_done = (sem("abs_done"), sem("softplus_done"), sem("log_done"),
                                                         sem("decay_done"))
        v_done, kv_done, scan_done, qs_done, o_done, o_copied = (
            sem("v_done"), sem("kv_done"), sem("scan_done"), sem("qs_done"), sem("o_done"), sem("o_copied"))
        mean_done, centred, squared, var_done, rstd_done, gated, on_done = (
            sem("mean_done"), sem("centred"), sem("squared"), sem("var_done"), sem("rstd_done"), sem("gated"), sem("on_done"))
        out_done, sum_done = sem("out_done"), sem("sum_done")
        block = st.enter_context(nc.Block())

        @block.sync
        def _(sp):
            for t, n in ((w_g1, "L1_attn_Wg1"), (w_k, "L1_attn_Wk"), (w_q, "L1_attn_Wq"), (w_v, "gla_Wv")):
                sp.dma_start(t[:, :, :], d[n].rearrange("(k p) n -> p k n", p=P)).then_inc(w_loaded, 16)
            sp.dma_start(w_g2[:, :], d["L1_attn_Wg2"]).then_inc(w_loaded, 16)
            for t, n in ((w_g, "gla_Wg"), (w_o, "gla_Wo")):
                sp.dma_start(t[:, :, :], d[n].rearrange("(k p) n -> p k n", p=P)).then_inc(w_end_loaded, 16)
            sp.dma_start(b_g[:, :], d["gla_bg_cols"]).then_inc(w_end_loaded, 16)

        PROJ = [(n, g) for n in ("g1", "kg", "k", "q", "v0", "v1") for g in range(G)]
        GATES = [("z%d" % k, g) for g in range(G) for k in range(KT)]
        ALL = PROJ + GATES
        act_before = [sum(w in ("g1", "kg", "z0", "z1") for w, _ in ALL[:n]) for n in range(len(ALL) + 1)]
        dve_before = [n - act_before[n] for n in range(len(ALL) + 1)]
        SETUP = 4
        FIRST_GATES = 4

        @block.tensor
        def _(pe):
            def projection(n):
                what, g = ALL[n]
                cols = slice(g * BANK, (g + 1) * BANK)
                if what == "kg":
                    pe.wait_ge(by_act, g + 1)
                    done = nc.tensor.matmul(ring[:, n % 4, :], w_g2[:, :], g1T[:, cols], start=True, stop=True)
                else:
                    w, rows = {"q": (w_q, P), "k": (w_k, P), "g1": (w_g1, R), "z0": (w_g[:, :, 0:P], P),
                               "v0": (w_v[:, :, 0:P], P), "v1": (w_v[:, :, P:2 * P], P), "z1": (w_g[:, :, P:2 * P], P)}[what]
                    for k in range(KT):
                        done = nc.tensor.matmul(ring[0:rows, n % 4, :], w[:, k, :], core.xT[:, k, cols],
                                                start=(k == 0), stop=(k == KT - 1))
                done.then_inc(proj_done, 1)

            pe.wait_ge(w_loaded, 16 * 5)
            for n in range(len(PROJ)):
                if n >= 4:
                    pe.wait_ge(by_act, act_before[n - 3]) if ALL[n - 4][0] in ("g1", "kg") else pe.wait_ge(by_dve, dve_before[n - 3])
                projection(n)
            pe.wait_ge(by_dve, dve_before[len(PROJ)])
            pe.wait_ge(setup, SETUP)

            def values(i, u):
                e, b = UNITS[u]
                wait(pe, kv_done, i * NU + u - 1)
                quad = (i * WIDE + e) // QUAD
                for c in range(GB):
                    cols = slice(b * S + c * BANK, b * S + (c + 1) * BANK)
                    done = nc.tensor.matmul(ring[:, 2 * (u % 2) + c, :], spread[:, e % QUAD, :], v_split[:, quad, cols],
                                            start=True, stop=True)
                done.then_inc(v_done, 1)

            def outputs(i, u):
                e, b = UNITS[u]
                pe.wait_ge(qs_done, i * NU + u + 1)
                if e == 0:
                    wait(pe, o_copied, i * B - B + b + 1)
                for c in range(GB):
                    done = nc.tensor.matmul(acc[:, GB * b + c, :], collect[:, e, :], qs[:, u % 2, c * BANK:(c + 1) * BANK],
                                            start=(e == 0), stop=(e == WIDE - 1))
                done.then_inc(o_done, 1)

            def one_round(i, first, last):
                if first:
                    values(i, 0)
                    values(i, 1)
                for u in range(NU):
                    if u + 2 < NU:
                        values(i, u + 2)
                    elif not last:
                        values(i + 1, u + 2 - NU)
                    if u > 0:
                        outputs(i, u - 1)
                    elif not first:
                        outputs(i - 1, NU - 1)

            rounds(pe, ROUNDS, one_round)
            pe.wait_ge(w_end_loaded, 48)
            pe.wait_ge(kv_done, DV * B)
            for n in range(len(PROJ), len(PROJ) + FIRST_GATES):
                projection(n)
            outputs(ROUNDS - 1, NU - 1)

            def means(g):
                pe.wait_ge(o_copied, (ROUNDS - 1) * B + g // GB + 1)
                for k in range(KT):
                    done = nc.tensor.matmul(acc[:, g, :], average[:, :], oT[:, k, g * BANK:(g + 1) * BANK],
                                            start=(k == 0), stop=(k == KT - 1))
                done.then_inc(mean_done, 1)

            def variances(g):
                pe.wait_ge(squared, g + 1)
                for k in range(KT):
                    done = nc.tensor.matmul(acc[:, g, :], average[:, :], squares[:, g % 2, k, :],
                                            start=(k == 0), stop=(k == KT - 1))
                done.then_inc(var_done, 1)

            for g in range(G):
                means(g)
            for g in range(G):
                variances(g)
                if g == 0:
                    for n in range(len(PROJ) + FIRST_GATES, len(ALL)):
                        pe.wait_ge(by_act, act_before[n - 3])
                        projection(n)
            pe.wait_ge(by_act, act_before[len(ALL)])
            for t in range(TILES):
                pe.wait_ge(on_done, t * P // BANK + 1)
                if t >= 4:
                    pe.wait_ge(sum_done, t - 3)
                for k in range(KT):
                    done = nc.tensor.matmul(ring[:, t % 4, 0:D], oT[:, k, t * P:(t + 1) * P], w_o[:, k, :],
                                            start=(k == 0), stop=(k == KT - 1))
                done.then_inc(out_done, 1)

        @block.gpsimd
        def _(pool):
            step = Links(pool, setup)
            nc.gpsimd.memset(collect[:, :, :], 0.0)
            nc.gpsimd.memset(eps[:, :], EPS)
            step.after(nc.gpsimd.memset(head_sel[:, :], 1.0))
            step.after(nc.gpsimd.affine_select(out=head_sel[:, :], in_=head_sel[:, :], compare_op=ALU.is_ge, fill=0.0,
                                               base=0, pattern=[[-DK, HEADS]], channel_multiplier=1))
            step.after(nc.gpsimd.affine_select(out=head_sel[:, :], in_=head_sel[:, :], compare_op=ALU.is_ge, fill=0.0,
                                               base=DK - 1, pattern=[[DK, HEADS]], channel_multiplier=-1))
            for e in range(WIDE):
                done = nc.gpsimd.tensor_copy(collect[:, e, e * HEADS:(e + 1) * HEADS], head_sel[:, :])
            step.after(done)
            pool.wait_ge(by_dve, 2 * G)

            def one_round(i, first, last):
                for u, (e, b) in enumerate(UNITS):
                    pool.wait_ge(scan_done, i * NU + u + 1)
                    wait(pool, o_done, i * NU + u - 1)
                    nc.gpsimd.tensor_tensor(qs[:, u % 2, :], state[:, u % 2, :], qT[:, b * S:(b + 1) * S],
                                            ALU.mult).then_inc(qs_done, 1)

            rounds(pool, ROUNDS, one_round)
            for g in range(G):
                cols = slice(g * BANK, (g + 1) * BANK)
                pool.wait_ge(squared, g + 1)
                pool.wait_ge(by_act, act_before[len(PROJ) + KT * (g + 1)])
                nc.gpsimd.tensor_tensor(oT[:, :, cols], oT[:, :, cols], gate[:, :, cols], ALU.mult).then_inc(gated, 1)

        @block.scalar
        def _(act):
            def copy_projection(n):
                what, g = ALL[n]
                act.wait_ge(proj_done, n + 1)
                cols = slice(g * BANK, (g + 1) * BANK)
                if what == "g1":
                    nc.scalar.activation(g1T[:, cols], ring[0:R, n % 4, :], ACT.Copy).then_inc(by_act, 1)
                elif what == "kg":
                    nc.scalar.activation(decay[:, cols], ring[:, n % 4, :], ACT.Copy).then_inc(by_act, 1)
                else:
                    k = int(what[1])
                    nc.scalar.activation(gate[:, k, cols], ring[:, n % 4, :], ACT.Silu, bias=b_g[:, k:k + 1]).then_inc(by_act, 1)

            act.wait_ge(w_loaded, 16 * 5)
            for n in range(2 * G):
                copy_projection(n)
            act.wait_ge(abs_done, 1)
            nc.scalar.activation(tmp[:, :], tmp[:, :], ACT.Exp, scale=-1.0).then_inc(s_act, 1)
            act.wait_ge(s_act, 1)
            nc.scalar.activation(tmp[:, :], tmp[:, :], ACT.Ln, bias=1.0).then_inc(softplus_done, 1)
            act.wait_ge(log_done, 1)
            nc.scalar.activation(decay[:, :], decay[:, :], ACT.Exp, scale=1.0 / GATE_NORM).then_inc(decay_done, 1)
            for n in range(4 * G, 6 * G):
                act.wait_ge(proj_done, n + 1)
                what, g = ALL[n]
                for half in range(2):
                    done = nc.scalar.copy(v_split[0:P // 2, 2 * int(what[1]) + half, g * BANK:(g + 1) * BANK],
                                          ring[half * (P // 2):(half + 1) * (P // 2), n % 4, :])
                done.then_inc(v_high_done, 1)

            for i in range(ROUNDS):
                for b in range(B):
                    act.wait_ge(o_done, i * NU + NU - B + b + 1)
                    nc.scalar.copy(oT[:, i, b * S:(b + 1) * S],
                                   acc[:, GB * b:GB * (b + 1), :].rearrange("p c n -> p (c n)")).then_inc(o_copied, 1)
                    if i == ROUNDS - 1 and b == 0:
                        act.wait_ge(w_end_loaded, 48)
                        for n in range(len(PROJ), len(PROJ) + FIRST_GATES):
                            copy_projection(n)

            for g in range(G):
                act.wait_ge(centred, g + 1)
                if g >= 2:
                    act.wait_ge(var_done, g - 1)
                nc.scalar.activation(squares[:, g % 2, :, :], oT[:, :, g * BANK:(g + 1) * BANK], ACT.Square).then_inc(squared, 1)
                if g == 1:
                    for n in range(len(PROJ) + FIRST_GATES, len(ALL)):
                        copy_projection(n)
            for g in range(G):
                act.wait_ge(var_done, g + 1)
                nc.scalar.activation(tmp[:, g * BANK:(g + 1) * BANK], acc[:, g, :], ACT.Ln, bias=eps[:, 0:1]).then_inc(s_act, 1)
            for g in range(G):
                act.wait_ge(s_act, 1 + g + 1)
                nc.scalar.activation(tmp[:, g * BANK:(g + 1) * BANK], tmp[:, g * BANK:(g + 1) * BANK], ACT.Exp,
                                     scale=-0.5).then_inc(rstd_done, 1)

        @block.vector
        def _(dve):
            step = Links(dve, s_dve)
            halves = core.ident[:, :].rearrange("p (z e o) -> p z e o", z=2, o=1)
            nc.vector.tensor_tensor(spread[:, :, :].rearrange("p q (h c) -> p (q h) c", c=DK),
                                    halves[:, 0, :, :].to_broadcast([P, P // 2, DK]),
                                    halves[:, 1, :, :].to_broadcast([P, P // 2, DK]), ALU.add)
            step.after(nc.vector.tensor_reduce(of_head[:, :], core.ident[:, :].rearrange("p (e h) -> p h e", h=HEADS), AX, ALU.add))
            nc.vector.tensor_scalar(average[:, :].rearrange("p (e h) -> p e h", h=HEADS),
                                    of_head[:, :].rearrange("p (o h) -> p o h", o=1).to_broadcast([P, WIDE, HEADS]),
                                    1.0 / DV, None, ALU.mult)
            dve.wait_ge(by_act, 2 * G)
            nc.vector.scalar_tensor_tensor(tmp[:, :], decay[:, :], -1.0, decay[:, :], ALU.mult, ALU.max).then_inc(abs_done, 1)

            def copy_projections(what, dst, factor):
                for g in range(G):
                    n = PROJ.index((what, g))
                    dve.wait_ge(proj_done, n + 1)
                    nc.vector.tensor_scalar(dst[:, g * BANK:(g + 1) * BANK], ring[:, n % 4, :], factor, None,
                                            ALU.mult).then_inc(by_dve, 1)

            copy_projections("k", kT, SCALE)
            dve.wait_ge(softplus_done, 1)
            nc.vector.scalar_tensor_tensor(decay[:, :], decay[:, :], 0.0, tmp[:, :], ALU.min, ALU.subtract).then_inc(log_done, 1)
            copy_projections("q", qT, 1.0)
            for j in range(KT * G):
                n = 4 * G + j
                cols = slice(j % G * BANK, (j % G + 1) * BANK)
                dve.wait_ge(v_high_done, j + 1)
                for half in range(2):
                    quad = 2 * (j // G) + half
                    done = nc.vector.tensor_tensor(v_split[P // 2:P, quad, cols], ring[half * (P // 2):(half + 1) * (P // 2), n % 4, :],
                                                   v_split[0:P // 2, quad, cols].bitcast(F32), ALU.subtract)
                done.then_inc(by_dve, 1)
            dve.wait_ge(decay_done, 1)

            def key_times_value(i, u):
                dve.wait_ge(v_done, i * NU + u + 1)
                wait(dve, scan_done, i * NU + u - 1)
                b = UNITS[u][1]
                nc.vector.tensor_tensor(kv[:, u % 2, :], ring[:, 2 * (u % 2):2 * (u % 2) + 2, :].rearrange("p c n -> p (c n)"),
                                        kT[:, b * S:(b + 1) * S], ALU.mult).then_inc(kv_done, 1)

            def one_round(i, first, last):
                if first:
                    key_times_value(i, 0)
                for u, (e, b) in enumerate(UNITS):
                    if u + 1 < NU:
                        key_times_value(i, u + 1)
                    elif not last:
                        key_times_value(i + 1, 0)
                    dve.wait_ge(kv_done, i * NU + u + 1)
                    wait(dve, qs_done, i * NU + u - 1)
                    nc.vector.tensor_tensor_scan(state[:, u % 2, :], decay[:, b * S:(b + 1) * S], kv[:, u % 2, :], 0.0,
                                                 ALU.mult, ALU.add).then_inc(scan_done, 1)

            rounds(dve, ROUNDS, one_round)
            for g in range(G):
                here = oT[:, :, g * BANK:(g + 1) * BANK]
                dve.wait_ge(mean_done, g + 1)
                nc.vector.tensor_tensor(here, here, acc[:, g:g + 1, :].to_broadcast([P, KT, BANK]), ALU.subtract).then_inc(centred, 1)

            def normalise(g):
                here = oT[:, :, g * BANK:(g + 1) * BANK]
                dve.wait_ge(gated, g + 1)
                dve.wait_ge(rstd_done, g + 1)
                rstd = tmp[:, g * BANK:(g + 1) * BANK].rearrange("p (o n) -> p o n", o=1).to_broadcast([P, KT, BANK])
                nc.vector.tensor_tensor(here, here, rstd, ALU.mult).then_inc(on_done, 1)

            normalise(0)
            for t in range(TILES):
                if t % 4 == 0 and t // 4 + 1 < G:
                    normalise(t // 4 + 1)
                dve.wait_ge(out_done, t + 1)
                nc.vector.tensor_tensor(core.x[:, t, :], ring[:, t % 4, 0:D], core.x[:, t, :], ALU.add).then_inc(sum_done, 1)
                dve.wait_ge(sum_done, t + 1)
                nc.vector.bn_stats(core.stats[:, t, :], core.x[:, t, :])


def expert_ffn(core, d):
    nc = core.nc
    E, K, F = EXPERTS, TOP, 512
    CAP = CAPACITY
    FT = F // P
    CT = CAP // P
    PARTS = [(0, 3), (3, CT)]
    PER = 2
    N = TILES * E
    UPS = FT * len(PARTS)
    TPS = KT * len(PARTS)
    GR = 4

    with ExitStack() as st:
        def sb(n, shape, dt=F32):
            return st.enter_context(nc.sbuf_tensor("moe_" + n, shape, dt))

        def sem(n):
            return core.sem("moe_" + n)

        w_r = sb("w_router", [P, KT, E])
        b_r = sb("b_router", [1, E])
        before = sb("before", [P, P])
        ones = sb("ones", [P, P])
        e_less8 = sb("e_less8", [P, E])
        e_row = sb("e_row", [P, E])
        spare = sb("spare", [P, K, TILES])
        logit, prob, hit, rest = (sb(n, [P, TILES, E]) for n in ("logit", "prob", "hit", "rest"))
        best = [sb(f"best{k}", [P, TILES, E]) for k in range(K)]
        chosen = sb("chosen", [P, TILES, E])
        upto = sb("upto", [P, TILES, E])
        rank = sb("rank", [P, TILES, E])
        row = [sb(f"row{n}", [P, TILES]) for n in range(3)]
        p_best = sb("p_best", [P, K, TILES])
        weight = sb("weight", [P, K, TILES])
        rk, slot, keep = (sb(n, [P, K, TILES]) for n in ("rk", "slot", "keep"))
        to_row = sb("to_row", [P, K, TILES], I32)
        from_row = sb("from_row", [P, K, TILES], I32)
        xe = sb("x_expert", [P, PER, CT, D])
        xeT = sb("x_expert_chan", [P, PER, KT, CAP])
        w1, w2 = sb("w1", [P, PER, KT, F]), sb("w2", [P, PER, FT, D])
        b1, b2 = sb("b1", [P, PER, FT]), sb("b2", [1, PER, D])
        hidden = sb("hidden", [P, PER, FT, CAP])
        ye = sb("y_expert", [P, PER, CT, D])
        got = sb("gathered", [P, GR, K, D])
        route = st.enter_context(nc.psum_tensor("moe_route", [P, BANK], F32))
        tp = st.enter_context(nc.psum_tensor("moe_tp", [P, 2, BANK], F32))
        up = st.enter_context(nc.psum_tensor("moe_up", [P, 3, BANK], F32))
        dn = st.enter_context(nc.psum_tensor("moe_dn", [P, 2, BANK], F32))

        r_loaded, setup, s_dve, logits_done, shifted, exp_done, chosen_done, rank_done, rows_ready = (
            sem(n) for n in ("r_loaded", "setup", "dve_steps", "logits_done", "shifted", "exp_done", "chosen_done",
                             "rank_done", "rows_ready"))
        x_loaded = [sem(f"x_loaded{m}") for m in range(PER)]
        scattered, w_loaded, tp_done, tp_copied, up_done, gelu_done, dn_done, dn_copied, stored = (
            sem(n) for n in ("scattered", "w_loaded", "tp_done", "tp_copied", "up_done", "gelu_done",
                             "dn_done", "dn_copied", "stored"))
        gathered = [sem(f"gathered{n}") for n in range(GR)]
        summed = sem("summed")
        block = st.enter_context(nc.Block())

        @block.sync
        def _(sp):
            sp.dma_start(w_r[:, :, :], d["L1_ffn_router_w"].rearrange("(k p) n -> p k n", p=P)).then_inc(r_loaded, 16)
            sp.dma_start(b_r[:, :], d["L1_ffn_router_b"].rearrange("(o n) -> o n", o=1)).then_inc(r_loaded, 16)
            rows = core.by_expert[0:E * CAP, :].rearrange("(e t p) c -> e p t c", e=E, p=P)
            results = core.y_by_expert[:, :].rearrange("(e t p) c -> e p t c", e=E, p=P)

            def one_round(r, first, last):
                e = r * PER
                for m in range(PER):
                    wait(sp, dn_done, e * CT)
                    sp.dma_start(w1[:, m, :, :], d["moe_w1"][e + m].rearrange("(k p) n -> p k n", p=P)).then_inc(w_loaded, 16)
                    sp.dma_start(w2[:, m, :, :], d["moe_w2"][e + m].rearrange("(k p) n -> p k n", p=P)).then_inc(w_loaded, 16)
                    sp.dma_start(b1[:, m, :], d["moe_b1_cols"][e + m]).then_inc(w_loaded, 16)
                    sp.dma_start(b2[0:1, m, :], d["moe_b2"][e + m].rearrange("(o n) -> o n", o=1)).then_inc(w_loaded, 16)
                for m in range(PER):
                    wait(sp, scattered, 16 * K * TILES)
                    wait(sp, tp_done, e * TPS)
                    sp.dma_start(xe[:, m, :, :], rows[e + m]).then_inc(x_loaded[m], 16)
                for m in range(PER):
                    wait(sp, dn_copied, e * CT + (m + 1) * CT)
                    sp.dma_start(results[e + m], ye[:, m, :, :]).then_inc(stored, 16)

            rounds(sp, E // PER, one_round)

        @block.tensor
        def _(pe):
            pe.wait_ge(r_loaded, 32)
            for t in range(TILES):
                dst = route[:, t * E:(t + 1) * E]
                for k in range(KT):
                    nc.tensor.matmul(dst, core.xT[:, k, t * P:(t + 1) * P], w_r[:, k, :], start=(k == 0), stop=False)
                last = nc.tensor.matmul(dst, core.ones_row[0:1, :], b_r[0:1, :], start=False, stop=True)
            last.then_inc(logits_done, 1)
            pe.wait_ge(chosen_done, 1)
            pe.wait_ge(setup, 6)
            ch = chosen[:, :, :].rearrange("p t e -> p (t e)")
            nc.tensor.matmul(route[:, N:2 * N], before[:, :], ch, start=True, stop=True)
            nc.tensor.matmul(route[:, 2 * N:3 * N], ones[:, :], ch, start=True, stop=True).then_inc(rank_done, 1)

            def one_round(r, first, last):
                e = r * PER
                for m in range(PER):
                    wait(pe, x_loaded[m], r * 16 + 16)
                    n = 0
                    for lo, hi in PARTS:
                        for k in range(KT):
                            if m * TPS + n >= 2:
                                wait(pe, tp_copied, e * TPS + m * TPS + n - 1)
                            else:
                                wait(pe, tp_copied, e * TPS)
                            for t in range(lo, hi):
                                last = nc.tensor.transpose(tp[:, n % 2, (t - lo) * P:(t - lo + 1) * P],
                                                           xe[:, m, t, k * P:(k + 1) * P], core.ident[:, :])
                            last.then_inc(tp_done, 1)
                            n += 1
                    wait(pe, w_loaded, e * 64 + 64 * PER)
                    n = 0
                    for q, (lo, hi) in enumerate(PARTS):
                        wait(pe, tp_copied, e * TPS + m * TPS + (q + 1) * KT)
                        for f in range(FT):
                            if m * UPS + n >= 3:
                                wait(pe, gelu_done, e * UPS + m * UPS + n - 2)
                            else:
                                wait(pe, gelu_done, e * UPS)
                            for k in range(KT):
                                last = nc.tensor.matmul(up[:, (m * UPS + n) % 3, 0:(hi - lo) * P], w1[:, m, k, f * P:(f + 1) * P],
                                                        xeT[:, m, k, lo * P:hi * P], start=(k == 0), stop=(k == KT - 1))
                            last.then_inc(up_done, 1)
                            n += 1
                    wait(pe, gelu_done, e * UPS + (m + 1) * UPS)
                    for t in range(CT):
                        n = m * CT + t
                        if n >= 2:
                            wait(pe, dn_copied, e * CT + n - 1)
                        else:
                            wait(pe, dn_copied, e * CT)
                        for f in range(FT):
                            nc.tensor.matmul(dn[:, n % 2, 0:D], hidden[:, m, f, t * P:(t + 1) * P], w2[:, m, f, :],
                                             start=(f == 0), stop=False)
                        nc.tensor.matmul(dn[:, n % 2, 0:D], core.ones_row[0:1, :], b2[0:1, m, :],
                                         start=False, stop=True).then_inc(dn_done, 1)

            rounds(pe, E // PER, one_round)

        @block.scalar
        def _(act):
            act.wait_ge(shifted, 1)
            nc.scalar.activation(prob[:, :, :], logit[:, :, :], ACT.Exp).then_inc(exp_done, 1)

            def one_round(r, first, last):
                e = r * PER
                for m in range(PER):
                    wait(act, dn_done, e * CT)
                    n = 0
                    for q, (lo, hi) in enumerate(PARTS):
                        for f in range(FT):
                            wait(act, up_done, e * UPS + m * UPS + n + 1)
                            nc.scalar.activation(hidden[:, m, f, lo * P:hi * P], up[:, (m * UPS + n) % 3, 0:(hi - lo) * P],
                                                 ACT.Gelu, bias=b1[:, m, f:f + 1]).then_inc(gelu_done, 1)
                            n += 1

            rounds(act, E // PER, one_round)

        @block.gpsimd
        def _(pool):
            step = Links(pool, setup)
            nc.gpsimd.memset(ones[:, :], 1.0)
            step.after(nc.gpsimd.memset(before[:, :], 1.0))
            step.after(nc.gpsimd.affine_select(out=before[:, :], in_=before[:, :], compare_op=ALU.is_gt, fill=0.0,
                                               base=0, pattern=[[1, P]], channel_multiplier=-1))
            step.after(nc.gpsimd.iota(e_less8[:, :], pattern=[[1, E]], base=-E, channel_multiplier=0,
                                      allow_small_or_imprecise_dtypes=True))
            step.after(nc.gpsimd.iota(e_row[:, :], pattern=[[CAP, E]], base=0, channel_multiplier=0,
                                      allow_small_or_imprecise_dtypes=True))
            step.after(nc.gpsimd.iota(spare[:, :, :], pattern=[[B * S, K], [P, TILES]], base=E * CAP, channel_multiplier=1,
                                      allow_small_or_imprecise_dtypes=True))
            step.after(nc.gpsimd.memset(upto[:, :, :], 1.0))
            pool.wait_ge(core.zeroed, 16)
            pool.wait_ge(rows_ready, 1)
            for t in range(TILES):
                for k in range(K):
                    nc.gpsimd.indirect_dma_start(out=core.by_expert[:, :],
                                                 out_offset=bass.IndirectOffsetOnAxis(ap=to_row[:, k, t:t + 1], axis=0),
                                                 in_=core.x[:, t, :], in_offset=None).then_inc(scattered, 16)
            pool.wait_ge(stored, 16 * E)
            for t in range(TILES):
                if t >= GR:
                    pool.wait_ge(summed, t - GR + 1)
                for k in range(K):
                    nc.gpsimd.indirect_dma_start(out=got[:, t % GR, k, :], out_offset=None, in_=core.y_by_expert[:, :],
                                                 in_offset=bass.IndirectOffsetOnAxis(ap=from_row[:, k, t:t + 1], axis=0)
                                                 ).then_inc(gathered[t % GR], 16)

        @block.vector
        def _(dve):
            step = Links(dve, s_dve)
            shape = [P, TILES, E]

            def per_tile(a):
                return a.rearrange("p (t o) -> p t o", o=1).to_broadcast(shape)

            def per_expert(a):
                return a[:, :].rearrange("p (o e) -> p o e", o=1).to_broadcast(shape)

            def combine(out, a, b, op):
                step.after(nc.vector.tensor_tensor(out, a, b, op))

            dve.wait_ge(logits_done, 1)
            lg = route[:, 0:N].rearrange("p (t e) -> p t e", e=E)
            step.after(nc.vector.tensor_reduce(row[0][:, :], lg, AX, ALU.max))
            nc.vector.tensor_tensor(logit[:, :, :], lg, per_tile(row[0][:, :]), ALU.subtract).then_inc(shifted, 1)
            dve.wait_ge(exp_done, 1)
            step.after(nc.vector.tensor_reduce(row[1][:, :], prob[:, :, :], AX, ALU.add))
            step.after(nc.vector.reciprocal(row[2][:, :], row[1][:, :]))
            combine(prob[:, :, :], prob[:, :, :], per_tile(row[2][:, :]), ALU.mult)
            dve.wait_ge(setup, 6)
            left = prob
            for k in range(K):
                step.after(nc.vector.tensor_reduce(p_best[:, k, :], left[:, :, :], AX, ALU.max))
                combine(hit[:, :, :], left[:, :, :], per_tile(p_best[:, k, :]), ALU.is_equal)
                combine(hit[:, :, :], hit[:, :, :], per_expert(e_less8), ALU.mult)
                step.after(nc.vector.tensor_reduce(row[0][:, :], hit[:, :, :], AX, ALU.min))
                combine(best[k][:, :, :], per_expert(e_less8), per_tile(row[0][:, :]), ALU.is_equal)
                if k + 1 < K:
                    step.after(nc.vector.scalar_tensor_tensor(rest[:, :, :], best[k][:, :, :], -2.0, left[:, :, :], ALU.mult, ALU.add))
                    left = rest
            combine(chosen[:, :, :], best[0][:, :, :], best[1][:, :, :], ALU.add)
            dve.sem_inc(chosen_done, 1)
            combine(row[1][:, :], p_best[:, 0, :], p_best[:, 1, :], ALU.add)
            step.after(nc.vector.tensor_scalar(row[1][:, :], row[1][:, :], 1e-9, None, ALU.max))
            step.after(nc.vector.reciprocal(row[2][:, :], row[1][:, :]))
            for k in range(K):
                combine(weight[:, k, :], p_best[:, k, :], row[2][:, :], ALU.mult)
            dve.wait_ge(rank_done, 1)
            totals = route[:, 2 * N:3 * N].rearrange("p (t e) -> p t e", e=E)
            for e in range(E):
                last = nc.vector.tensor_tensor_scan(rest[:, :, e], upto[:, :, e], totals[:, :, e], 0.0, ALU.mult, ALU.add)
            step.after(last)
            combine(rest[:, :, :], rest[:, :, :], totals, ALU.subtract)
            combine(rank[:, :, :], rest[:, :, :], route[:, N:2 * N].rearrange("p (t e) -> p t e", e=E), ALU.add)
            for k in range(K):
                combine(hit[:, :, :], best[k][:, :, :], rank[:, :, :], ALU.mult)
                step.after(nc.vector.tensor_reduce(rk[:, k, :], hit[:, :, :], AX, ALU.add))
                combine(hit[:, :, :], best[k][:, :, :], per_expert(e_row), ALU.mult)
                step.after(nc.vector.tensor_reduce(slot[:, k, :], hit[:, :, :], AX, ALU.add))
            combine(slot[:, :, :], slot[:, :, :], rk[:, :, :], ALU.add)
            step.after(nc.vector.tensor_scalar(keep[:, :, :], rk[:, :, :], float(CAP), None, ALU.is_lt))
            combine(weight[:, :, :], weight[:, :, :], keep[:, :, :], ALU.mult)
            combine(from_row[:, :, :], slot[:, :, :], keep[:, :, :], ALU.mult)
            combine(slot[:, :, :], slot[:, :, :], spare[:, :, :], ALU.subtract)
            combine(slot[:, :, :], slot[:, :, :], keep[:, :, :], ALU.mult)
            combine(to_row[:, :, :], slot[:, :, :], spare[:, :, :], ALU.add)
            dve.sem_inc(rows_ready, 1)

            def one_round(r, first, last):
                e = r * PER
                for m in range(PER):
                    wait(dve, up_done, e * UPS)
                    n = 0
                    for lo, hi in PARTS:
                        for k in range(KT):
                            wait(dve, tp_done, e * TPS + m * TPS + n + 1)
                            nc.vector.tensor_copy(xeT[:, m, k, lo * P:hi * P], tp[:, n % 2, 0:(hi - lo) * P]).then_inc(tp_copied, 1)
                            n += 1
                    wait(dve, stored, e * 16)
                    for t in range(CT):
                        n = m * CT + t
                        wait(dve, dn_done, e * CT + n + 1)
                        nc.vector.tensor_copy(ye[:, m, t, :], dn[:, n % 2, 0:D]).then_inc(dn_copied, 1)

            rounds(dve, E // PER, one_round)
            for t in range(TILES):
                dve.wait_ge(gathered[t % GR], 16 * K * (t // GR + 1))
                for k in range(K):
                    last = nc.vector.scalar_tensor_tensor(core.x[:, t, :], got[:, t % GR, k, :], weight[:, k, t:t + 1],
                                                          core.x[:, t, :], ALU.mult, ALU.add)
                    step.after(last)
                nc.vector.bn_stats(core.stats[:, t, :], core.x[:, t, :]).then_inc(summed, 1)


LAYERS = [latent_attention, cross_attention_0, lora_ffn, gated_linear_attention, cross_attention_1, expert_ffn]


def build(nc, d, out, layers=range(len(LAYERS))):
    with ExitStack() as stack:
        core = Core(nc, stack)
        constants_and_loads(core, d)
        for nth, n in enumerate(layers):
            LAYERS[n](core, d)
            layer_norm(core, nth, out if n == layers[-1] else None)


def arrays_of(inputs):
    import numpy as np
    a = {n: np.ascontiguousarray(v) for n, v in inputs.items()}
    a["x_chan"] = np.ascontiguousarray(a["x"].reshape(B * S, D).T)
    a["ctx_chan"] = np.ascontiguousarray(a["ctx_1024"].reshape(B * CTX, D).T)
    a["w_q_pairs"] = np.ascontiguousarray(a["L0_attn_w_q"].reshape(KT, P, 8, P).transpose(2, 1, 0, 3))
    a["w_kv_up_pairs"] = np.ascontiguousarray(a["L0_attn_w_kv_up"].reshape(P, 16, P).transpose(1, 0, 2))
    a["x0_mask"] = a.pop("mask_BxSxS2_bf0")
    a["x1_mask"] = a.pop("mask_Bx1xSxS2_ik1").reshape(B, S, CTX)
    for n in ("Wq", "Wk", "Wv", "Wo", "bq", "bk", "bv", "bo"):
        a["x0_" + n] = a.pop("L0_xattn_" + n)
    for n in ("Wq", "Wk", "Wv", "Wo"):
        a["x1_" + n] = np.ascontiguousarray(a.pop("L1_xattn_" + n).T)
    a["w1T"] = np.ascontiguousarray(a.pop("L0_ffn_W1").T)
    a["w2T"] = np.ascontiguousarray(a.pop("L0_ffn_W2").T)
    a["L0_ffn_b1_cols"] = np.ascontiguousarray(a.pop("L0_ffn_b1").reshape(-1, P).T)
    a["L0_ffn_scale"] = a["L0_ffn_scale"].reshape(1, 1)
    DV = D // HEADS
    for n in ("Wv", "Wg"):
        a["gla_" + n] = np.ascontiguousarray(a.pop("L1_attn_" + n).reshape(D, HEADS, DV).transpose(0, 2, 1)).reshape(D, D)
    a["gla_Wo"] = np.ascontiguousarray(a.pop("L1_attn_Wo").reshape(HEADS, DV, D).transpose(1, 0, 2)).reshape(D, D)
    a["gla_bg_cols"] = np.ascontiguousarray(a.pop("L1_attn_bg").reshape(HEADS, DV).T.reshape(KT, P).T)
    a["moe_w1"], a["moe_w2"], a["moe_b2"] = a.pop("L1_ffn_w1"), a.pop("L1_ffn_w2"), a.pop("L1_ffn_b2")
    a["moe_b1_cols"] = np.ascontiguousarray(a.pop("L1_ffn_b1").reshape(EXPERTS, -1, P).transpose(0, 2, 1))
    a["x1_bo"] = a.pop("L1_xattn_bo")
    return a


def kernel(**inputs):
    import numpy as np
    from concourse import bacc
    from concourse.bass_utils import run_bass_kernel_spmd

    nc = bacc.Bacc("TRN2", target_bir_lowering=False, num_devices=1)
    arrays = {"in_" + n: v for n, v in arrays_of({n: np.asarray(v) for n, v in inputs.items()}).items()}
    d = {n[3:]: nc.dram_tensor(n, v.shape, mybir.dt.from_np(v.dtype), kind="ExternalInput").ap() for n, v in arrays.items()}
    out = nc.dram_tensor("out", (B, S, D), F32, kind="ExternalOutput").ap()
    build(nc, d, out)
    return run_bass_kernel_spmd(nc, [arrays], core_ids=[0]).results[0]["out"]
```

```python
import concourse.bass as bass
from concourse import mybir
from contextlib import ExitStack

F32 = mybir.dt.float32
F32R = mybir.dt.float32r
BF16 = mybir.dt.bfloat16
I32 = mybir.dt.int32
U8 = mybir.dt.uint8
ALU = mybir.AluOpType
ACT = mybir.ActivationFunctionType
AX = mybir.AxisListType.X

P = 128
B, S, D = 2, 1024, 256
CTX = 154
KT = D // P
TILES = B * S // P
SEQ_TILES = S // P
HEADS = 16
EPS = 1e-5
BANK = 512
NEG = -1e30


EXPERTS, TOP = 8, 2
CAPACITY = -(-5 * B * S * TOP // (4 * EXPERTS))


class Links:

    def __init__(self, engine, sem, base=0):
        self.engine, self.sem, self.base, self.n = engine, sem, base, 0

    def after(self, instruction):
        instruction.then_inc(self.sem, 1)
        self.n += 1
        self.engine.wait_ge(self.sem, self.base + self.n)

    def mark(self, instruction):
        instruction.then_inc(self.sem, 1)
        self.n += 1
        return self.base + self.n

    def reached(self, mark):
        self.engine.wait_ge(self.sem, mark)


def wait(engine, sem, n):
    if not isinstance(n, int) or n > 0:
        engine.wait_ge(sem, n)


def rounds(engine, n, body):
    body(0, True, n == 1)
    if n > 2:
        with engine.Fori(1, n - 1) as i:
            body(i, False, False)
    if n > 1:
        body(n - 1, False, True)


class Core:

    def __init__(self, nc, stack):
        self.nc = nc
        self.stack = self.semaphores = stack

        def sb(name, shape, dt=F32):
            return stack.enter_context(nc.sbuf_tensor(name, shape, dt))

        self.x = sb("x_tok", [P, TILES, D])
        self.xT = sb("x_chan", [P, KT, B * S])
        self.ctxT = sb("ctx_chan", [P, KT, B, CTX])
        self.ident = sb("ident", [P, P])
        self.ident_bf = sb("ident_bf", [P, P], BF16)
        self.ones_row = sb("ones_row", [1, P])
        self.stats = sb("ln_stats", [P, TILES, 6])
        self.mean_var = sb("ln_mean_var", [P, TILES, 2])
        self.var_eps = sb("ln_var_eps", [P, TILES])
        self.rstd = sb("ln_rstd", [P, TILES])
        self.minus_half = sb("minus_half", [P, TILES])
        self.zeros = sb("zeros", [P, D])
        rows = EXPERTS * CAPACITY
        self.by_expert = nc.dram_tensor("rows_by_expert", (rows + TOP * B * S, D), F32).ap()
        self.y_by_expert = nc.dram_tensor("results_by_expert", (rows, D), F32).ap()
        self.ln_sems = [self.sem("ln_" + n) for n in ("dve_steps", "var_ready", "rstd_ready", "x_ready", "xT_in_psum",
                                                      "xT_copied", "stored")]
        self.zeroed = self.sem("rows_zeroed")
        self.xT_loaded, self.x_loaded = self.sem("x_chan_loaded"), self.sem("x_and_context_loaded")
        self.weights = {}
        self.to_zero, self.to_load = [], []

    def tile(self, name, shape, dt=F32):
        return self.stack.enter_context(self.nc.sbuf_tensor(name, shape, dt))

    def start_zeroing(self, pool):
        for zero in self.to_zero:
            zero(pool)
        self.to_zero = []

    def start_loads(self, sp, layers=9):
        for load in self.to_load[:layers]:
            load(sp)
        self.to_load = self.to_load[layers:]

    def sem(self, name):
        return self.semaphores.enter_context(self.nc.semaphore(name))


def constants_and_loads(core, d):
    nc = core.nc
    with ExitStack() as st:
        made = core.sem("constants_made")
        block = st.enter_context(nc.Block())

        @block.sync
        def _(sp):
            sp.dma_start(core.xT[:, :, :], d["x_chan"].rearrange("(k p) n -> p k n", p=P)).then_inc(core.xT_loaded, 16)
            sp.wait_ge(made, 4)
            rows = EXPERTS * CAPACITY
            sp.dma_start(core.by_expert[0:rows, :].rearrange("(t p) c -> p t c", p=P),
                         core.zeros[:, :].rearrange("p (o c) -> p o c", o=1).to_broadcast([P, rows // P, D])).then_inc(core.zeroed, 16)

        @block.gpsimd
        def _(pool):
            step = Links(pool, made)
            nc.gpsimd.memset(core.ones_row[:, :], 1.0)
            nc.gpsimd.memset(core.minus_half[:, :], -0.5)
            step.after(nc.gpsimd.memset(core.ident[:, :], 0.0))
            step.after(nc.gpsimd.affine_select(out=core.ident[:, :], in_=core.ident[:, :], compare_op=ALU.not_equal,
                                               fill=1.0, base=0, pattern=[[-1, P]], channel_multiplier=1))
            step.after(nc.gpsimd.tensor_copy(core.ident_bf[:, :], core.ident[:, :]))
            step.after(nc.gpsimd.memset(core.zeros[:, :], 0.0))


def load_tokens(core, d, sp):
    sp.dma_start(core.x[:, :, :], d["x"].rearrange("b (t p) c -> p (b t) c", p=P)).then_inc(core.x_loaded, 16)
    sp.dma_start(core.ctxT[:, :, :, :].rearrange("p k b n -> p k (b n)"),
                 d["ctx_chan"].rearrange("(k p) n -> p k n", p=P)).then_inc(core.x_loaded, 16)


def layer_norm(core, nth, out=None):
    nc = core.nc
    RING = 4
    GROUP = 4
    COPIES = TILES // GROUP * KT
    s_dve, var_ready, rstd_ready, x_ready, xT_in_psum, xT_copied, stored = core.ln_sems
    with ExitStack() as st:
        ring = st.enter_context(nc.psum_tensor(f"ln{nth}_xT_psum", [P, RING, BANK], F32))
        block = st.enter_context(nc.Block())

        @block.vector
        def _(dve):
            step = Links(dve, s_dve, nth)
            for t in range(TILES):
                last = nc.vector.bn_aggr(core.mean_var[:, t, :], core.stats[:, t, :])
            step.after(last)
            nc.vector.tensor_scalar(core.var_eps[:, :], core.mean_var[:, :, 1], EPS, None, ALU.add).then_inc(var_ready, 1)
            dve.wait_ge(rstd_ready, nth + 1)
            for t in range(TILES):
                nc.vector.tensor_scalar(core.x[:, t, :], core.x[:, t, :], core.mean_var[:, t, 0:1],
                                        core.rstd[:, t:t + 1], ALU.subtract, ALU.mult).then_inc(x_ready, 1)

        @block.gpsimd
        def _(pool):
            pool.wait_ge(var_ready, nth + 1)
            nc.gpsimd.tensor_tensor(core.rstd[:, :], core.var_eps[:, :], core.minus_half[:, :], ALU.pow).then_inc(rstd_ready, 1)

        if out is not None:
            @block.sync
            def _(sp):
                o = out.rearrange("b (t p) c -> p (b t) c", p=P)
                for g in range(TILES // GROUP):
                    sp.wait_ge(x_ready, TILES * nth + GROUP * (g + 1))
                    sp.dma_start(o[:, GROUP * g:GROUP * (g + 1), :],
                                 core.x[:, GROUP * g:GROUP * (g + 1), :]).then_inc(stored, 16)
                sp.wait_ge(stored, 16 * (TILES // GROUP))
            return

        @block.sync
        def _(sp):
            core.start_loads(sp, 1)

        @block.tensor
        def _(pe):
            for g in range(TILES // GROUP):
                for k in range(KT):
                    n = g * KT + k
                    if n >= RING:
                        pe.wait_ge(xT_copied, COPIES * nth + n - RING + 1)
                    for i in range(GROUP):
                        pe.wait_ge(x_ready, TILES * nth + GROUP * g + i + 1)
                        last = nc.tensor.transpose(ring[:, n % RING, i * P:(i + 1) * P],
                                                   core.x[:, GROUP * g + i, k * P:(k + 1) * P], core.ident[:, :])
                    last.then_inc(xT_in_psum, 1)

        @block.scalar
        def _(act):
            for g in range(TILES // GROUP):
                for k in range(KT):
                    n = g * KT + k
                    act.wait_ge(xT_in_psum, COPIES * nth + n + 1)
                    nc.scalar.activation(core.xT[:, k, g * BANK:(g + 1) * BANK], ring[:, n % RING, :],
                                         ACT.Copy).then_inc(xT_copied, 1)


def latent_attention(core, d):
    nc = core.nc
    DH, RANK = 64, P
    PAIRS = HEADS * DH // P
    SCALE = DH ** -0.5
    GROUPS = S // BANK
    PROJECTIONS = [(what, g) for what in "qkv" for g in range(GROUPS)]
    UNITS = [(b, t, h) for b in range(B) for t in range(SEQ_TILES) for h in range(2)]
    NU = len(UNITS)
    CHUNK = BANK // P
    VW = 2 * DH + 2
    HALF = NU // B
    NPROJ = len(PROJECTIONS)
    USES = [(u, c) for u, (b, t, h) in enumerate(UNITS) for c in range((t + CHUNK) // CHUNK)]
    NC = len(USES)
    START = [min(i for i, (v, _) in enumerate(USES) if v == u) for u in range(NU)] + [NC]
    RING = 2
    assert NC % RING == 0

    def projections_at(u, last):
        n = u % HALF
        if n >= NPROJ or (last and u >= HALF):
            return []
        return [(u // HALF * NPROJ + n, (PROJECTIONS[n][0], 1 - u // HALF, PROJECTIONS[n][1]))]

    def spare(n):
        return 2 * (n % 2) + 1

    def blocks(u):
        return UNITS[u][1] + 1

    def shifted(i, u):
        return (i - 1, u + NU) if u < 0 else (i + 1, u - NU) if u >= NU else (i, u)

    with ExitStack() as st:
        def sb(n, shape, dt=F32):
            return st.enter_context(nc.sbuf_tensor("mla_" + n, shape, dt))

        def sem(n):
            return core.sem("mla_" + n)

        w_down = sb("w_down", [P, KT, RANK])
        w_q = sb("w_q", [P, KT, P])
        w_k = sb("w_k", [P, P])
        w_v = sb("w_v", [P, P])
        latT = sb("latent_chan", [P, B * S])
        assert PAIRS * D == B * S
        w_out = latT[:, :].rearrange("p (k n) -> p k n", k=PAIRS)
        q_split = sb("q_split", [P, 2, B * S], F32R)
        k_high = sb("k_high", [P, 2, B * S], F32R)
        k_low = sb("k_low", [P, 2, B * S], F32R)
        v = sb("v_tok", [P, TILES, 2, VW], F32R)
        causal = sb("causal", [P, P], BF16)
        causal32 = sb("causal32", [P, P])
        p_tok = sb("exps_tok", [P, 2, S])
        pT_high = sb("exps_key_high", [P, 2, SEQ_TILES, P], F32R)
        pT_low = sb("exps_key_low", [P, 2, SEQ_TILES, P], F32R)
        y = sb("y_tok", [P, TILES, HEADS * DH])
        yT_high, yT_low = (t[:, :, 0:PAIRS * P].rearrange("p b (k q) -> p b k q", k=PAIRS) for t in (k_high, k_low))
        w_high, w_low = (q_split[:, n, :].rearrange("p (k c) -> p k c", k=PAIRS) for n in range(2))
        neg_max = sb("neg_max", [P, 4])
        inv_sum = sb("inv_sum", [P, 2])
        y_high = sb("y_high", [P, 2, DH])
        one_zero = sb("one_zero", [P, 2])
        scores = st.enter_context(nc.psum_tensor("mla_scores", [P, 4, BANK], F32))
        tpose = st.enter_context(nc.psum_tensor("mla_tpose", [P, RING, BANK], F32))
        outp = st.enter_context(nc.psum_tensor("mla_outp", [P, 2, BANK], F32))

        w_loaded, setup = sem("w_loaded"), sem("setup")
        wd_loaded, lat_done, lat_copied = sem("wd_loaded"), sem("lat_done"), sem("lat_copied")
        proj_done, proj_act, proj_dve = sem("proj_done"), sem("proj_by_act"), sem("proj_by_dve")
        qk_done, max_done, exp_done, t_done = sem("qk_done"), sem("max_done"), sem("exp_done"), sem("t_done")
        inverted, y_high_done = sem("inverted"), sem("y_high_done")
        yT_split, w_out_split = sem("yT_split"), sem("w_out_split")
        pT_high_done, pT_split, pv_done, y_done = sem("pT_high_done"), sem("pT_split"), sem("pv_done"), sem("y_done")
        yT_done, yT_copied, out_done, sum_done = sem("yT_done"), sem("yT_copied"), sem("out_done"), sem("sum_done")
        block = st.enter_context(nc.Block())

        @block.sync
        def _(sp):
            sp.dma_start(w_down[:, :, :], d["L0_attn_w_kv_down"].rearrange("(k p) n -> p k n", p=P)).then_inc(wd_loaded, 16)

            def weights(i, first, last):
                if not first:
                    sp.wait_ge(proj_dve, NPROJ + B * NPROJ * (i - 1) + NPROJ)
                sp.dma_start(w_q[:, :, :], d["w_q_pairs"][i]).then_inc(w_loaded, 16)
                sp.dma_start(w_k[:, :], d["w_kv_up_pairs"][i]).then_inc(w_loaded, 16)
                sp.dma_start(w_v[:, :], d["w_kv_up_pairs"][i + PAIRS]).then_inc(w_loaded, 16)
                if first:
                    load_tokens(core, d, sp)

            rounds(sp, PAIRS, weights)
            sp.wait_ge(proj_dve, NPROJ + B * NPROJ * (PAIRS - 1) + NPROJ)
            sp.dma_start(w_out, d["L0_attn_w_out"].rearrange("(k p) n -> p k n", p=P)).then_inc(wd_loaded, 16)

        @block.gpsimd
        def _(pool):
            step = Links(pool, setup)
            step.after(nc.gpsimd.memset(one_zero[:, 0:1], 1.0))
            step.after(nc.gpsimd.memset(one_zero[:, 1:2], 0.0))
            step.after(nc.gpsimd.tensor_copy(v[:, :, :, DH:DH + 2].rearrange("p t h c -> p (t h) c"),
                                             one_zero[:, :].rearrange("p (o c) -> p o c", o=1).to_broadcast([P, 2 * TILES, 2])))
            step.after(nc.gpsimd.memset(k_low[DH:P, 0, :].bitcast(F32), 0.0))
            step.after(nc.gpsimd.memset(k_low[0:DH, 1, :].bitcast(F32), 0.0))
            step.after(nc.gpsimd.memset(causal32[:, :], 0.0))
            step.after(nc.gpsimd.affine_select(out=causal32[:, :], in_=causal32[:, :], compare_op=ALU.is_ge, fill=NEG,
                                               base=0, pattern=[[-1, P]], channel_multiplier=1))
            step.after(nc.gpsimd.tensor_copy(causal[:, :], causal32[:, :]))

        @block.tensor
        def _(pe):
            pe.wait_ge(core.xT_loaded, 16)
            pe.wait_ge(wd_loaded, 16)
            for g in range(B * GROUPS):
                for k in range(KT):
                    done = nc.tensor.matmul(scores[:, g, :], w_down[:, k, :], core.xT[:, k, g * BANK:(g + 1) * BANK],
                                            start=(k == 0), stop=(k == KT - 1))
                done.then_inc(lat_done, 1)
            pe.wait_ge(lat_copied, B * GROUPS)
            pe.wait_ge(setup, 8)

            def projection(what, b, g, bank):
                n = b * GROUPS + g
                if what == "q":
                    for k in range(KT):
                        done = nc.tensor.matmul(bank, w_q[:, k, :], core.xT[:, k, n * BANK:(n + 1) * BANK],
                                                start=(k == 0), stop=(k == KT - 1))
                elif what == "k":
                    done = nc.tensor.matmul(bank, w_k[:, :], latT[:, n * BANK:(n + 1) * BANK], start=True, stop=True)
                else:
                    for j in range(CHUNK):
                        done = nc.tensor.matmul(bank[:, j * P:(j + 1) * P], latT[:, (CHUNK * n + j) * P:(CHUNK * n + j + 1) * P],
                                                w_v[:, :], start=True, stop=True)
                return done

            def qk(i, u, last=False):
                b, t, h = UNITS[u]
                if u % HALF == HALF // 2 and not last:
                    pe.wait_ge(proj_dve, NPROJ + B * NPROJ * i + NPROJ * (u // HALF + 1))
                wait(pe, exp_done, NU * i + u - 1)
                width = (t + 1) * P
                for c in range(0, width, BANK):
                    n = min(BANK, width - c)
                    bank = 2 * (u % 2) + c // BANK
                    diagonal = c + n == width
                    lhs = q_split[:, h, b * S + t * P:b * S + (t + 1) * P]
                    nc.tensor.matmul(scores[:, bank, 0:n], lhs, k_high[:, h, b * S + c:b * S + c + n], start=True, stop=False)
                    done = nc.tensor.matmul(scores[:, bank, 0:n], lhs, k_low[:, h, b * S + c:b * S + c + n],
                                            start=False, stop=not diagonal)
                    if diagonal:
                        done = nc.tensor.matmul(scores[:, bank, n - P:n], core.ident_bf[:, :], causal[:, :],
                                                start=False, stop=True)
                done.then_inc(qk_done, 1)

            def transposes(i, u):
                pe.wait_ge(exp_done, NU * i + u + 1)
                for c in range(START[u], START[u + 1]):
                    wait(pe, pT_split, NC * i + c - RING + 1)
                    part = USES[c][1]
                    for j in range(min(CHUNK, blocks(u) - part * CHUNK)):
                        at = (part * CHUNK + j) * P
                        done = nc.tensor.transpose(tpose[:, c % RING, j * P:(j + 1) * P],
                                                   p_tok[:, u % 2, at:at + P], core.ident[:, :])
                    done.then_inc(t_done, 1)

            def pv(i, u):
                b, t, h = UNITS[u]
                pe.wait_ge(pT_split, NC * i + START[u + 1])
                wait(pe, y_done, NU * i + u - 1)
                for j in range(blocks(u)):
                    for pT in pT_high, pT_low:
                        done = nc.tensor.matmul(outp[:, u % 2, 0:VW], pT[:, u % 2, j, :], v[:, b * SEQ_TILES + j, h, :],
                                                start=(j == 0 and pT is pT_high),
                                                stop=(j == blocks(u) - 1 and pT is pT_low))
                done.then_inc(pv_done, 1)

            pe.wait_ge(w_loaded, 48)
            for n, (what, g) in enumerate(PROJECTIONS):
                if n >= 4:
                    pe.wait_ge(proj_dve, n - 3)
                projection(what, 0, g, scores[:, n % 4, :]).then_inc(proj_done, 1)
            pe.wait_ge(proj_dve, len(PROJECTIONS))

            def pair(i, first, last):
                if first:
                    qk(i, 0)
                    qk(i, 1)
                for u in range(NU):
                    if u + 2 < NU or not last:
                        qk(*shifted(i, u + 2), last and u + 2 > HALF)
                    if u >= 2 or not first:
                        pv(*shifted(i, u - 2))
                    transposes(i, u)
                    for n, what in projections_at(u, last):
                        if n == NPROJ:
                            pe.wait_ge(w_loaded, 48 * i + 96)
                        pe.wait_ge(proj_dve, NPROJ + B * NPROJ * i + n - 1)
                        projection(*what, scores[:, spare(n), :]).then_inc(proj_done, 1)
                if last:
                    pv(i, NU - 2)
                    pv(i, NU - 1)

            rounds(pe, PAIRS, pair)
            pe.wait_ge(y_done, NU * PAIRS)

            def project(t):
                pe.wait_ge(yT_split, 2 * t + 2)
                if t >= 2:
                    pe.wait_ge(sum_done, t - 1)
                if t == 0:
                    pe.wait_ge(w_out_split, 2)
                for k in range(PAIRS):
                    for yT, w in (yT_high, w_high), (yT_high, w_low), (yT_low, w_high):
                        done = nc.tensor.matmul(tpose[:, t % 2, 0:D], yT[:, t % 2, k, :], w[:, k, :],
                                                start=(k == 0 and yT is yT_high and w is w_high),
                                                stop=(k == PAIRS - 1 and yT is yT_low))
                done.then_inc(out_done, 1)

            for t in range(TILES):
                for half in range(2):
                    n = 2 * t + half
                    if n >= 4:
                        pe.wait_ge(yT_split, n - 3)
                    for j in range(4):
                        k = 4 * half + j
                        last = nc.tensor.transpose(scores[:, n % 4, j * P:(j + 1) * P], y[:, t, k * P:(k + 1) * P],
                                                   core.ident[:, :])
                    last.then_inc(yT_done, 1)
                if t >= 1:
                    project(t - 1)
            project(TILES - 1)

        HEAD = [slice(0, DH), slice(DH, P)]

        LAG = 4

        @block.scalar
        def _(act):
            for g in range(B * GROUPS):
                act.wait_ge(lat_done, g + 1)
                nc.scalar.activation(latT[:, g * BANK:(g + 1) * BANK], scores[:, g, :], ACT.Copy).then_inc(lat_copied, 1)
            act.wait_ge(setup, 8)

            def high_parts(what, b, g, src):
                n = b * GROUPS + g
                cols = slice(n * BANK, (n + 1) * BANK)
                if what == "v":
                    return nc.scalar.activation(v[:, CHUNK * n:CHUNK * (n + 1), :, 0:DH],
                                                src.rearrange("p (t h e) -> p t h e", t=CHUNK, h=2), ACT.Copy)
                if what == "k":
                    nc.scalar.copy(k_high[HEAD[1], 0, cols], src[HEAD[0], :])
                for h in range(2):
                    done = nc.scalar.activation((q_split if what == "q" else k_high)[HEAD[h], h, cols], src[HEAD[h], :],
                                                ACT.Copy, scale=SCALE if what == "q" else 1.0)
                return done

            for n, (what, g) in enumerate(PROJECTIONS):
                act.wait_ge(proj_done, n + 1)
                high_parts(what, 0, g, scores[:, n % 4, :]).then_inc(proj_act, 1)

            def read_ring(i, u):
                for c in range(START[u], START[u + 1]):
                    act.wait_ge(t_done, NC * i + c + 1)
                    part = USES[c][1]
                    wait(act, pv_done, NU * i + u - 1)
                    n = min(CHUNK, blocks(u) - part * CHUNK)
                    nc.scalar.copy(pT_high[:, u % 2, part * CHUNK:part * CHUNK + n, :].rearrange("p j q -> p (j q)"),
                                   tpose[:, c % RING, 0:n * P]).then_inc(pT_high_done, 1)

            def normalise_high(i, u):
                act.wait_ge(inverted, NU * i + u + 1)
                nc.scalar.activation(y_high[:, u % 2, :], outp[:, u % 2, 0:DH], ACT.Copy,
                                     scale=inv_sum[:, u % 2:u % 2 + 1]).then_inc(y_high_done, 1)

            def exponentials(i, u, first):
                act.wait_ge(max_done, NU * i + u + 1)
                if u >= 2:
                    act.wait_ge(t_done, NC * i + START[u - 1])
                elif not first:
                    act.wait_ge(t_done, NC * (i - 1) + START[NU + u - 1])
                nc.scalar.activation(p_tok[:, u % 2, 0:blocks(u) * P],
                                     scores[:, 2 * (u % 2):2 * (u % 2) + 2, :].rearrange("p c n -> p (c n)")[:, 0:blocks(u) * P],
                                     ACT.Exp, bias=neg_max[:, u % 4:u % 4 + 1]).then_inc(exp_done, 1)

            def pair(i, first, last):
                for u in range(NU + LAG if last else NU):
                    if u >= LAG or not first:
                        normalise_high(*shifted(i, u - LAG))
                    if u < NU:
                        exponentials(i, u, first)
                    if u == 0 and not first or 1 <= u <= NU:
                        read_ring(*shifted(i, u - 1) if u < 1 else (i, u - 1))
                    for n, what in projections_at(u - 1, last) if u >= 1 else []:
                        act.wait_ge(proj_done, NPROJ + B * NPROJ * i + n + 1)
                        high_parts(*what, scores[:, spare(n), :]).then_inc(proj_act, 1)

            rounds(act, PAIRS, pair)
            act.wait_ge(exp_done, NU * PAIRS)
            act.wait_ge(wd_loaded, 32)
            nc.scalar.copy(w_high, w_out).then_inc(w_out_split, 1)
            for n in range(2 * TILES):
                t, half = n // 2, n % 2
                act.wait_ge(yT_done, n + 1)
                if t >= 2:
                    act.wait_ge(out_done, t - 1)
                nc.scalar.activation(yT_high[:, t % 2, 4 * half:4 * half + 4, :].rearrange("p k q -> p (k q)"),
                                     scores[:, n % 4, :], ACT.Copy).then_inc(yT_copied, 1)

        @block.vector
        def _(dve):

            def low_parts(what, b, g, src):
                n = b * GROUPS + g
                cols = slice(n * BANK, (n + 1) * BANK)
                if what == "v":
                    tiles = slice(CHUNK * n, CHUNK * (n + 1))
                    return nc.vector.tensor_tensor(v[:, tiles, :, DH + 2:VW], src.rearrange("p (t h e) -> p t h e", t=CHUNK, h=2),
                                                   v[:, tiles, :, 0:DH].bitcast(F32), ALU.subtract)
                high, low = (q_split, q_split) if what == "q" else (k_high, k_low)
                if what == "k":
                    nc.vector.tensor_copy(k_high[HEAD[0], 1, cols], src[HEAD[1], :])
                for h in range(2):
                    rows = HEAD[1 - h] if what == "q" else HEAD[h]
                    done = nc.vector.scalar_tensor_tensor(low[rows, h, cols], src[HEAD[h], :], SCALE if what == "q" else 1.0,
                                                          high[HEAD[h], h, cols].bitcast(F32), ALU.mult, ALU.subtract)
                return done

            for n, (what, g) in enumerate(PROJECTIONS):
                dve.wait_ge(proj_act, n + 1)
                low_parts(what, 0, g, scores[:, n % 4, :]).then_inc(proj_dve, 1)

            def read_ring(i, u):
                for c in range(START[u], START[u + 1]):
                    dve.wait_ge(pT_high_done, NC * i + c + 1)
                    part = USES[c][1]
                    n = min(CHUNK, blocks(u) - part * CHUNK)
                    here = (slice(None), u % 2, slice(part * CHUNK, part * CHUNK + n), slice(None))
                    nc.vector.tensor_tensor(pT_low[here].rearrange("p j q -> p (j q)"), tpose[:, c % RING, 0:n * P],
                                            pT_high[here].rearrange("p j q -> p (j q)").bitcast(F32),
                                            ALU.subtract).then_inc(pT_split, 1)

            def maximum(i, u):
                dve.wait_ge(qk_done, NU * i + u + 1)
                wait(dve, exp_done, NU * i + u - 3)
                nc.vector.tensor_reduce(
                    neg_max[:, u % 4:u % 4 + 1],
                    scores[:, 2 * (u % 2):2 * (u % 2) + 2, :].rearrange("p c n -> p (c n)")[:, 0:blocks(u) * P],
                    AX, ALU.max, negate=True).then_inc(max_done, 1)

            def inverse(i, u):
                dve.wait_ge(pv_done, NU * i + u + 1)
                nc.vector.reciprocal(inv_sum[:, u % 2:u % 2 + 1], outp[:, u % 2, DH:DH + 1]).then_inc(inverted, 1)

            def add_low(i, u):
                b, t, h = UNITS[u]
                dve.wait_ge(y_high_done, NU * i + u + 1)
                nc.vector.scalar_tensor_tensor(y[:, b * SEQ_TILES + t, bass.ds(i * P + h * DH, DH)],
                                               outp[:, u % 2, DH + 2:VW], inv_sum[:, u % 2:u % 2 + 1],
                                               y_high[:, u % 2, :], ALU.mult, ALU.add).then_inc(y_done, 1)

            def pair(i, first, last):
                for u in range(NU + LAG if last else NU):
                    behind = shifted(i, u - LAG) if u >= LAG or not first else None
                    if behind:
                        inverse(*behind)
                    if u < NU:
                        maximum(i, u)
                    if u < 2 and not first or 2 <= u < NU + 2:
                        read_ring(*shifted(i, u - 2) if u < 2 else (i, u - 2))
                    for n, what in projections_at(u - 2, last) if 2 <= u < NU else []:
                        dve.wait_ge(proj_act, NPROJ + B * NPROJ * i + n + 1)
                        low_parts(*what, scores[:, spare(n), :]).then_inc(proj_dve, 1)
                    if behind:
                        add_low(*behind)

            rounds(dve, PAIRS, pair)
            dve.wait_ge(core.x_loaded, 32)
            dve.wait_ge(w_out_split, 1)
            nc.vector.tensor_tensor(w_low, w_out, w_high.bitcast(F32), ALU.subtract).then_inc(w_out_split, 1)

            def low_part(n):
                t, here = n // 2, (slice(None), n // 2 % 2, slice(n % 2 * 4, n % 2 * 4 + 4), slice(None))
                dve.wait_ge(yT_copied, n + 1)
                nc.vector.tensor_tensor(yT_low[here].rearrange("p k q -> p (k q)"), scores[:, n % 4, :],
                                        yT_high[here].rearrange("p k q -> p (k q)").bitcast(F32), ALU.subtract).then_inc(yT_split, 1)

            low_part(0)
            low_part(1)
            for t in range(TILES):
                if t + 1 < TILES:
                    low_part(2 * t + 2)
                    low_part(2 * t + 3)
                dve.wait_ge(out_done, t + 1)
                nc.vector.tensor_tensor(core.x[:, t, :], tpose[:, t % 2, 0:D], core.x[:, t, :], ALU.add).then_inc(sum_done, 1)
                dve.wait_ge(sum_done, t + 1)
                nc.vector.bn_stats(core.stats[:, t, :], core.x[:, t, :])


class CrossWeights:

    def __init__(self, core, d, name, block_diagonal):
        DH = D // HEADS
        self.w = {n: core.tile(f"{name}_w{n}", [P, KT, D]) for n in "qkvo"}
        self.bias_col = core.tile(name + "_bias_col", [P, 2, KT])
        self.bias_row = core.tile(name + "_bias_row", [1, D])
        self.bias_out = core.tile(name + "_bias_out", [P, D])
        self.loaded, zeroed = core.sem(name + "_w_loaded"), core.sem(name + "_w_zeroed")
        self.loads = 16 * (3 * D // DH + 2 if block_diagonal else 8)
        w, loaded = self.w, self.loaded

        def zero(pool):
            for n in "kqv":
                core.nc.gpsimd.memset(w[n][:, :, :], 0.0).then_inc(zeroed, 1)

        def load(sp):
            if block_diagonal:
                sp.wait_ge(zeroed, 3)
                for n in "kqv":
                    for h in range(HEADS):
                        r = h * DH % P
                        sp.dma_start(w[n][r:r + DH, h * DH // P, h * DH:(h + 1) * DH], d[f"{name}_W{n}"]).then_inc(loaded, 16)
                sp.dma_start(w["o"][:, :, :], d[name + "_Wo"].rearrange("(k p) n -> p k n", p=P)).then_inc(loaded, 16)
            else:
                for n in "kvqo":
                    sp.dma_start(w[n][:, :, :], d[f"{name}_W{n}"].rearrange("(k p) n -> p k n", p=P)).then_inc(loaded, 16)
                for j, n in enumerate("qk"):
                    sp.dma_start(self.bias_col[:, j, :], d[f"{name}_b{n}"].rearrange("(k p) -> p k", p=P),
                                 allow_slow_non_contiguous=True).then_inc(loaded, 16)
                sp.dma_start(self.bias_row[0:1, :], d[name + "_bv"].rearrange("(o n) -> o n", o=1)).then_inc(loaded, 16)
            sp.dma_start(self.bias_out[:, :], d[name + "_bo"].rearrange("(o n) -> o n", o=1).to_broadcast([P, D])).then_inc(loaded, 16)

        if block_diagonal:
            core.to_zero.append(zero)
        core.to_load.append(load)


class FfnWeights:

    def __init__(self, core, d):
        FT = 4 * D // P
        self.w1T = core.tile("ffn_w1T", [P, KT, 4 * D])
        self.w2T = core.tile("ffn_w2T", [P, FT, D])
        self.b1 = core.tile("ffn_b1", [P, FT])
        self.b2 = core.tile("ffn_b2", [P, D])
        self.scale = core.tile("ffn_scale", [P, 1])
        self.loaded = core.sem("ffn_w_loaded")

        def load(sp):
            for tile, src in ((self.scale[:, :], d["L0_ffn_scale"].to_broadcast([P, 1])),
                              (self.w1T[:, :, :], d["w1T"].rearrange("(k p) n -> p k n", p=P)),
                              (self.w2T[:, :, :], d["w2T"].rearrange("(k p) n -> p k n", p=P)),
                              (self.b1[:, :], d["L0_ffn_b1_cols"]),
                              (self.b2[:, :], d["L0_ffn_b2"].rearrange("(o n) -> o n", o=1).to_broadcast([P, D]))):
                sp.dma_start(tile, src).then_inc(self.loaded, 16)

        core.to_load.append(load)


class GlaWeights:

    def __init__(self, core, d):
        R = 16
        self.w_q, self.w_k = core.tile("gla_w_q", [P, KT, P]), core.tile("gla_w_k", [P, KT, P])
        self.w_g1, self.w_g2 = core.tile("gla_w_g1", [P, KT, R]), core.tile("gla_w_g2", [R, P])
        self.w_v, self.w_g, self.w_o = (core.tile("gla_w_" + n, [P, KT, D]) for n in "vgo")
        self.b_g = core.tile("gla_b_g", [P, KT])
        self.loaded = core.sem("gla_w_loaded")
        self.loads = 16 * 8

        def load(sp):
            for tile, n in ((self.w_g1, "L1_attn_Wg1"), (self.w_k, "L1_attn_Wk"), (self.w_q, "L1_attn_Wq"), (self.w_v, "gla_Wv"),
                            (self.w_g, "gla_Wg"), (self.w_o, "gla_Wo")):
                sp.dma_start(tile[:, :, :], d[n].rearrange("(k p) n -> p k n", p=P)).then_inc(self.loaded, 16)
            sp.dma_start(self.w_g2[:, :], d["L1_attn_Wg2"]).then_inc(self.loaded, 16)
            sp.dma_start(self.b_g[:, :], d["gla_bg_cols"]).then_inc(self.loaded, 16)

        core.to_load.append(load)


class RouterWeights:

    def __init__(self, core, d):
        self.w = core.tile("moe_w_router", [P, KT, EXPERTS])
        self.b = core.tile("moe_b_router", [P, EXPERTS])
        self.loaded = core.sem("moe_router_loaded")

        def load(sp):
            sp.dma_start(self.w[:, :, :], d["L1_ffn_router_w"].rearrange("(k p) n -> p k n", p=P)).then_inc(self.loaded, 16)
            sp.dma_start(self.b[:, :], d["L1_ffn_router_b"].rearrange("(o n) -> o n", o=1).to_broadcast([P, EXPERTS])
                         ).then_inc(self.loaded, 16)

        core.to_load.append(load)


def cross_attention(core, d, name, block_diagonal, mask_value):
    nc = core.nc
    DH = D // HEADS
    HH = HEADS // 2
    HB = 3
    SB = 3
    REST = CTX - P
    RH = 4
    VW = HH * (DH + 1)
    SCALE = DH ** -0.5
    UNITS = [(b, half) for b in range(B) for half in range(2)]
    NU = len(UNITS)
    CHUNK = BANK // P
    BLOCKS = [(h, None) for h in range(HH)] + [(None, r) for r in range(HH // RH)]
    NCH = -(-len(BLOCKS) // CHUNK)

    def by_dve(c):
        return c == 1

    ACT_CHUNKS = NCH - 1

    with ExitStack() as st:
        def sb(n, shape, dt=F32):
            return st.enter_context(nc.sbuf_tensor(f"{name}_{n}", shape, dt))

        def ps(n, shape):
            return st.enter_context(nc.psum_tensor(f"{name}_{n}", shape, F32))

        def sem(n):
            return core.sem(f"{name}_{n}")

        own_weights = core.weights[name]
        w, bias_col, bias_row, bias_out = own_weights.w, own_weights.bias_col, own_weights.bias_row, own_weights.bias_out
        w_loaded, LOADS = own_weights.loaded, own_weights.loads
        mask_raw = sb("mask_raw", [P, TILES, CTX], U8 if mask_value[0] == "hidden" else I32)
        mask = sb("mask", [P, TILES, CTX], BF16)
        head_of = sb("head_of", [P, HH])
        k_heads = [sb("k_heads_" + n, [P, B, KT, HH, CTX], F32R) for n in ("high", "low")]
        q_parts = [sb("q_chan_" + n, [P, B, KT, P], F32R) for n in ("high", "low")]
        kT_parts = [sb("k_chan_" + n, [P, KT, B * CTX], F32R) for n in ("high", "low")]
        v = sb("v_tok", [P, B, 2, HH * (VW + DH + 1)])
        v_rest = sb("v_rest", [RH * REST, B, 2, HH // RH, VW])
        row_of = sb("row_of", [RH * REST, RH])
        kT = sb("k_chan", [P, KT, B * CTX])
        qT = sb("q_chan", [P, B, KT, P])
        s_max = sb("s_max", [P, HB * SB])
        SLOTS = HB * SB
        p_tok = sb("exps_tok", [P, 2, SLOTS * CTX])
        ctx_rest = sb("ctx_rest", [P, KT, B, RH * REST])
        pT = sb("exps_key", [P, 2, len(BLOCKS), P])
        inv_sum = sb("inv_sum", [P, HEADS])
        y = sb("y_tok", [P, D])
        yT = sb("y_chan", [P, KT, P])
        scores = ps("scores", [P, SB, BANK])
        tpose = ps("tpose", [P, 2, BANK])
        outp = ps("outp", [P, 2, HH, DH + 1])
        q_ps = ps("q_psum", [P, KT, P])
        fin = ps("fin", [P, 2, D])

        mask_loaded, setup = sem("mask_loaded"), sem("setup")
        kT_split = sem("k_chan_split")
        kv_done, kv_copied, kv_heads = sem("kv_done"), sem("kv_copied"), sem("kv_heads")
        q_split = sem("q_split")
        q_done, q_copied, qk_done, sub_done, exp_done = sem("q_done"), sem("q_copied"), sem("qk_done"), sem("sub_done"), sem("exp_done")
        t_done, copied_act, copied_dve, pv_done = sem("t_done"), sem("pT_by_act"), sem("pT_by_dve"), sem("pv_done")
        y_done, yT_done, yT_copied, out_done, sum_done, s_dve = (sem("y_done"), sem("yT_done"), sem("yT_copied"),
                                                                 sem("out_done"), sem("sum_done"), sem("dve_steps"))
        mask_ready, bias_added, v_ready = sem("mask_ready"), sem("bias_added"), sem("v_ready")
        block = st.enter_context(nc.Block())

        def copy_chunk(copy, u, c):
            first = c * CHUNK
            n = min(CHUNK, len(BLOCKS) - first)
            rows = P if first < HH else RH * REST
            return copy(pT[0:rows, u % 2, first:first + n, :].rearrange("p j q -> p (j q)"), tpose[0:rows, (NCH * u + c) % 2, 0:n * P])

        SETUP = 3 + 1 + 3 + 3

        @block.sync
        def _(sp):
            sp.dma_start(mask_raw[:, :, :], d[name + "_mask"].rearrange("b (t p) c -> p (b t) c", p=P)).then_inc(mask_loaded, 16)
            core.start_loads(sp)

        @block.gpsimd
        def _(pool):
            step = Links(pool, setup)
            step.after(nc.gpsimd.memset(head_of[:, :], 1.0))
            step.after(nc.gpsimd.affine_select(out=head_of[:, :], in_=head_of[:, :], compare_op=ALU.is_ge, fill=0.0,
                                               base=0, pattern=[[-DH, HH]], channel_multiplier=1))
            step.after(nc.gpsimd.affine_select(out=head_of[:, :], in_=head_of[:, :], compare_op=ALU.is_ge, fill=0.0,
                                               base=DH - 1, pattern=[[DH, HH]], channel_multiplier=-1))
            for b in range(B):
                for k in range(KT):
                    last = nc.gpsimd.tensor_copy(ctx_rest[:, k, b, :].rearrange("p (h n) -> p h n", h=RH),
                                                 core.ctxT[:, k, b:b + 1, P:CTX].to_broadcast([P, RH, REST]))
            step.after(last)
            step.after(nc.gpsimd.memset(row_of[:, :], 1.0))
            step.after(nc.gpsimd.affine_select(out=row_of[:, :], in_=row_of[:, :], compare_op=ALU.is_ge, fill=0.0,
                                               base=0, pattern=[[-REST, RH]], channel_multiplier=1))
            step.after(nc.gpsimd.affine_select(out=row_of[:, :], in_=row_of[:, :], compare_op=ALU.is_ge, fill=0.0,
                                               base=REST - 1, pattern=[[REST, RH]], channel_multiplier=-1))
            step.after(nc.gpsimd.memset(v[:, :, :, :], 0.0))
            step.after(nc.gpsimd.memset(v_rest[:, :, :, :, :], 0.0))
            own = v[:, :, :, :].rearrange("p b f (h c) -> p b f h c", c=VW + DH + 1)
            for b in range(B):
                for half in range(2):
                    last = nc.gpsimd.memset(own[:, b, half, :, DH:DH + 1], 1.0)
                    for r in range(HH // RH):
                        first = r * RH * (DH + 1)
                        ones = v_rest[:, b, half, r, first:first + RH * (DH + 1)].rearrange("p (h c) -> p h c", c=DH + 1)
                        last = nc.gpsimd.tensor_copy(ones[:, :, DH], row_of[:, :])
            step.after(last)
            core.start_zeroing(pool)
            pool.wait_ge(w_loaded, LOADS)
            nc.gpsimd.tensor_tensor(core.x[:, :, :], core.x[:, :, :],
                                    bias_out[:, :].rearrange("p (o c) -> p o c", o=1).to_broadcast([P, TILES, D]),
                                    ALU.add).then_inc(bias_added, 1)

        @block.tensor
        def _(pe):
            pe.wait_ge(w_loaded, LOADS)
            for m in range(KT):
                parts = [m] if block_diagonal else list(range(KT))
                for k in parts:
                    last = nc.tensor.matmul(scores[:, m, 0:B * CTX], w["k"][:, k, m * P:(m + 1) * P],
                                            core.ctxT[:, k, :, :].rearrange("p b n -> p (b n)"),
                                            start=(k == parts[0]), stop=(k == parts[-1]))
                last.then_inc(kv_done, 1)
            pe.wait_ge(setup, 4)
            for b in range(B):
                for rest in range(2):
                    n = 2 * b + rest
                    rows = RH * REST if rest else P
                    dst = tpose[0:rows, n % 2, 0:D]
                    if n >= 2:
                        pe.wait_ge(v_ready, n - 1)
                    for k in range(KT):
                        src = ctx_rest[:, k, b, :] if rest else core.ctxT[:, k, b, 0:P]
                        last = nc.tensor.matmul(dst, src, w["v"][:, k, :],
                                                start=(k == 0), stop=(block_diagonal and k == KT - 1))
                    if not block_diagonal:
                        last = nc.tensor.matmul(dst, core.ones_row[0:1, 0:rows], bias_row[0:1, :], start=False, stop=True)
                    last.then_inc(kv_done, 1)
            pe.wait_ge(kv_heads, 2 * B * KT)
            pe.wait_ge(v_ready, 2 * B)
            pe.wait_ge(mask_ready, 1)

            def queries(i, b):
                wait(pe, q_copied, KT * (i * B + b))
                for m in range(KT):
                    parts = [m] if block_diagonal else list(range(KT))
                    for k in parts:
                        last = nc.tensor.matmul(q_ps[:, m, :], w["q"][:, k, m * P:(m + 1) * P],
                                                core.xT[:, k, bass.ds(i * P + b * S, P)],
                                                start=(k == parts[0]), stop=(k == parts[-1]))
                last.then_inc(q_done, 1)

            def qk(i, u):
                b, half = UNITS[u]
                if half == 0:
                    pe.wait_ge(q_split, i * B + b + 1)
                wait(pe, sub_done, i * NU + u)
                for c in range(SB):
                    heads = range(c * HB, min(HH, (c + 1) * HB))
                    n = len(heads) * CTX
                    nc.tensor.matmul(scores[:, c, 0:HB * CTX].rearrange("p (h n) -> p h n", h=HB), core.ident_bf[:, :],
                                     mask[:, bass.ds(i + b * SEQ_TILES, 1), :].to_broadcast([P, HB, CTX]),
                                     start=True, stop=False)
                    for q, k in ((0, 0), (1, 0), (0, 1)):
                        last = nc.tensor.matmul(scores[:, c, 0:n], q_parts[q][:, b, half, :],
                                                k_heads[k][:, b, half, c * HB:c * HB + len(heads), :].rearrange("p h n -> p (h n)"),
                                                start=False, stop=(k == 1))
                last.then_inc(qk_done, 1)

            def transposes(i, u):
                wait(pe, exp_done, i * NU + u + 1)
                for c in range(NCH):
                    ring = (NCH * u + c) % 2
                    if c >= 2:
                        wait(pe, copied_act, (i * NU + u) * ACT_CHUNKS + 1)
                    elif c == 0:
                        wait(pe, copied_act, (i * NU + u) * ACT_CHUNKS)
                        wait(pe, copied_dve, i * NU + u)
                    for j, (h, r) in enumerate(BLOCKS[c * CHUNK:(c + 1) * CHUNK]):
                        rows = P if r is None else RH * REST
                        first = SLOTS * REST + h * P if r is None else r * RH * REST
                        src = p_tok[:, u % 2, first:first + rows]
                        last = nc.tensor.transpose(tpose[0:rows, ring, j * P:(j + 1) * P], src, core.ident[:, :])
                    last.then_inc(t_done, 1)

            def pv(i, u):
                b, half = UNITS[u]
                wait(pe, copied_act, (i * NU + u + 1) * ACT_CHUNKS)
                wait(pe, copied_dve, i * NU + u + 1)
                if half == 0:
                    wait(pe, y_done, i * B + b)
                for n, (h, r) in enumerate(BLOCKS):
                    rows = P if r is None else RH * REST
                    value = v[:, b, half, h * VW:(h + 1) * VW] if r is None else v_rest[:, b, half, r, :]
                    last = nc.tensor.matmul(outp[:, half, :, :].rearrange("p h c -> p (h c)"), pT[0:rows, u % 2, n, :],
                                            value, start=(n == 0), stop=(n == len(BLOCKS) - 1))
                last.then_inc(pv_done, 1)

            def transpose_y(i, b):
                pe.wait_ge(y_done, i * B + b + 1)
                wait(pe, sum_done, i * B + b)
                for k in range(KT):
                    done = nc.tensor.transpose(fin[:, 0, k * P:(k + 1) * P], y[:, k * P:(k + 1) * P], core.ident[:, :])
                done.then_inc(yT_done, 1)

            def project(i, b):
                pe.wait_ge(yT_copied, i * B + b + 1)
                for k in range(KT):
                    done = nc.tensor.matmul(fin[:, 1, :], yT[:, k, :], w["o"][:, k, :], start=(k == 0), stop=(k == KT - 1))
                done.then_inc(out_done, 1)

            def one_round(i, first, last):
                if first:
                    queries(i, 0)
                    qk(i, 0)
                for u in range(NU):
                    if u + 1 < NU:
                        qk(i, u + 1)
                    elif not last:
                        qk(i + 1, 0)
                    if u == 0:
                        queries(i, 1)
                        if not first:
                            project(i - 1, 0)
                    if u == 2:
                        if not last:
                            queries(i + 1, 0)
                        if not first:
                            project(i - 1, 1)
                    transposes(i, u)
                    if u > 0:
                        pv(i, u - 1)
                    elif not first:
                        pv(i - 1, NU - 1)
                    if u == 3:
                        transpose_y(i, 0)
                    if u == 1 and not first:
                        transpose_y(i - 1, 1)
                if last:
                    pv(i, NU - 1)
                    project(i, 0)
                    transpose_y(i, 1)
                    project(i, 1)

            rounds(pe, SEQ_TILES, one_round)

        @block.scalar
        def _(act):
            for m in range(KT):
                act.wait_ge(kv_done, m + 1)
                if block_diagonal:
                    nc.scalar.activation(kT[:, m, :], scores[:, m, 0:B * CTX], ACT.Copy).then_inc(kv_copied, 1)
                else:
                    nc.scalar.activation(kT[:, m, :], scores[:, m, 0:B * CTX], ACT.Identity,
                                         bias=bias_col[:, 1, m:m + 1]).then_inc(kv_copied, 1)
            act.wait_ge(setup, SETUP)
            for b in range(B):
                act.wait_ge(kv_done, KT + 2 * b + 1)
                for half in range(2):
                    own = v[:, b, half, :].rearrange("p (h c) -> p h c", c=VW + DH + 1)
                    last = nc.scalar.activation(own[:, :, 0:DH], tpose[:, 0, half * P:(half + 1) * P].rearrange("p (h e) -> p h e", h=HH),
                                                ACT.Copy)
                last.then_inc(v_ready, 1)
                act.wait_ge(v_ready, 2 * b + 2)

            def queries(i, b):
                act.wait_ge(q_done, i * B + b + 1)
                wait(act, q_split, (i - 1) * B + b + 1)
                for m in range(KT):
                    if block_diagonal:
                        nc.scalar.activation(qT[:, b, m, :], q_ps[:, m, :], ACT.Copy).then_inc(q_copied, 1)
                    else:
                        nc.scalar.activation(qT[:, b, m, :], q_ps[:, m, :], ACT.Identity,
                                             bias=bias_col[:, 0, m:m + 1]).then_inc(q_copied, 1)

            def exps(i, u):
                act.wait_ge(sub_done, i * NU + u + 1)
                e = p_tok[:, u % 2, 0:SLOTS * REST + HH * P]
                nc.scalar.activation(e, e, ACT.Exp, scale=SCALE).then_inc(exp_done, 1)

            def copies(i, u):
                for c in range(NCH):
                    if by_dve(c):
                        continue
                    act.wait_ge(t_done, (i * NU + u) * NCH + c + 1)
                    wait(act, pv_done, i * NU + u - 1)
                    copy_chunk(nc.scalar.copy, u, c).then_inc(copied_act, 1)

            def yT_copy(i, b):
                act.wait_ge(yT_done, i * B + b + 1)
                wait(act, out_done, i * B + b)
                nc.scalar.activation(yT[:, :, :].rearrange("p k q -> p (k q)"), fin[:, 0, :], ACT.Copy).then_inc(yT_copied, 1)

            def one_round(i, first, last):
                if first:
                    queries(i, 0)
                for u in range(NU):
                    exps(i, u)
                    if u == 0:
                        queries(i, 1)
                    if u == 2 and not last:
                        queries(i + 1, 0)
                    copies(i, u)
                    if u == 3:
                        yT_copy(i, 0)
                    if u == 1 and not first:
                        yT_copy(i - 1, 1)
                if last:
                    yT_copy(i, 1)

            rounds(act, SEQ_TILES, one_round)

        @block.vector
        def _(dve):
            dve.wait_ge(mask_loaded, 16)
            nc.vector.tensor_scalar(mask[:, :, :], mask_raw[:, :, :], 0.0, mask_value[1],
                                    ALU.not_equal if mask_value[0] == "hidden" else ALU.is_equal, ALU.mult).then_inc(mask_ready, 1)
            dve.wait_ge(setup, 3)
            dve.wait_ge(kv_copied, KT)
            nc.vector.tensor_copy(kT_parts[0][:, :, :], kT[:, :, :]).then_inc(kT_split, 1)
            dve.wait_ge(kT_split, 1)
            nc.vector.tensor_tensor(kT_parts[1][:, :, :], kT[:, :, :], kT_parts[0][:, :, :].bitcast(F32), ALU.subtract).then_inc(kT_split, 1)
            dve.wait_ge(kT_split, 2)
            for b in range(B):
                for m in range(KT):
                    for part in range(2):
                        nc.vector.tensor_tensor(k_heads[part][:, b, m, :, :],
                                                kT_parts[part][:, m, b * CTX:(b + 1) * CTX].bitcast(F32).rearrange("p (o n) -> p o n", o=1)
                                                .to_broadcast([P, HH, CTX]),
                                                head_of[:, :].rearrange("p (h o) -> p h o", o=1).to_broadcast([P, HH, CTX]),
                                                ALU.mult).then_inc(kv_heads, 1)
            dve.wait_ge(setup, SETUP)
            for b in range(B):
                dve.wait_ge(kv_done, KT + 2 * b + 2)
                dve.wait_ge(v_ready, 2 * b + 1)
                for half in range(2):
                    for r in range(HH // RH):
                        first = r * RH * (DH + 1)
                        nh = half * HH + r * RH
                        last = nc.vector.tensor_tensor(
                            v_rest[:, b, half, r, first:first + RH * (DH + 1)].rearrange("p (h c) -> p h c", c=DH + 1)[:, :, 0:DH],
                            tpose[0:RH * REST, 1, nh * DH:(nh + RH) * DH].rearrange("p (h e) -> p h e", h=RH),
                            row_of[:, :].rearrange("p (h o) -> p h o", o=1).to_broadcast([RH * REST, RH, DH]), ALU.mult)
                last.then_inc(v_ready, 1)
            dve.wait_ge(bias_added, 1)
            sc = scores[:, :, 0:HB * CTX].rearrange("p c (h n) -> p c h n", h=HB)
            by_head = outp[:, :, :, :].rearrange("p f h c -> p (f h) c")

            def split_queries(i, b, step):
                dve.wait_ge(q_copied, KT * (i * B + b + 1))
                wait(dve, qk_done, (i - 1) * NU + 2 * b + 2)
                step.after(nc.vector.tensor_copy(q_parts[0][:, b, :, :], qT[:, b, :, :]))
                nc.vector.tensor_tensor(q_parts[1][:, b, :, :], qT[:, b, :, :], q_parts[0][:, b, :, :].bitcast(F32),
                                        ALU.subtract).then_inc(q_split, 1)

            def shift(i, u, step):
                dve.wait_ge(qk_done, i * NU + u + 1)
                step.after(nc.vector.tensor_reduce(s_max[:, :].rearrange("p (c h) -> p c h", c=SB), sc, AX, ALU.max))
                wait(dve, t_done, (i * NU + u - 1) * NCH)
                for lo, hi, dst in ((P, CTX, p_tok[:, u % 2, 0:SLOTS * REST]), (0, P, p_tok[:, u % 2, SLOTS * REST:])):
                    last = nc.vector.tensor_tensor(
                        dst.rearrange("p (c h n) -> p c h n", c=SB, h=HB), sc[:, :, :, lo:hi],
                        s_max[:, :].rearrange("p (c h o) -> p c h o", c=SB, o=1).to_broadcast([P, SB, HB, hi - lo]),
                        ALU.subtract)
                last.then_inc(sub_done, 1)

            def copies(i, u):
                for c in range(NCH):
                    if by_dve(c):
                        dve.wait_ge(t_done, (i * NU + u) * NCH + c + 1)
                        wait(dve, pv_done, i * NU + u - 1)
                        copy_chunk(nc.vector.tensor_copy, u, c).then_inc(copied_dve, 1)

            def normalise(i, b, step):
                dve.wait_ge(pv_done, i * NU + 2 * b + 2)
                step.after(nc.vector.reciprocal(inv_sum[:, :], by_head[:, :, DH]))
                wait(dve, yT_done, i * B + b)
                nc.vector.tensor_tensor(y[:, :].rearrange("p (h e) -> p h e", h=HEADS), by_head[:, :, 0:DH],
                                        inv_sum[:, :].rearrange("p (h o) -> p h o", o=1).to_broadcast([P, HEADS, DH]),
                                        ALU.mult).then_inc(y_done, 1)

            def add(i, b):
                dve.wait_ge(out_done, i * B + b + 1)
                tile = bass.ds(i + b * SEQ_TILES, 1)
                xt = core.x[:, tile, :].rearrange("p o c -> p (o c)")
                nc.vector.tensor_tensor(xt, fin[:, 1, :], xt, ALU.add).then_inc(sum_done, 1)
                dve.wait_ge(sum_done, i * B + b + 1)
                nc.vector.bn_stats(core.stats[:, tile, :].rearrange("p o c -> p (o c)"), xt)

            def one_round(i, first, last):
                step = Links(dve, s_dve, 0 if first else i * (NU + 2 * B))
                if first:
                    split_queries(i, 0, step)
                for u in range(NU):
                    shift(i, u, step)
                    if u == 1:
                        split_queries(i, 1, step)
                    if u == 3 and not last:
                        split_queries(i + 1, 0, step)
                    if u > 0:
                        copies(i, u - 1)
                    elif not first:
                        copies(i - 1, NU - 1)
                    if u == 1 and not first:
                        add(i - 1, 0)
                        normalise(i - 1, 1, step)
                    if u == 3:
                        if not first:
                            add(i - 1, 1)
                        normalise(i, 0, step)
                if last:
                    copies(i, NU - 1)
                    add(i, 0)
                    normalise(i, 1, step)
                    add(i, 1)

            rounds(dve, SEQ_TILES, one_round)


def cross_attention_0(core, d):
    cross_attention(core, d, "x0", False, ("hidden", -1e18))


def cross_attention_1(core, d):
    cross_attention(core, d, "x1", True, ("seen", -1e20))


def lora_ffn(core, d):
    nc = core.nc
    H = 4 * D
    FT = H // P
    LORA, FIRST = 16, 1
    NP = LORA // 4
    BLOCKS = S // BANK
    BT = BANK // P
    RING = 4

    with ExitStack() as st:
        def sb(n, shape, dt=F32):
            return st.enter_context(nc.sbuf_tensor("ffn_" + n, shape, dt))

        def sem(n):
            return core.sem("ffn_" + n)

        own = core.weights["ffn"]
        w1T, w2T, b1, b2, scale, w_loaded = own.w1T, own.w2T, own.b1, own.b2, own.scale, own.loaded
        w1 = sb("w1_seq", [P, B, KT, H])
        w2 = sb("w2_seq", [P, B, FT, D])
        even = sb("even_scaled", [P, B, LORA // 2, D])
        hidden = sb("hidden", [P, B, FT, BANK])
        ring = st.enter_context(nc.psum_tensor("ffn_ring", [P, RING, BANK], F32))
        outp = st.enter_context(nc.psum_tensor("ffn_out", [P, 2, BANK], F32))
        spread_done, even_ready = sem("spread_done"), sem("even_ready")
        w1_ready, w2_ready, bias_added = sem("w1_ready"), sem("w2_ready"), sem("bias_added")
        up_done, gelu_done, out_done, sum_done = sem("up_done"), sem("gelu_done"), sem("out_done"), sem("sum_done")
        block = st.enter_context(nc.Block())

        @block.sync
        def _(sp):
            core.start_loads(sp)

        @block.tensor
        def _(pe):
            for b in range(B):
                for n in range(LORA // 4):
                    g = b * (LORA // 4) + n
                    if g >= RING:
                        pe.wait_ge(even_ready, g - RING + 1)
                    for j in range(2):
                        token = FIRST + 2 * (2 * n + j)
                        last = nc.tensor.matmul(ring[:, g % RING, j * D:(j + 1) * D],
                                                core.ident[:, token:token + 1].to_broadcast([P, P]),
                                                core.x[:, b * SEQ_TILES, :], start=True, stop=True)
                    last.then_inc(spread_done, 1)
            pe.wait_ge(even_ready, B * LORA // 4)

            def one_round(i, first, last):
                for b in range(B):
                    if first:
                        pe.wait_ge(w1_ready, b + 1)
                    for f in range(FT):
                        n = b * FT + f
                        if n >= RING:
                            wait(pe, gelu_done, i * (B * FT) + n - RING + 1)
                        else:
                            wait(pe, gelu_done, i * (B * FT))
                        for k in range(KT):
                            last = nc.tensor.matmul(ring[:, n % RING, :], w1[:, b, k, f * P:(f + 1) * P],
                                                    core.xT[:, k, bass.ds(i * BANK + b * S, BANK)],
                                                    start=(k == 0), stop=(k == KT - 1))
                        last.then_inc(up_done, 1)
                for b in range(B):
                    if first:
                        pe.wait_ge(w2_ready, b + 1)
                    wait(pe, gelu_done, i * (B * FT) + (b + 1) * FT)
                    for t in range(BT):
                        n = b * BT + t
                        if n >= 2:
                            wait(pe, sum_done, i * (B * BT) + n - 1)
                        else:
                            wait(pe, sum_done, i * (B * BT))
                        for f in range(FT):
                            done = nc.tensor.matmul(outp[:, n % 2, 0:D], hidden[:, b, f, t * P:(t + 1) * P], w2[:, b, f, :],
                                                    start=(f == 0), stop=(f == FT - 1))
                        done.then_inc(out_done, 1)

            rounds(pe, BLOCKS, one_round)

        @block.gpsimd
        def _(pool):
            core.start_zeroing(pool)
            pool.wait_ge(w_loaded, 80)
            pool.wait_ge(spread_done, B * LORA // 4)
            nc.gpsimd.tensor_tensor(core.x[:, :, :], core.x[:, :, :],
                                    b2[:, :].rearrange("p (o c) -> p o c", o=1).to_broadcast([P, TILES, D]),
                                    ALU.add).then_inc(bias_added, 1)

        @block.scalar
        def _(act):
            act.wait_ge(w_loaded, 80)
            for g in range(B * LORA // 4):
                act.wait_ge(spread_done, g + 1)
                n = 2 * g % (LORA // 2)
                nc.scalar.activation(even[:, 2 * g // (LORA // 2), n:n + 2, :].rearrange("p n c -> p (n c)"), ring[:, g % RING, :],
                                     ACT.Copy, scale=scale[:, 0:1]).then_inc(even_ready, 1)

            def one_round(i, first, last):
                for b in range(B):
                    wait(act, out_done, i * (B * BT))
                    for f in range(FT):
                        n = b * FT + f
                        wait(act, up_done, i * (B * FT) + n + 1)
                        nc.scalar.activation(hidden[:, b, f, :], ring[:, n % RING, :], ACT.Gelu,
                                             bias=b1[:, f:f + 1]).then_inc(gelu_done, 1)

            rounds(act, BLOCKS, one_round)

        @block.vector
        def _(dve):
            dve.wait_ge(w_loaded, 80)

            def odd(b, k, i):
                token = b * S + FIRST + 2 * i + 1
                return core.xT[:, k, token:token + 1]

            for b in range(B):
                dve.wait_ge(even_ready, (b + 1) * LORA // 4)
                for k in range(KT):
                    for i in range(NP):
                        cols = slice(i * D, (i + 1) * D)
                        last = nc.vector.scalar_tensor_tensor(w1[:, b, k, cols], even[:, b, i, :], odd(b, k, i), w1T[:, k, cols],
                                                              ALU.mult, ALU.add)
                last.then_inc(w1_ready, 1)
            for b in range(B):
                for k in range(KT):
                    for i in range(NP):
                        cols = slice(i * (D // NP), (i + 1) * (D // NP))

                        def parts(w):
                            return w.rearrange("p (j k) c -> p j k c", k=KT)[:, :, k, cols]

                        last = nc.vector.scalar_tensor_tensor(parts(w2[:, b, :, :]),
                                                              even[:, b, NP + i, :].rearrange("p (o j) -> p j o", j=4),
                                                              odd(b, k, NP + i), parts(w2T[:, :, :]), ALU.mult, ALU.add)
                last.then_inc(w2_ready, 1)
            dve.wait_ge(bias_added, 1)

            def one_round(i, first, last):
                for b in range(B):
                    for t in range(BT):
                        n = b * BT + t
                        wait(dve, out_done, i * (B * BT) + n + 1)
                        tile = bass.ds(i * BT + (b * SEQ_TILES + t), 1)
                        xt = core.x[:, tile, :].rearrange("p o c -> p (o c)")
                        nc.vector.tensor_tensor(xt, outp[:, n % 2, 0:D], xt, ALU.add).then_inc(sum_done, 1)
                        wait(dve, sum_done, i * (B * BT) + n + 1)
                        nc.vector.bn_stats(core.stats[:, tile, :].rearrange("p o c -> p (o c)"), xt)

            rounds(dve, BLOCKS, one_round)
def gated_linear_attention(core, d):
    nc = core.nc
    DK = D // 2 // HEADS
    DV = D // HEADS
    GATE_NORM = 16.0
    SCALE = DK ** -0.5
    R = 16
    G = B * S // BANK
    GB = S // BANK
    WIDE = P // HEADS
    QUAD = P // 2 // HEADS
    UNITS = [(e, b) for e in range(WIDE) for b in range(B)]
    NU = len(UNITS)
    ROUNDS = DV // WIDE

    with ExitStack() as st:
        def sb(n, shape, dt=F32):
            return st.enter_context(nc.sbuf_tensor("gla_" + n, shape, dt))

        def sem(n):
            return core.sem("gla_" + n)

        own = core.weights["gla"]
        w_q, w_k, w_g1, w_g2, w_v, w_g, w_o, b_g = own.w_q, own.w_k, own.w_g1, own.w_g2, own.w_v, own.w_g, own.w_o, own.b_g
        spread = sb("spread", [P, QUAD, P], F32R)
        head_sel = sb("head_sel", [P, HEADS])
        collect = sb("collect", [P, WIDE, P])
        of_head = sb("of_head", [P, HEADS])
        average = sb("average", [P, P])
        qT, kT = sb("q_chan", [P, B * S]), sb("k_chan", [P, B * S])
        g1T = sb("g1_chan", [R, B * S])
        decay = sb("decay", [P, B * S])
        tmp = sb("tmp", [P, B * S])
        v_split = sb("v_split", [P, DV // QUAD, B * S], F32R)
        gate = sb("gate", [P, KT, B * S])
        kv = sb("kv", [P, 2, S])
        state = sb("state", [P, 2, S])
        qs = sb("q_state", [P, 2, S])
        oT = sb("o_chan", [P, KT, B * S])
        squares = sb("squares", [P, 2, KT, BANK])
        eps = sb("eps", [P, 1])
        ring = st.enter_context(nc.psum_tensor("gla_ring", [P, 4, BANK], F32))
        acc = st.enter_context(nc.psum_tensor("gla_acc", [P, 4, BANK], F32))
        setup, s_dve, s_act = sem("setup"), sem("dve_steps"), sem("act_steps")
        v_high_done, proj_done, by_act, by_dve = sem("v_high_done"), sem("proj_done"), sem("proj_by_act"), sem("proj_by_dve")
        abs_done, softplus_done, log_done, decay_done = (sem("abs_done"), sem("softplus_done"), sem("log_done"),
                                                         sem("decay_done"))
        v_done, kv_done, scan_done, qs_done, o_done, o_copied = (
            sem("v_done"), sem("kv_done"), sem("scan_done"), sem("qs_done"), sem("o_done"), sem("o_copied"))
        mean_done, centred, squared, var_done, rstd_done, gated, on_done = (
            sem("mean_done"), sem("centred"), sem("squared"), sem("var_done"), sem("rstd_done"), sem("gated"), sem("on_done"))
        out_done, sum_done = sem("out_done"), sem("sum_done")
        block = st.enter_context(nc.Block())

        @block.sync
        def _(sp):
            core.start_loads(sp)

        PROJ = [(n, g) for n in ("g1", "kg", "k", "q", "v0", "v1") for g in range(G)]
        GATES = [("z%d" % k, g) for g in range(G) for k in range(KT)]
        ALL = PROJ + GATES
        act_before = [sum(w in ("g1", "kg", "z0", "z1") for w, _ in ALL[:n]) for n in range(len(ALL) + 1)]
        dve_before = [n - act_before[n] for n in range(len(ALL) + 1)]
        SETUP = 4
        FIRST_GATES = 4

        @block.tensor
        def _(pe):
            def projection(n):
                what, g = ALL[n]
                cols = slice(g * BANK, (g + 1) * BANK)
                if what == "kg":
                    pe.wait_ge(by_act, g + 1)
                    done = nc.tensor.matmul(ring[:, n % 4, :], w_g2[:, :], g1T[:, cols], start=True, stop=True)
                else:
                    w, rows = {"q": (w_q, P), "k": (w_k, P), "g1": (w_g1, R), "z0": (w_g[:, :, 0:P], P),
                               "v0": (w_v[:, :, 0:P], P), "v1": (w_v[:, :, P:2 * P], P), "z1": (w_g[:, :, P:2 * P], P)}[what]
                    for k in range(KT):
                        done = nc.tensor.matmul(ring[0:rows, n % 4, :], w[:, k, :], core.xT[:, k, cols],
                                                start=(k == 0), stop=(k == KT - 1))
                done.then_inc(proj_done, 1)

            pe.wait_ge(own.loaded, own.loads)
            for n in range(len(PROJ)):
                if n >= 4:
                    pe.wait_ge(by_act, act_before[n - 3]) if ALL[n - 4][0] in ("g1", "kg") else pe.wait_ge(by_dve, dve_before[n - 3])
                projection(n)
            pe.wait_ge(by_dve, dve_before[len(PROJ)])
            pe.wait_ge(setup, SETUP)

            def values(i, u):
                e, b = UNITS[u]
                wait(pe, kv_done, i * NU + u - 1)
                quad = (i * WIDE + e) // QUAD
                for c in range(GB):
                    cols = slice(b * S + c * BANK, b * S + (c + 1) * BANK)
                    done = nc.tensor.matmul(ring[:, 2 * (u % 2) + c, :], spread[:, e % QUAD, :], v_split[:, quad, cols],
                                            start=True, stop=True)
                done.then_inc(v_done, 1)

            def outputs(i, u):
                e, b = UNITS[u]
                pe.wait_ge(qs_done, i * NU + u + 1)
                if e == 0:
                    wait(pe, o_copied, i * B - B + b + 1)
                for c in range(GB):
                    done = nc.tensor.matmul(acc[:, GB * b + c, :], collect[:, e, :], qs[:, u % 2, c * BANK:(c + 1) * BANK],
                                            start=(e == 0), stop=(e == WIDE - 1))
                done.then_inc(o_done, 1)

            def one_round(i, first, last):
                if first:
                    values(i, 0)
                    values(i, 1)
                for u in range(NU):
                    if u + 2 < NU:
                        values(i, u + 2)
                    elif not last:
                        values(i + 1, u + 2 - NU)
                    if u > 0:
                        outputs(i, u - 1)
                    elif not first:
                        outputs(i - 1, NU - 1)

            rounds(pe, ROUNDS, one_round)
            pe.wait_ge(kv_done, DV * B)
            for n in range(len(PROJ), len(PROJ) + FIRST_GATES):
                projection(n)
            outputs(ROUNDS - 1, NU - 1)

            def means(g):
                pe.wait_ge(o_copied, (ROUNDS - 1) * B + g // GB + 1)
                for k in range(KT):
                    done = nc.tensor.matmul(acc[:, g, :], average[:, :], oT[:, k, g * BANK:(g + 1) * BANK],
                                            start=(k == 0), stop=(k == KT - 1))
                done.then_inc(mean_done, 1)

            def variances(g):
                pe.wait_ge(squared, g + 1)
                for k in range(KT):
                    done = nc.tensor.matmul(acc[:, g, :], average[:, :], squares[:, g % 2, k, :],
                                            start=(k == 0), stop=(k == KT - 1))
                done.then_inc(var_done, 1)

            for g in range(G):
                means(g)
            for g in range(G):
                variances(g)
                if g == 0:
                    for n in range(len(PROJ) + FIRST_GATES, len(ALL)):
                        pe.wait_ge(by_act, act_before[n - 3])
                        projection(n)
            pe.wait_ge(by_act, act_before[len(ALL)])
            for t in range(TILES):
                pe.wait_ge(on_done, t * P // BANK + 1)
                if t >= 4:
                    pe.wait_ge(sum_done, t - 3)
                for k in range(KT):
                    done = nc.tensor.matmul(ring[:, t % 4, 0:D], oT[:, k, t * P:(t + 1) * P], w_o[:, k, :],
                                            start=(k == 0), stop=(k == KT - 1))
                done.then_inc(out_done, 1)

        @block.gpsimd
        def _(pool):
            core.start_zeroing(pool)
            step = Links(pool, setup)
            nc.gpsimd.memset(collect[:, :, :], 0.0)
            nc.gpsimd.memset(eps[:, :], EPS)
            step.after(nc.gpsimd.memset(head_sel[:, :], 1.0))
            step.after(nc.gpsimd.affine_select(out=head_sel[:, :], in_=head_sel[:, :], compare_op=ALU.is_ge, fill=0.0,
                                               base=0, pattern=[[-DK, HEADS]], channel_multiplier=1))
            step.after(nc.gpsimd.affine_select(out=head_sel[:, :], in_=head_sel[:, :], compare_op=ALU.is_ge, fill=0.0,
                                               base=DK - 1, pattern=[[DK, HEADS]], channel_multiplier=-1))
            for e in range(WIDE):
                done = nc.gpsimd.tensor_copy(collect[:, e, e * HEADS:(e + 1) * HEADS], head_sel[:, :])
            step.after(done)
            pool.wait_ge(by_dve, 2 * G)

            def one_round(i, first, last):
                for u, (e, b) in enumerate(UNITS):
                    pool.wait_ge(scan_done, i * NU + u + 1)
                    wait(pool, o_done, i * NU + u - 1)
                    nc.gpsimd.tensor_tensor(qs[:, u % 2, :], state[:, u % 2, :], qT[:, b * S:(b + 1) * S],
                                            ALU.mult).then_inc(qs_done, 1)

            rounds(pool, ROUNDS, one_round)
            for g in range(G):
                cols = slice(g * BANK, (g + 1) * BANK)
                pool.wait_ge(squared, g + 1)
                pool.wait_ge(by_act, act_before[len(PROJ) + KT * (g + 1)])
                nc.gpsimd.tensor_tensor(oT[:, :, cols], oT[:, :, cols], gate[:, :, cols], ALU.mult).then_inc(gated, 1)

        @block.scalar
        def _(act):
            def copy_projection(n):
                what, g = ALL[n]
                act.wait_ge(proj_done, n + 1)
                cols = slice(g * BANK, (g + 1) * BANK)
                if what == "g1":
                    nc.scalar.activation(g1T[:, cols], ring[0:R, n % 4, :], ACT.Copy).then_inc(by_act, 1)
                elif what == "kg":
                    nc.scalar.activation(decay[:, cols], ring[:, n % 4, :], ACT.Copy).then_inc(by_act, 1)
                else:
                    k = int(what[1])
                    nc.scalar.activation(gate[:, k, cols], ring[:, n % 4, :], ACT.Silu, bias=b_g[:, k:k + 1]).then_inc(by_act, 1)

            act.wait_ge(own.loaded, own.loads)
            for n in range(2 * G):
                copy_projection(n)
            act.wait_ge(abs_done, 1)
            nc.scalar.activation(tmp[:, :], tmp[:, :], ACT.Exp, scale=-1.0).then_inc(s_act, 1)
            act.wait_ge(s_act, 1)
            nc.scalar.activation(tmp[:, :], tmp[:, :], ACT.Ln, bias=1.0).then_inc(softplus_done, 1)
            act.wait_ge(log_done, 1)
            nc.scalar.activation(decay[:, :], decay[:, :], ACT.Exp, scale=1.0 / GATE_NORM).then_inc(decay_done, 1)
            for n in range(4 * G, 6 * G):
                act.wait_ge(proj_done, n + 1)
                what, g = ALL[n]
                for half in range(2):
                    done = nc.scalar.copy(v_split[0:P // 2, 2 * int(what[1]) + half, g * BANK:(g + 1) * BANK],
                                          ring[half * (P // 2):(half + 1) * (P // 2), n % 4, :])
                done.then_inc(v_high_done, 1)

            for i in range(ROUNDS):
                for b in range(B):
                    act.wait_ge(o_done, i * NU + NU - B + b + 1)
                    nc.scalar.copy(oT[:, i, b * S:(b + 1) * S],
                                   acc[:, GB * b:GB * (b + 1), :].rearrange("p c n -> p (c n)")).then_inc(o_copied, 1)
                    if i == ROUNDS - 1 and b == 0:
                        for n in range(len(PROJ), len(PROJ) + FIRST_GATES):
                            copy_projection(n)

            for g in range(G):
                act.wait_ge(centred, g + 1)
                if g >= 2:
                    act.wait_ge(var_done, g - 1)
                nc.scalar.activation(squares[:, g % 2, :, :], oT[:, :, g * BANK:(g + 1) * BANK], ACT.Square).then_inc(squared, 1)
                if g == 1:
                    for n in range(len(PROJ) + FIRST_GATES, len(ALL)):
                        copy_projection(n)
            for g in range(G):
                act.wait_ge(var_done, g + 1)
                nc.scalar.activation(tmp[:, g * BANK:(g + 1) * BANK], acc[:, g, :], ACT.Ln, bias=eps[:, 0:1]).then_inc(s_act, 1)
            for g in range(G):
                act.wait_ge(s_act, 1 + g + 1)
                nc.scalar.activation(tmp[:, g * BANK:(g + 1) * BANK], tmp[:, g * BANK:(g + 1) * BANK], ACT.Exp,
                                     scale=-0.5).then_inc(rstd_done, 1)

        @block.vector
        def _(dve):
            step = Links(dve, s_dve)
            halves = core.ident[:, :].rearrange("p (z e o) -> p z e o", z=2, o=1)
            nc.vector.tensor_tensor(spread[:, :, :].rearrange("p q (h c) -> p (q h) c", c=DK),
                                    halves[:, 0, :, :].to_broadcast([P, P // 2, DK]),
                                    halves[:, 1, :, :].to_broadcast([P, P // 2, DK]), ALU.add)
            step.after(nc.vector.tensor_reduce(of_head[:, :], core.ident[:, :].rearrange("p (e h) -> p h e", h=HEADS), AX, ALU.add))
            nc.vector.tensor_scalar(average[:, :].rearrange("p (e h) -> p e h", h=HEADS),
                                    of_head[:, :].rearrange("p (o h) -> p o h", o=1).to_broadcast([P, WIDE, HEADS]),
                                    1.0 / DV, None, ALU.mult)
            dve.wait_ge(by_act, 2 * G)
            nc.vector.scalar_tensor_tensor(tmp[:, :], decay[:, :], -1.0, decay[:, :], ALU.mult, ALU.max).then_inc(abs_done, 1)

            def copy_projections(what, dst, factor):
                for g in range(G):
                    n = PROJ.index((what, g))
                    dve.wait_ge(proj_done, n + 1)
                    nc.vector.tensor_scalar(dst[:, g * BANK:(g + 1) * BANK], ring[:, n % 4, :], factor, None,
                                            ALU.mult).then_inc(by_dve, 1)

            copy_projections("k", kT, SCALE)
            dve.wait_ge(softplus_done, 1)
            nc.vector.scalar_tensor_tensor(decay[:, :], decay[:, :], 0.0, tmp[:, :], ALU.min, ALU.subtract).then_inc(log_done, 1)
            copy_projections("q", qT, 1.0)
            for j in range(KT * G):
                n = 4 * G + j
                cols = slice(j % G * BANK, (j % G + 1) * BANK)
                dve.wait_ge(v_high_done, j + 1)
                for half in range(2):
                    quad = 2 * (j // G) + half
                    done = nc.vector.tensor_tensor(v_split[P // 2:P, quad, cols], ring[half * (P // 2):(half + 1) * (P // 2), n % 4, :],
                                                   v_split[0:P // 2, quad, cols].bitcast(F32), ALU.subtract)
                done.then_inc(by_dve, 1)
            dve.wait_ge(decay_done, 1)

            def key_times_value(i, u):
                dve.wait_ge(v_done, i * NU + u + 1)
                wait(dve, scan_done, i * NU + u - 1)
                b = UNITS[u][1]
                nc.vector.tensor_tensor(kv[:, u % 2, :], ring[:, 2 * (u % 2):2 * (u % 2) + 2, :].rearrange("p c n -> p (c n)"),
                                        kT[:, b * S:(b + 1) * S], ALU.mult).then_inc(kv_done, 1)

            def one_round(i, first, last):
                if first:
                    key_times_value(i, 0)
                for u, (e, b) in enumerate(UNITS):
                    if u + 1 < NU:
                        key_times_value(i, u + 1)
                    elif not last:
                        key_times_value(i + 1, 0)
                    dve.wait_ge(kv_done, i * NU + u + 1)
                    wait(dve, qs_done, i * NU + u - 1)
                    nc.vector.tensor_tensor_scan(state[:, u % 2, :], decay[:, b * S:(b + 1) * S], kv[:, u % 2, :], 0.0,
                                                 ALU.mult, ALU.add).then_inc(scan_done, 1)

            rounds(dve, ROUNDS, one_round)
            for g in range(G):
                here = oT[:, :, g * BANK:(g + 1) * BANK]
                dve.wait_ge(mean_done, g + 1)
                nc.vector.tensor_tensor(here, here, acc[:, g:g + 1, :].to_broadcast([P, KT, BANK]), ALU.subtract).then_inc(centred, 1)

            def normalise(g):
                here = oT[:, :, g * BANK:(g + 1) * BANK]
                dve.wait_ge(gated, g + 1)
                dve.wait_ge(rstd_done, g + 1)
                rstd = tmp[:, g * BANK:(g + 1) * BANK].rearrange("p (o n) -> p o n", o=1).to_broadcast([P, KT, BANK])
                nc.vector.tensor_tensor(here, here, rstd, ALU.mult).then_inc(on_done, 1)

            normalise(0)
            for t in range(TILES):
                if t % 4 == 0 and t // 4 + 1 < G:
                    normalise(t // 4 + 1)
                dve.wait_ge(out_done, t + 1)
                nc.vector.tensor_tensor(core.x[:, t, :], ring[:, t % 4, 0:D], core.x[:, t, :], ALU.add).then_inc(sum_done, 1)
                dve.wait_ge(sum_done, t + 1)
                nc.vector.bn_stats(core.stats[:, t, :], core.x[:, t, :])


def expert_ffn(core, d):
    nc = core.nc
    E, K, F = EXPERTS, TOP, 512
    CAP = CAPACITY
    FT = F // P
    CT = CAP // P
    PARTS = [(0, 3), (3, CT)]
    PER = 2
    N = TILES * E
    UPS = FT * len(PARTS)
    TPS = KT * len(PARTS)
    GR = 4

    with ExitStack() as st:
        def sb(n, shape, dt=F32):
            return st.enter_context(nc.sbuf_tensor("moe_" + n, shape, dt))

        def sem(n):
            return core.sem("moe_" + n)

        router = core.weights["router"]
        w_r, b_r, r_loaded = router.w, router.b, router.loaded
        before = sb("before", [P, P])
        ones = sb("ones", [P, P])
        e_less8 = sb("e_less8", [P, E])
        e_row = sb("e_row", [P, E])
        spare = sb("spare", [P, K, TILES])
        logit, prob, hit, rest = (sb(n, [P, TILES, E]) for n in ("logit", "prob", "hit", "rest"))
        best = [sb(f"best{k}", [P, TILES, E]) for k in range(K)]
        chosen = sb("chosen", [P, TILES, E])
        upto = sb("upto", [P, TILES, E])
        rank = sb("rank", [P, TILES, E])
        row = [sb(f"row{n}", [P, TILES]) for n in range(3)]
        p_best = sb("p_best", [P, K, TILES])
        weight = sb("weight", [P, K, TILES])
        rk, slot, keep = (sb(n, [P, K, TILES]) for n in ("rk", "slot", "keep"))
        to_row = sb("to_row", [P, K, TILES], I32)
        from_row = sb("from_row", [P, K, TILES], I32)
        xe = sb("x_expert", [P, PER, CT, D])
        xeT = sb("x_expert_chan", [P, PER, KT, CAP])
        w1, w2 = sb("w1", [P, PER, KT, F]), sb("w2", [P, PER, FT, D])
        b1, b2 = sb("b1", [P, PER, FT]), sb("b2", [P, PER, D])
        hidden = sb("hidden", [P, PER, FT, CAP])
        ye = sb("y_expert", [P, PER, CT, D])
        got = sb("gathered", [P, GR, K, D])
        route = st.enter_context(nc.psum_tensor("moe_route", [P, BANK], F32))
        tp = st.enter_context(nc.psum_tensor("moe_tp", [P, 2, BANK], F32))
        up = st.enter_context(nc.psum_tensor("moe_up", [P, 3, BANK], F32))
        dn = st.enter_context(nc.psum_tensor("moe_dn", [P, 2, BANK], F32))

        setup, s_dve, logits_done, shifted, exp_done, chosen_done, rank_done, rows_ready = (
            sem(n) for n in ("setup", "dve_steps", "logits_done", "shifted", "exp_done", "chosen_done",
                             "rank_done", "rows_ready"))
        x_loaded = [sem(f"x_loaded{m}") for m in range(PER)]
        w_loaded = [sem(f"w_loaded{m}") for m in range(PER)]
        stored = [sem(f"stored{m}") for m in range(PER)]
        scattered, tp_done, tp_copied, up_done, gelu_done, dn_done, dn_copied = (
            sem(n) for n in ("scattered", "tp_done", "tp_copied", "up_done", "gelu_done",
                             "dn_done", "dn_copied"))
        gathered = [sem(f"gathered{n}") for n in range(GR)]
        summed = sem("summed")
        block = st.enter_context(nc.Block())

        @block.sync
        def _(sp):
            core.start_loads(sp)
            rows = core.by_expert[0:E * CAP, :].rearrange("(e t p) c -> e p t c", e=E, p=P)
            results = core.y_by_expert[:, :].rearrange("(e t p) c -> e p t c", e=E, p=P)

            def load_weights(e, m):
                sp.dma_start(w1[:, m, :, :], d["moe_w1"][e].rearrange("(k p) n -> p k n", p=P)).then_inc(w_loaded[m], 16)
                sp.dma_start(w2[:, m, :, :], d["moe_w2"][e].rearrange("(k p) n -> p k n", p=P)).then_inc(w_loaded[m], 16)
                sp.dma_start(b1[:, m, :], d["moe_b1_cols"][e]).then_inc(w_loaded[m], 16)
                sp.dma_start(b2[:, m, :], d["moe_b2"][e].rearrange("(o n) -> o n", o=1).to_broadcast([P, D])).then_inc(w_loaded[m], 16)

            for m in range(PER):
                load_weights(m, m)
            sp.wait_ge(scattered, 16 * K * TILES)
            for m in range(PER):
                sp.dma_start(xe[:, m, :, :], rows[m]).then_inc(x_loaded[m], 16)

            def one_round(r, first, last):
                e = r * PER
                if not last:
                    for m in range(PER):
                        sp.wait_ge(tp_done, (e + m + 1) * TPS)
                        sp.dma_start(xe[:, m, :, :], rows[e + PER + m]).then_inc(x_loaded[m], 16)
                for m in range(PER):
                    sp.wait_ge(dn_copied, (e + m + 1) * CT)
                    sp.dma_start(results[e + m], ye[:, m, :, :]).then_inc(stored[m], 16)
                    if not last:
                        load_weights(e + PER + m, m)

            rounds(sp, E // PER, one_round)

        @block.tensor
        def _(pe):
            pe.wait_ge(r_loaded, 32)
            for t in range(TILES):
                dst = route[:, t * E:(t + 1) * E]
                for k in range(KT):
                    last = nc.tensor.matmul(dst, core.xT[:, k, t * P:(t + 1) * P], w_r[:, k, :], start=(k == 0), stop=(k == KT - 1))
            last.then_inc(logits_done, 1)
            pe.wait_ge(chosen_done, 1)
            pe.wait_ge(setup, 6)
            ch = chosen[:, :, :].rearrange("p t e -> p (t e)")
            nc.tensor.matmul(route[:, N:2 * N], before[:, :], ch, start=True, stop=True)
            nc.tensor.matmul(route[:, 2 * N:3 * N], ones[:, :], ch, start=True, stop=True).then_inc(rank_done, 1)

            def one_round(r, first, last):
                e = r * PER
                for m in range(PER):
                    wait(pe, x_loaded[m], r * 16 + 16)
                    n = 0
                    for lo, hi in PARTS:
                        for k in range(KT):
                            if m * TPS + n >= 2:
                                wait(pe, tp_copied, e * TPS + m * TPS + n - 1)
                            else:
                                wait(pe, tp_copied, e * TPS)
                            for t in range(lo, hi):
                                last = nc.tensor.transpose(tp[:, n % 2, (t - lo) * P:(t - lo + 1) * P],
                                                           xe[:, m, t, k * P:(k + 1) * P], core.ident[:, :])
                            last.then_inc(tp_done, 1)
                            n += 1
                    pe.wait_ge(w_loaded[m], r * 64 + 64)
                    n = 0
                    for q, (lo, hi) in enumerate(PARTS):
                        wait(pe, tp_copied, e * TPS + m * TPS + (q + 1) * KT)
                        for f in range(FT):
                            if m * UPS + n >= 3:
                                wait(pe, gelu_done, e * UPS + m * UPS + n - 2)
                            else:
                                wait(pe, gelu_done, e * UPS)
                            for k in range(KT):
                                last = nc.tensor.matmul(up[:, (m * UPS + n) % 3, 0:(hi - lo) * P], w1[:, m, k, f * P:(f + 1) * P],
                                                        xeT[:, m, k, lo * P:hi * P], start=(k == 0), stop=(k == KT - 1))
                            last.then_inc(up_done, 1)
                            n += 1
                    wait(pe, gelu_done, e * UPS + (m + 1) * UPS)
                    for t in range(CT):
                        n = m * CT + t
                        if n >= 2:
                            wait(pe, dn_copied, e * CT + n - 1)
                        else:
                            wait(pe, dn_copied, e * CT)
                        for f in range(FT):
                            done = nc.tensor.matmul(dn[:, n % 2, 0:D], hidden[:, m, f, t * P:(t + 1) * P], w2[:, m, f, :],
                                                    start=(f == 0), stop=(f == FT - 1))
                        done.then_inc(dn_done, 1)

            rounds(pe, E // PER, one_round)

        @block.scalar
        def _(act):
            act.wait_ge(shifted, 1)
            nc.scalar.activation(prob[:, :, :], logit[:, :, :], ACT.Exp).then_inc(exp_done, 1)

            def one_round(r, first, last):
                e = r * PER
                for m in range(PER):
                    wait(act, dn_done, (e - PER + m + 1) * CT)
                    n = 0
                    for q, (lo, hi) in enumerate(PARTS):
                        for f in range(FT):
                            wait(act, up_done, e * UPS + m * UPS + n + 1)
                            if q == 0 and f == 0:
                                act.wait_ge(w_loaded[m], r * 64 + 64)
                            nc.scalar.activation(hidden[:, m, f, lo * P:hi * P], up[:, (m * UPS + n) % 3, 0:(hi - lo) * P],
                                                 ACT.Gelu, bias=b1[:, m, f:f + 1]).then_inc(gelu_done, 1)
                            n += 1

            rounds(act, E // PER, one_round)

        @block.gpsimd
        def _(pool):
            core.start_zeroing(pool)
            step = Links(pool, setup)
            nc.gpsimd.memset(ones[:, :], 1.0)
            step.after(nc.gpsimd.memset(before[:, :], 1.0))
            step.after(nc.gpsimd.affine_select(out=before[:, :], in_=before[:, :], compare_op=ALU.is_gt, fill=0.0,
                                               base=0, pattern=[[1, P]], channel_multiplier=-1))
            step.after(nc.gpsimd.iota(e_less8[:, :], pattern=[[1, E]], base=-E, channel_multiplier=0,
                                      allow_small_or_imprecise_dtypes=True))
            step.after(nc.gpsimd.iota(e_row[:, :], pattern=[[CAP, E]], base=0, channel_multiplier=0,
                                      allow_small_or_imprecise_dtypes=True))
            step.after(nc.gpsimd.iota(spare[:, :, :], pattern=[[B * S, K], [P, TILES]], base=E * CAP, channel_multiplier=1,
                                      allow_small_or_imprecise_dtypes=True))
            step.after(nc.gpsimd.memset(upto[:, :, :], 1.0))
            pool.wait_ge(core.zeroed, 16)
            pool.wait_ge(rows_ready, 1)
            for t in range(TILES):
                for k in range(K):
                    nc.gpsimd.indirect_dma_start(out=core.by_expert[:, :],
                                                 out_offset=bass.IndirectOffsetOnAxis(ap=to_row[:, k, t:t + 1], axis=0),
                                                 in_=core.x[:, t, :], in_offset=None).then_inc(scattered, 16)
            for m in range(PER):
                pool.wait_ge(stored[m], 16 * E // PER)
            for t in range(TILES):
                if t >= GR:
                    pool.wait_ge(summed, t - GR + 1)
                for k in range(K):
                    nc.gpsimd.indirect_dma_start(out=got[:, t % GR, k, :], out_offset=None, in_=core.y_by_expert[:, :],
                                                 in_offset=bass.IndirectOffsetOnAxis(ap=from_row[:, k, t:t + 1], axis=0)
                                                 ).then_inc(gathered[t % GR], 16)

        @block.vector
        def _(dve):
            step = Links(dve, s_dve)
            shape = [P, TILES, E]

            def per_tile(a):
                return a.rearrange("p (t o) -> p t o", o=1).to_broadcast(shape)

            def per_expert(a):
                return a[:, :].rearrange("p (o e) -> p o e", o=1).to_broadcast(shape)

            def combine(out, a, b, op):
                step.after(nc.vector.tensor_tensor(out, a, b, op))

            dve.wait_ge(r_loaded, 32)
            dve.wait_ge(logits_done, 1)
            lg = route[:, 0:N].rearrange("p (t e) -> p t e", e=E)
            combine(logit[:, :, :], lg, per_expert(b_r), ALU.add)
            step.after(nc.vector.tensor_reduce(row[0][:, :], logit[:, :, :], AX, ALU.max))
            nc.vector.tensor_tensor(logit[:, :, :], logit[:, :, :], per_tile(row[0][:, :]), ALU.subtract).then_inc(shifted, 1)
            dve.wait_ge(exp_done, 1)
            step.after(nc.vector.tensor_reduce(row[1][:, :], prob[:, :, :], AX, ALU.add))
            step.after(nc.vector.reciprocal(row[2][:, :], row[1][:, :]))
            combine(prob[:, :, :], prob[:, :, :], per_tile(row[2][:, :]), ALU.mult)
            dve.wait_ge(setup, 6)
            left = prob
            for k in range(K):
                step.after(nc.vector.tensor_reduce(p_best[:, k, :], left[:, :, :], AX, ALU.max))
                combine(hit[:, :, :], left[:, :, :], per_tile(p_best[:, k, :]), ALU.is_equal)
                combine(hit[:, :, :], hit[:, :, :], per_expert(e_less8), ALU.mult)
                step.after(nc.vector.tensor_reduce(row[0][:, :], hit[:, :, :], AX, ALU.min))
                combine(best[k][:, :, :], per_expert(e_less8), per_tile(row[0][:, :]), ALU.is_equal)
                if k + 1 < K:
                    step.after(nc.vector.scalar_tensor_tensor(rest[:, :, :], best[k][:, :, :], -2.0, left[:, :, :], ALU.mult, ALU.add))
                    left = rest
            combine(chosen[:, :, :], best[0][:, :, :], best[1][:, :, :], ALU.add)
            dve.sem_inc(chosen_done, 1)
            combine(row[1][:, :], p_best[:, 0, :], p_best[:, 1, :], ALU.add)
            step.after(nc.vector.tensor_scalar(row[1][:, :], row[1][:, :], 1e-9, None, ALU.max))
            step.after(nc.vector.reciprocal(row[2][:, :], row[1][:, :]))
            for k in range(K):
                combine(weight[:, k, :], p_best[:, k, :], row[2][:, :], ALU.mult)
            dve.wait_ge(rank_done, 1)
            totals = route[:, 2 * N:3 * N].rearrange("p (t e) -> p t e", e=E)
            for e in range(E):
                last = nc.vector.tensor_tensor_scan(rest[:, :, e], upto[:, :, e], totals[:, :, e], 0.0, ALU.mult, ALU.add)
            step.after(last)
            combine(rest[:, :, :], rest[:, :, :], totals, ALU.subtract)
            combine(rank[:, :, :], rest[:, :, :], route[:, N:2 * N].rearrange("p (t e) -> p t e", e=E), ALU.add)
            for k in range(K):
                combine(hit[:, :, :], best[k][:, :, :], rank[:, :, :], ALU.mult)
                step.after(nc.vector.tensor_reduce(rk[:, k, :], hit[:, :, :], AX, ALU.add))
                combine(hit[:, :, :], best[k][:, :, :], per_expert(e_row), ALU.mult)
                step.after(nc.vector.tensor_reduce(slot[:, k, :], hit[:, :, :], AX, ALU.add))
            combine(slot[:, :, :], slot[:, :, :], rk[:, :, :], ALU.add)
            step.after(nc.vector.tensor_scalar(keep[:, :, :], rk[:, :, :], float(CAP), None, ALU.is_lt))
            combine(weight[:, :, :], weight[:, :, :], keep[:, :, :], ALU.mult)
            combine(from_row[:, :, :], slot[:, :, :], keep[:, :, :], ALU.mult)
            combine(slot[:, :, :], slot[:, :, :], spare[:, :, :], ALU.subtract)
            combine(slot[:, :, :], slot[:, :, :], keep[:, :, :], ALU.mult)
            combine(to_row[:, :, :], slot[:, :, :], spare[:, :, :], ALU.add)
            dve.sem_inc(rows_ready, 1)

            def one_round(r, first, last):
                e = r * PER
                for m in range(PER):
                    wait(dve, up_done, (e - PER + m + 1) * UPS)
                    n = 0
                    for lo, hi in PARTS:
                        for k in range(KT):
                            wait(dve, tp_done, e * TPS + m * TPS + n + 1)
                            nc.vector.tensor_copy(xeT[:, m, k, lo * P:hi * P], tp[:, n % 2, 0:(hi - lo) * P]).then_inc(tp_copied, 1)
                            n += 1
                    wait(dve, stored[m], r * 16)
                    for t in range(CT):
                        n = m * CT + t
                        wait(dve, dn_done, e * CT + n + 1)
                        nc.vector.tensor_tensor(ye[:, m, t, :], dn[:, n % 2, 0:D], b2[:, m, :], ALU.add).then_inc(dn_copied, 1)

            rounds(dve, E // PER, one_round)
            for t in range(TILES):
                dve.wait_ge(gathered[t % GR], 16 * K * (t // GR + 1))
                for k in range(K):
                    last = nc.vector.scalar_tensor_tensor(core.x[:, t, :], got[:, t % GR, k, :], weight[:, k, t:t + 1],
                                                          core.x[:, t, :], ALU.mult, ALU.add)
                    step.after(last)
                nc.vector.bn_stats(core.stats[:, t, :], core.x[:, t, :]).then_inc(summed, 1)


LAYERS = [latent_attention, cross_attention_0, lora_ffn, gated_linear_attention, cross_attention_1, expert_ffn]


def build(nc, d, out, layers=range(len(LAYERS))):
    with ExitStack() as stack:
        core = Core(nc, stack)
        constants_and_loads(core, d)
        held = {}
        if layers[0] > 0:
            with ExitStack() as st:
                block = st.enter_context(nc.Block())

                @block.sync
                def _(sp):
                    load_tokens(core, d, sp)
                    sp.wait_ge(core.xT_loaded, 16)
                    sp.wait_ge(core.x_loaded, 32)

        def make_weights():
            weights = (("gla", GlaWeights), ("x1", lambda core, d: CrossWeights(core, d, "x1", True)),
                       ("router", RouterWeights), ("ffn", FfnWeights), ("x0", lambda core, d: CrossWeights(core, d, "x0", False)))
            for name, make in weights:
                held[name] = core.stack = ExitStack() if name in ("ffn", "x0") else stack
                core.weights[name] = make(core, d)
            core.stack = stack
            core.to_load.reverse()

        for nth, n in enumerate(layers):
            if n > 0 and not core.weights:
                make_weights()
            LAYERS[n](core, d)
            if n == 0 and len(layers) > 1:
                make_weights()
            if n == 1:
                held["x0"].close()
            if n == 2:
                held["ffn"].close()
            layer_norm(core, nth, out if n == layers[-1] else None)


def arrays_of(inputs):
    import numpy as np
    a = {n: np.ascontiguousarray(v) for n, v in inputs.items()}
    a["x_chan"] = np.ascontiguousarray(a["x"].reshape(B * S, D).T)
    a["ctx_chan"] = np.ascontiguousarray(a["ctx_1024"].reshape(B * CTX, D).T)
    a["w_q_pairs"] = np.ascontiguousarray(a["L0_attn_w_q"].reshape(KT, P, 8, P).transpose(2, 1, 0, 3))
    a["w_kv_up_pairs"] = np.ascontiguousarray(a["L0_attn_w_kv_up"].reshape(P, 16, P).transpose(1, 0, 2))
    a["x0_mask"] = a.pop("mask_BxSxS2_bf0")
    a["x1_mask"] = a.pop("mask_Bx1xSxS2_ik1").reshape(B, S, CTX)
    for n in ("Wq", "Wk", "Wv", "Wo", "bq", "bk", "bv", "bo"):
        a["x0_" + n] = a.pop("L0_xattn_" + n)
    for n in ("Wq", "Wk", "Wv", "Wo"):
        a["x1_" + n] = np.ascontiguousarray(a.pop("L1_xattn_" + n).T)
    a["w1T"] = np.ascontiguousarray(a.pop("L0_ffn_W1").T)
    a["w2T"] = np.ascontiguousarray(a.pop("L0_ffn_W2").T)
    a["L0_ffn_b1_cols"] = np.ascontiguousarray(a.pop("L0_ffn_b1").reshape(-1, P).T)
    a["L0_ffn_scale"] = a["L0_ffn_scale"].reshape(1, 1)
    DV = D // HEADS
    for n in ("Wv", "Wg"):
        a["gla_" + n] = np.ascontiguousarray(a.pop("L1_attn_" + n).reshape(D, HEADS, DV).transpose(0, 2, 1)).reshape(D, D)
    a["gla_Wo"] = np.ascontiguousarray(a.pop("L1_attn_Wo").reshape(HEADS, DV, D).transpose(1, 0, 2)).reshape(D, D)
    a["gla_bg_cols"] = np.ascontiguousarray(a.pop("L1_attn_bg").reshape(HEADS, DV).T.reshape(KT, P).T)
    a["moe_w1"], a["moe_w2"], a["moe_b2"] = a.pop("L1_ffn_w1"), a.pop("L1_ffn_w2"), a.pop("L1_ffn_b2")
    a["moe_b1_cols"] = np.ascontiguousarray(a.pop("L1_ffn_b1").reshape(EXPERTS, -1, P).transpose(0, 2, 1))
    a["x1_bo"] = a.pop("L1_xattn_bo")
    return a


def kernel(**inputs):
    import numpy as np
    from concourse import bacc
    from concourse.bass_utils import run_bass_kernel_spmd

    nc = bacc.Bacc("TRN2", target_bir_lowering=False, num_devices=1)
    arrays = {"in_" + n: v for n, v in arrays_of({n: np.asarray(v) for n, v in inputs.items()}).items()}
    d = {n[3:]: nc.dram_tensor(n, v.shape, mybir.dt.from_np(v.dtype), kind="ExternalInput").ap() for n, v in arrays.items()}
    out = nc.dram_tensor("out", (B, S, D), F32, kind="ExternalOutput").ap()
    build(nc, d, out)
    return run_bass_kernel_spmd(nc, [arrays], core_ids=[0]).results[0]["out"]
```
